# Optimizing a Trainium2 kernel written in Bass

```python
import numpy as np
import jax
import jax.numpy as jnp

def _softmax(x, axis=-1):
    return jax.nn.softmax(x, axis=axis)

def _gelu(x):
    return jax.nn.gelu(x, approximate=True)

def _silu(x):
    return jax.nn.silu(x)

def _sigmoid(x):
    return jax.nn.sigmoid(x)

def _layernorm(x, axis=-1, eps=1e-05):
    m = jnp.mean(x, axis=axis, keepdims=True)
    v = jnp.var(x, axis=axis, keepdims=True)
    return (x - m) / jnp.sqrt(v + eps)

def _scatter_add(tgt, idx, src, axis=0):
    return tgt.at[idx].add(src)

def _segment_sum(src, seg, n):
    return jax.ops.segment_sum(src, seg, n)
kernel_name = 'mk_xattn_ffn_d2_seqx_r2_3cee37'

def setup_inputs(seed: int=0):
    np.random.seed(seed)
    _w = jnp.asarray

    def _rec_inputs():
        import jax
        import jax.numpy as jnp
        _rk = jax.random.key(seed)
        x = 7.22e-05 + 1 * jax.random.normal(jax.random.fold_in(_rk, 1), (16, 224, 512), jnp.float32)
        _lenS = 224 - jax.random.randint(jax.random.fold_in(_rk, 7), (16,), 0, max(1, 224 // 4) + 1, jnp.int32)
        _lenS2 = 750 - jax.random.randint(jax.random.fold_in(_rk, 8), (16,), 0, max(1, 750 // 4) + 1, jnp.int32)
        _ctx_1024P = jax.random.normal(jax.random.fold_in(_rk, 11), (16, 16, 512), jnp.float32)
        _ctx_1024c = jax.random.dirichlet(jax.random.fold_in(_rk, 511), 0.3 * jnp.ones((16,), jnp.float32), (16, 750))
        _ctx_1024t = jnp.einsum('bsk,bkd->bsd', _ctx_1024c, _ctx_1024P)
        _ctx_1024t = _ctx_1024t * jax.lax.rsqrt(jnp.mean(jnp.square(_ctx_1024t)) + 1e-12) * 0.953939
        ctx_1024 = 4.13588e-05 + 0.999923 * (_ctx_1024t + 0.3 * jax.random.normal(jax.random.fold_in(_rk, 611), (16, 750, 512), jnp.float32))
        return (x, ctx_1024)
    x, ctx_1024 = _rec_inputs()

    def _L0_xattn_setup():
        import jax, jax.numpy as jnp
        import numpy as np
        D_MODEL = 512
        N_HEADS = 16
        D_K = D_MODEL // N_HEADS
        B, S = (4, 1024)
        key = jax.random.key(seed)
        ks = jax.random.split(key, 11)
        scale = 1.0 / np.sqrt(D_MODEL)
        inp = {'query': jax.random.normal(ks[0], (B, S, D_MODEL), jnp.float32), 'key_': jax.random.normal(ks[1], (B, S, D_MODEL), jnp.float32), 'value': jax.random.normal(ks[2], (B, S, D_MODEL), jnp.float32), 'W_Q': jax.random.normal(ks[3], (D_MODEL, D_MODEL), jnp.float32) * scale, 'b_Q': jnp.zeros((D_MODEL,), jnp.float32), 'W_K': jax.random.normal(ks[4], (D_MODEL, D_MODEL), jnp.float32) * scale, 'b_K': jnp.zeros((D_MODEL,), jnp.float32), 'W_V': jax.random.normal(ks[5], (D_MODEL, D_MODEL), jnp.float32) * scale, 'b_V': jnp.zeros((D_MODEL,), jnp.float32), 'W_O': jax.random.normal(ks[6], (D_MODEL, D_MODEL), jnp.float32) * scale, 'b_O': jnp.zeros((D_MODEL,), jnp.float32)}
        return inp
    _L0_xattn_all = _L0_xattn_setup()
    _L0_xattn_in = {k: v for k, v in _L0_xattn_all.items() if k in ('W_Q', 'b_Q', 'W_K', 'b_K', 'W_V', 'b_V', 'W_O', 'b_O')}
    del _L0_xattn_all

    def _L0_ffn_setup():
        import jax, jax.numpy as jnp
        import numpy as np
        B, S = (2, 1024)
        H = 512
        I = 128
        E = 128
        K = 8
        G = 8
        TG = 4
        NS = 2

        def _mlp(x, w_gu, w_d):
            gu = x @ w_gu
            g, u = (gu[..., :I], gu[..., I:])
            return jax.nn.silu(g) * u @ w_d
        key = jax.random.key(seed)
        ks = jax.random.split(key, 6)
        s = 0.02
        return {'x': jax.random.normal(ks[0], (B, S, H), jnp.float32), 'Wg': jax.random.normal(ks[1], (E, H), jnp.float32) * s, 'W_gate_up': jax.random.normal(ks[2], (E, H, 2 * I), jnp.float32) * s, 'W_down': jax.random.normal(ks[3], (E, I, H), jnp.float32) * s, 'Ws_gate_up': jax.random.normal(ks[4], (NS, H, 2 * I), jnp.float32) * s, 'Ws_down': jax.random.normal(ks[5], (NS, I, H), jnp.float32) * s}
    _L0_ffn_all = _L0_ffn_setup()
    _L0_ffn_in = {k: v for k, v in _L0_ffn_all.items() if k in ('Wg', 'W_gate_up', 'W_down', 'Ws_gate_up', 'Ws_down')}
    del _L0_ffn_all

    def _L1_xattn_setup():
        import jax, jax.numpy as jnp
        import numpy as np
        D_MODEL = 512
        NUM_HEADS = 16
        HEAD_DIM = D_MODEL // NUM_HEADS
        key = jax.random.key(seed)
        ks = jax.random.split(key, 10)
        B, SQ, SKV = (2, 1024, 1024)
        s = 1.0 / np.sqrt(D_MODEL)
        inp = {'query': jax.random.normal(ks[0], (B, SQ, D_MODEL), jnp.float32), 'key_value': jax.random.normal(ks[1], (B, SKV, D_MODEL), jnp.float32), 'Wq': jax.random.normal(ks[2], (D_MODEL, D_MODEL), jnp.float32) * s, 'bq': jnp.zeros((D_MODEL,), jnp.float32), 'Wk': jax.random.normal(ks[3], (D_MODEL, D_MODEL), jnp.float32) * s, 'bk': jnp.zeros((D_MODEL,), jnp.float32), 'Wv': jax.random.normal(ks[4], (D_MODEL, D_MODEL), jnp.float32) * s, 'bv': jnp.zeros((D_MODEL,), jnp.float32), 'Wo': jax.random.normal(ks[5], (D_MODEL, D_MODEL), jnp.float32) * s, 'bo': jnp.zeros((D_MODEL,), jnp.float32)}
        return inp
    _L1_xattn_all = _L1_xattn_setup()
    _L1_xattn_in = {k: v for k, v in _L1_xattn_all.items() if k in ('Wq', 'bq', 'Wk', 'bk', 'Wv', 'bv', 'Wo', 'bo')}
    del _L1_xattn_all

    def _L1_ffn_setup():
        import jax, jax.numpy as jnp
        import numpy as np
        FP8_MAX = 448.0
        FP8 = jnp.float8_e4m3fn
        key = jax.random.key(seed)
        kx, kw, kb = jax.random.split(key, 3)
        B, S, D_in, D_out = (4, 4096, 512, 512)
        x = jax.random.normal(kx, (B, S, D_in), dtype=jnp.float32)
        w = jax.random.normal(kw, (D_out, D_in), dtype=jnp.float32) * 0.02
        weight_scale = jnp.maximum(jnp.max(jnp.abs(w)), 1e-12) / FP8_MAX
        weight = (w / weight_scale).astype(FP8)
        bias = jax.random.normal(kb, (D_out,), dtype=jnp.float32) * 0.01
        return {'x': x, 'weight': weight, 'weight_scale': weight_scale, 'bias': bias}
    _L1_ffn_all = _L1_ffn_setup()
    _L1_ffn_in = {k: v for k, v in _L1_ffn_all.items() if k in ('weight', 'weight_scale', 'bias')}
    del _L1_ffn_all
    return {'x': x, 'ctx_1024': ctx_1024, 'L0_xattn_W_Q': _L0_xattn_in['W_Q'], 'L0_xattn_b_Q': _L0_xattn_in['b_Q'], 'L0_xattn_W_K': _L0_xattn_in['W_K'], 'L0_xattn_b_K': _L0_xattn_in['b_K'], 'L0_xattn_W_V': _L0_xattn_in['W_V'], 'L0_xattn_b_V': _L0_xattn_in['b_V'], 'L0_xattn_W_O': _L0_xattn_in['W_O'], 'L0_xattn_b_O': _L0_xattn_in['b_O'], 'L0_ffn_Wg': _L0_ffn_in['Wg'], 'L0_ffn_W_gate_up': _L0_ffn_in['W_gate_up'], 'L0_ffn_W_down': _L0_ffn_in['W_down'], 'L0_ffn_Ws_gate_up': _L0_ffn_in['Ws_gate_up'], 'L0_ffn_Ws_down': _L0_ffn_in['Ws_down'], 'L1_xattn_Wq': _L1_xattn_in['Wq'], 'L1_xattn_bq': _L1_xattn_in['bq'], 'L1_xattn_Wk': _L1_xattn_in['Wk'], 'L1_xattn_bk': _L1_xattn_in['bk'], 'L1_xattn_Wv': _L1_xattn_in['Wv'], 'L1_xattn_bv': _L1_xattn_in['bv'], 'L1_xattn_Wo': _L1_xattn_in['Wo'], 'L1_xattn_bo': _L1_xattn_in['bo'], 'L1_ffn_weight': _L1_ffn_in['weight'], 'L1_ffn_weight_scale': _L1_ffn_in['weight_scale'], 'L1_ffn_bias': _L1_ffn_in['bias']}

def reference(x, ctx_1024, L0_xattn_W_Q, L0_xattn_b_Q, L0_xattn_W_K, L0_xattn_b_K, L0_xattn_W_V, L0_xattn_b_V, L0_xattn_W_O, L0_xattn_b_O, L0_ffn_Wg, L0_ffn_W_gate_up, L0_ffn_W_down, L0_ffn_Ws_gate_up, L0_ffn_Ws_down, L1_xattn_Wq, L1_xattn_bq, L1_xattn_Wk, L1_xattn_bk, L1_xattn_Wv, L1_xattn_bv, L1_xattn_Wo, L1_xattn_bo, L1_ffn_weight, L1_ffn_weight_scale, L1_ffn_bias):
    import jax
    import jax.numpy as jnp

    def _L0_xattn_ref(query, key_, value, W_Q, b_Q, W_K, b_K, W_V, b_V, W_O, b_O):
        import jax, jax.numpy as jnp
        import numpy as np
        D_MODEL = 512
        N_HEADS = 16
        D_K = D_MODEL // N_HEADS
        B, S = (4, 1024)
        b = query.shape[0]

        def split_heads(x):
            return x.reshape(b, -1, N_HEADS, D_K).transpose(0, 2, 1, 3)
        Q = split_heads(query @ W_Q.T + b_Q)
        K = split_heads(key_ @ W_K.T + b_K)
        V = split_heads(value @ W_V.T + b_V)
        scores = jnp.einsum('bhqd,bhkd->bhqk', Q, K) / jnp.sqrt(jnp.float32(D_K))
        weights = jax.nn.softmax(scores, axis=-1)
        attn = jnp.einsum('bhqk,bhkd->bhqd', weights, V)
        attn = attn.transpose(0, 2, 1, 3).reshape(b, -1, D_MODEL)
        out = attn @ W_O.T + b_O
        return out

    def _L0_ffn_ref(x, Wg, W_gate_up, W_down, Ws_gate_up, Ws_down):
        import jax, jax.numpy as jnp
        import numpy as np
        B, S = (2, 1024)
        H = 512
        I = 128
        E = 128
        K = 8
        G = 8
        TG = 4
        NS = 2

        def _mlp(x, w_gu, w_d):
            gu = x @ w_gu
            g, u = (gu[..., :I], gu[..., I:])
            return jax.nn.silu(g) * u @ w_d
        b, s, h = x.shape
        xf = x.reshape(-1, h)
        n = xf.shape[0]
        shared = (_mlp(xf, Ws_gate_up[0], Ws_down[0]) + _mlp(xf, Ws_gate_up[1], Ws_down[1])) / NS
        logits = xf @ Wg.T
        gsize = E // G
        gl = logits.reshape(n, G, gsize)
        g_top_l, g_top_i = jax.lax.top_k(gl, TG)
        cand_l = g_top_l.reshape(n, G * TG)
        cand_i = g_top_i.reshape(n, G * TG)
        top_l, pos = jax.lax.top_k(cand_l, K)
        topk_idx = pos // TG * gsize + jnp.take_along_axis(cand_i, pos, axis=1)
        topk_w = jax.nn.softmax(top_l, axis=-1)
        flat_idx = topk_idx.reshape(-1)
        flat_w = topk_w.reshape(-1)
        order = jnp.argsort(flat_idx)
        tok = order // K
        xs = xf[tok]
        gsz = jnp.bincount(flat_idx, length=E).astype(jnp.int32)
        gu = jax.lax.ragged_dot(xs, W_gate_up, gsz)
        hmid = jax.nn.silu(gu[:, :I]) * gu[:, I:]
        yo = jax.lax.ragged_dot(hmid, W_down, gsz)
        yo = yo * flat_w[order][:, None]
        routed = jnp.zeros_like(xf).at[tok].add(yo)
        return (shared + routed).reshape(b, s, h)

    def _L1_xattn_ref(query, key_value, Wq, bq, Wk, bk, Wv, bv, Wo, bo):
        import jax, jax.numpy as jnp
        import numpy as np
        D_MODEL = 512
        NUM_HEADS = 16
        HEAD_DIM = D_MODEL // NUM_HEADS
        B, SQ, _ = query.shape
        SKV = key_value.shape[1]
        Q = query @ Wq.T + bq
        K = key_value @ Wk.T + bk
        V = key_value @ Wv.T + bv
        Q = Q.reshape(B, SQ, NUM_HEADS, HEAD_DIM).transpose(0, 2, 1, 3)
        K = K.reshape(B, SKV, NUM_HEADS, HEAD_DIM).transpose(0, 2, 1, 3)
        V = V.reshape(B, SKV, NUM_HEADS, HEAD_DIM).transpose(0, 2, 1, 3)
        scores = jnp.einsum('bhqd,bhkd->bhqk', Q, K) / np.sqrt(HEAD_DIM)
        causal = jnp.tril(jnp.ones((SQ, SKV), bool))
        scores = jnp.where(causal[None, None], scores, -jnp.inf)
        attn = jax.nn.softmax(scores, axis=-1)
        out = jnp.einsum('bhqk,bhkd->bhqd', attn, V)
        out = out.transpose(0, 2, 1, 3).reshape(B, SQ, D_MODEL)
        return out @ Wo.T + bo

    def _L1_ffn_ref(x, weight, weight_scale, bias):
        import jax, jax.numpy as jnp
        import numpy as np
        FP8_MAX = 448.0
        FP8 = jnp.float8_e4m3fn
        amax = jnp.max(jnp.abs(x), axis=-1, keepdims=True)
        x_scale = jnp.maximum(amax, 1e-12) / FP8_MAX
        qinput = (x / x_scale).astype(FP8)
        A = qinput.astype(x.dtype) * x_scale
        Bm = weight.astype(x.dtype) * weight_scale
        out = jnp.einsum('bsk,nk->bsn', A, Bm) + bias
        return out.astype(x.dtype)
    x = x + _L0_xattn_ref(_layernorm(x, axis=-1), ctx_1024, ctx_1024, L0_xattn_W_Q, L0_xattn_b_Q, L0_xattn_W_K, L0_xattn_b_K, L0_xattn_W_V, L0_xattn_b_V, L0_xattn_W_O, L0_xattn_b_O)
    x = x + _L0_ffn_ref(_layernorm(x, axis=-1), L0_ffn_Wg, L0_ffn_W_gate_up, L0_ffn_W_down, L0_ffn_Ws_gate_up, L0_ffn_Ws_down)
    x = x + _L1_xattn_ref(_layernorm(x, axis=-1), ctx_1024, L1_xattn_Wq, L1_xattn_bq, L1_xattn_Wk, L1_xattn_bk, L1_xattn_Wv, L1_xattn_bv, L1_xattn_Wo, L1_xattn_bo)
    x = x + _L1_ffn_ref(_layernorm(x, axis=-1), L1_ffn_weight, L1_ffn_weight_scale, L1_ffn_bias)
    return x

_drawn_inputs = setup_inputs


def setup_inputs(seed=0):
    import zlib

    import numpy as np

    out = dict(_drawn_inputs(seed))
    spreads = {'L0_xattn_b_Q': (0.0, 0.429),
     'L0_xattn_b_K': (0.0, 2.0),
     'L0_xattn_b_V': (0.0, 0.1),
     'L0_xattn_b_O': (0.0, 0.1),
     'L1_xattn_bq': (0.0, 1.52),
     'L1_xattn_bk': (0.0, 2.0),
     'L1_xattn_bv': (0.0, 0.328),
     'L1_xattn_bo': (0.0, 0.344)}
    factors = {'L0_ffn_Wg': 6.318,
     'L0_ffn_W_gate_up': 5.969,
     'L0_ffn_W_down': 5.959,
     'L0_ffn_Ws_gate_up': 3.711,
     'L0_ffn_Ws_down': 3.719,
     'L1_ffn_bias': 24.701}
    for name, (base, spread) in spreads.items():
        noise = np.random.default_rng([zlib.crc32(name.encode()), seed]).standard_normal(out[name].shape)
        drawn = base * np.exp(spread * noise) if base else spread * noise
        out[name] = jnp.asarray(drawn.astype(out[name].dtype))
    for name, factor in factors.items():
        out[name] = (out[name] * factor).astype(out[name].dtype)
    return out
```

```python
from contextlib import ExitStack

import concourse.bass as bass
from concourse import mybir
from concourse.alu_op_type import AluOpType as ALU

F32 = mybir.dt.float32
F32R = mybir.dt.float32r
BF16 = mybir.dt.bfloat16
I32 = mybir.dt.int32
U32 = mybir.dt.uint32
ACT = mybir.ActivationFunctionType
AX = mybir.AxisListType

P = 128
B, SQ, D = 16, 224, 512
N = B * SQ
NT = N // P
KC = D // P
H, DH = 16, 32
G = D // P
HG = P // DH
QH = SQ // 2
SC = float(DH) ** -0.5
EPS = 1e-5
MASKED = -1e30


def early(t, n):
    return isinstance(t, int) and t < n


def over_tiles(eng, step, n=NT):
    step(0, 0)
    step(1, 1)
    with eng.Fori(1, n // 2) as i:
        step(2 * i, 0)
        step(2 * i + 1, 1)


def make_identity(nc, c, name, n=P, dt=F32):
    ident = c.enter_context(nc.sbuf_tensor(name, [P, P], dt))
    with nc.cleanup_on_exit(), ExitStack() as s:
        zeroed = nc.alloc_semaphore(name + "_zeroed")
        block = s.enter_context(nc.Block())

        @block.gpsimd
        def _(pool):
            nc.gpsimd.memset(ident[:], 0.0).then_inc(zeroed, 1)
            pool.wait_ge(zeroed, 1)
            nc.gpsimd.affine_select(out=ident[:], in_=ident[:], compare_op=ALU.not_equal, fill=1.0,
                                    base=0, pattern=[[-1, P]], channel_multiplier=1).then_inc(zeroed, 1)
            pool.wait_ge(zeroed, 2)
    return ident


def norm_query(nc, tag, ident, x, w_t, bias, qh, ql):
    with nc.cleanup_on_exit(), ExitStack() as c:
        def sb(name, shape, dt=F32):
            return c.enter_context(nc.sbuf_tensor(f"{tag}_{name}", shape, dt))

        def sem(name):
            return nc.alloc_semaphore(f"{tag}_{name}")

        w = sb("w", [P, KC, D])
        b = sb("b", [P, KC])
        xin = sb("xin", [P, 4, D])
        stats = sb("stats", [P, 2, 6])
        mv = sb("mv", [P, 2, 2])
        ve = sb("ve", [P, 2, 1])
        rstd = sb("rstd", [P, 2, 1])
        power = sb("power", [P, 1])
        xn = sb("xn", [P, 2, D])
        xnt = sb("xnt", [P, 2, KC, P])
        qf = sb("qf", [P, 2, KC, P])
        q_hi = sb("q_hi", [P, 2, KC, P], F32R)
        q_lo = sb("q_lo", [P, 2, KC, P], F32R)
        ps_t = c.enter_context(nc.psum_tensor(f"{tag}_ps_t", [P, 2, KC, P], F32))
        ps_q = c.enter_context(nc.psum_tensor(f"{tag}_ps_q", [P, 2, KC, P], F32))
        w_in, power_set, held = sem("w_in"), sem("power_set"), sem("held")
        x_in = [sem(f"x_in{s}") for s in range(4)]
        q_out = [sem("q_out0"), sem("q_out1")]
        stats_made, mv_made, ve_made, rstd_made, normed = map(sem, ("stats_made", "mv_made", "ve_made", "rstd_made", "normed"))
        transposed, xnt_made, q_made, qf_made, hi_made, lo_made = map(
            sem, ("transposed", "xnt_made", "q_made", "qf_made", "hi_made", "lo_made"))
        block = c.enter_context(nc.Block())

        @block.sync
        def _(sp):
            sp.dma_start(w[:], w_t.rearrange("(c p) n -> p c n", p=P)).then_inc(w_in, 16)
            sp.dma_start(b[:], bias.rearrange("(c p) -> p c", p=P), allow_slow_non_contiguous=True).then_inc(w_in, 16)

            def load(t, s):
                if not early(t, 4):
                    sp.wait_ge(normed, t - 3)
                sp.dma_start(xin[:, s, :], x[bass.ds(t * P, P), :]).then_inc(x_in[s], 16)

            def store(t, s):
                sp.wait_ge(hi_made, t + 1)
                sp.wait_ge(lo_made, t + 1)
                for q, d in ((q_hi, qh), (q_lo, ql)):
                    sp.dma_start(d.rearrange("(c p) n -> p c n", p=P)[:, :, bass.ds(t * P, P)],
                                 q[:, s].bitcast(F32)).then_inc(q_out[s], 16)

            for s in range(4):
                load(s, s)
            with sp.Fori(0, NT // 4 - 1) as i:
                for s in range(4):
                    load(4 * i + s + 4, s)
                    store(4 * i + s, s % 2)
            for s in range(4):
                store(NT - 4 + s, s % 2)
            for s in range(2):
                sp.wait_ge(q_out[s], 32 * (NT // 2))

        @block.vector
        def _(dve):
            def norm(i, r):
                t, s = 4 * i + r, r % 2
                dve.wait_ge(x_in[r % 4], 16 * (i + r // 4 + 1))
                if not early(t, 2):
                    dve.wait_ge(rstd_made, t - 1)
                nc.vector.bn_stats(stats[:, s], xin[:, r % 4]).then_inc(stats_made, 1)
                hold(dve, stats_made, t + 1, held)
                nc.vector.bn_aggr(mv[:, s], stats[:, s]).then_inc(mv_made, 1)
                dve.wait_ge(mv_made, t + 1)
                nc.vector.tensor_scalar(ve[:, s], mv[:, s, 1:2], EPS, None, ALU.add).then_inc(ve_made, 1)

            def scale(i, r):
                t, s = 4 * i + r, r % 2
                dve.wait_ge(rstd_made, t + 1)
                if not early(t, 2):
                    dve.wait_ge(transposed, t - 1)
                nc.vector.tensor_scalar(xn[:, s], xin[:, r % 4], mv[:, s, 0:1], rstd[:, s], ALU.subtract, ALU.mult
                                        ).then_inc(normed, 1)

            def bias_add(t, s):
                dve.wait_ge(q_made, t + 1)
                if not early(t, 2):
                    dve.wait_ge(hi_made, t - 1)
                    dve.wait_ge(lo_made, t - 1)
                nc.vector.tensor_tensor(qf[:, s], ps_q[:, s], b[:, :, None].broadcast_to([P, KC, P]),
                                        ALU.add).then_inc(qf_made, 1)

            def low(t, s):
                dve.wait_ge(hi_made, t + 1)
                if not early(t, 2):
                    dve.wait_ge(q_out[s], (t - s) * 16)
                nc.vector.tensor_tensor(q_lo[:, s], qf[:, s], q_hi[:, s].bitcast(F32), ALU.subtract
                                        ).then_inc(lo_made, 1)

            dve.wait_ge(w_in, 32)
            norm(0, 0)
            scale(0, 0)
            norm(0, 1)
            scale(0, 1)

            def four(i, last):
                for s in range(4):
                    if not (last and s >= 2):
                        norm(i, s + 2)
                        scale(i, s + 2)
                    bias_add(4 * i + s, s % 2)
                    low(4 * i + s, s % 2)
            four(0, False)
            with dve.Fori(1, NT // 4 - 1) as i:
                four(i, False)
            four(NT // 4 - 1, True)

        @block.gpsimd
        def _(pool):
            nc.gpsimd.memset(power[:], -0.5).then_inc(power_set, 1)
            pool.wait_ge(power_set, 1)

            def step(t, s):
                pool.wait_ge(ve_made, t + 1)
                if not early(t, 2):
                    pool.wait_ge(normed, t - 1)
                nc.gpsimd.tensor_tensor(rstd[:, s], ve[:, s], power[:], ALU.pow).then_inc(rstd_made, 1)
            over_tiles(pool, step)

        @block.scalar
        def _(act):
            def copy_t(t, s):
                act.wait_ge(transposed, t + 1)
                if not early(t, 2):
                    act.wait_ge(q_made, t - 1)
                nc.scalar.copy(xnt[:, s], ps_t[:, s]).then_inc(xnt_made, 1)

            def high(t, s):
                act.wait_ge(qf_made, t + 1)
                if not early(t, 2):
                    act.wait_ge(q_out[s], (t - s) * 16)
                nc.scalar.copy(q_hi[:, s], qf[:, s]).then_inc(hi_made, 1)

            copy_t(0, 0)
            copy_t(1, 1)

            def both(i):
                for s in range(2):
                    high(2 * i + s, s)
                    copy_t(2 * i + s + 2, s)
            both(0)
            with act.Fori(1, NT // 2 - 1) as i:
                both(i)
            high(NT - 2, 0)
            high(NT - 1, 1)

        @block.tensor
        def _(pe):
            def turn(t, s):
                pe.wait_ge(normed, t + 1)
                if not early(t, 2):
                    pe.wait_ge(xnt_made, t - 1)
                for k in range(KC):
                    last = nc.tensor.transpose(ps_t[:, s, k], xn[:, s, k * P:(k + 1) * P], ident[:])
                last.then_inc(transposed, 1)

            def project(t, s):
                pe.wait_ge(xnt_made, t + 1)
                if not early(t, 2):
                    pe.wait_ge(qf_made, t - 1)
                for o in range(KC):
                    for k in range(KC):
                        last = nc.tensor.matmul(ps_q[:, s, o], w[:, k, o * P:(o + 1) * P], xnt[:, s, k],
                                                start=k == 0, stop=k == KC - 1)
                last.then_inc(q_made, 1)

            turn(0, 0)
            pe.wait_ge(w_in, 32)
            turn(1, 1)

            def both(i):
                for s in range(2):
                    project(2 * i + s, s)
                    turn(2 * i + s + 2, s)
            both(0)
            with pe.Fori(1, NT // 2 - 1) as i:
                both(i)
            project(NT - 2, 0)
            project(NT - 1, 1)


def attend(nc, tag, ident, qh, ql, ctx_t, wk_t, bk, wv_t, out, nkeys, causal):
    ck = 112 if causal else 125
    nc_k = nkeys // ck
    k_cuts = [(0, nkeys)] if causal else [(0, 375), (375, 750)]
    m_cuts = [(0, 0, QH), (1, 0, SQ)] if causal else [(q, a, e) for q in range(2) for a, e in ((0, 376), (376, 750))]
    if causal:
        s_cuts = [(0, 0, 0, 0, 0), (1, QH, 0, SQ, SQ)]
        s_pieces = [(0, 1, SQ + QH)]
        n_banks, p_cols = 2, SQ + QH
    else:
        s_cuts = [(k, 0, k // 2, (k % 2) * SQ, k * SQ) for k in range(nc_k)]
        s_pieces = [(0, 2, 2 * SQ), (2, 1, 2 * SQ)]
        n_banks, p_cols = 3, nc_k * SQ
    n_exp = len(s_pieces)
    v_plan = [[0], [1], [], []] if causal else [[0, 1], [2, 3], [4], [5]]
    n_kp = len(k_cuts)
    pj_batch = 4 * n_kp + nc_k
    KA = 3
    pj_pro = nc_k + KA * n_kp
    n_ring = HG * len(m_cuts) + 2
    assert pj_batch % 2 == 0 and n_ring % 2 == 0
    BI = 2
    NI = B // BI

    with nc.cleanup_on_exit(), ExitStack() as c:
        def sb(name, shape, dt=F32):
            return c.enter_context(nc.sbuf_tensor(f"{tag}_{name}", shape, dt))

        def ps(name, shape):
            return c.enter_context(nc.psum_tensor(f"{tag}_{name}", shape, F32))

        def sem(name):
            return nc.alloc_semaphore(f"{tag}_{name}")

        wk = sb("wk", [P, KC, D])
        wv = sb("wv", [P, KC, D])
        bk_sb = sb("bk", [P, G])
        ct = sb("ct", [P, 2, KC, nkeys])
        qs = sb("qs", [P, 4, HG, SQ], F32R)
        ks = sb("ks", [P, 4, HG, nkeys], F32R)
        k_f = sb("k_f", [P, 2, 376])
        k_hi = sb("k_hi", [P, 2, nkeys], F32R)
        k_lo = sb("k_lo", [P, 2, nkeys], F32R)
        v = sb("v", [P, 2, nc_k, H, DH + 1])
        probs = sb("probs", [P, 2, p_cols])
        maxima = sb("maxima", [P, 2, HG, len(m_cuts)])
        m_col = sb("m_col", [P, 2, 2, P])
        one_hot = sb("one_hot", [HG, HG, nkeys])
        recip = sb("recip", [P, 2, 2 * HG])
        o_sb = sb("o", [P, 2, 2, D])
        if causal:
            ident_b = sb("ident_b", [P, P], BF16)
            mask_qk = sb("mask_qk", [P, QH], BF16)
            mask_kq = sb("mask_kq", [P, QH], BF16)
        if causal:
            ps_s = ps("ps_s", [P, 2, 512])
        else:
            ps_s = ps("ps_s", [P, 3, 512])
        ps_m = ps("ps_m", [P, 2, 512])
        ps_j = ps("ps_j", [P, 2, 512])
        ps_o = ps("ps_o", [P, 2, HG, 64])

        w_in, held = sem("w_in"), sem("held")
        ones_in = sem("ones_in")
        ct_in = [sem("ct_in0"), sem("ct_in1")]
        qs_in = [sem(f"qs_in{s}") for s in range(4)]
        ks_in = [sem(f"ks_in{s}") for s in range(4)]
        pj_made, pj_read = sem("pj_made"), sem("pj_read")
        k_hi_made, k_lo_made = sem("k_hi_made"), sem("k_lo_made")
        ring_made, ring_read = sem("ring_made"), sem("ring_read")
        col_made, rows_made = sem("col_made"), sem("rows_made")
        st_made, exp_made = sem("st_made"), sem("exp_made")
        pv_made, recip_made, o_made = sem("pv_made"), sem("recip_made"), sem("o_made")
        o_out = [sem("o_out0"), sem("o_out1")]

        with ExitStack() as cc:
            zeroed = sem("zeroed")
            pre = cc.enter_context(nc.Block())

            @pre.gpsimd
            def _(pool):
                nc.gpsimd.memset(one_hot[:], 1.0).then_inc(zeroed, 1)
                nc.gpsimd.memset(v[:], 1.0).then_inc(zeroed, 1)
                nc.gpsimd.memset(m_col[:], 0.0).then_inc(zeroed, 1)
                n = 3
                if causal:
                    nc.gpsimd.tensor_copy(ident_b[:], ident[:]).then_inc(zeroed, 1)
                    nc.gpsimd.memset(mask_qk[:], 0.0).then_inc(zeroed, 1)
                    nc.gpsimd.memset(mask_kq[:], 0.0).then_inc(zeroed, 1)
                    n = 6
                pool.wait_ge(zeroed, n)
                nc.gpsimd.affine_select(out=one_hot[:], in_=one_hot[:], compare_op=ALU.is_equal, fill=0.0,
                                        base=0, pattern=[[-1, HG], [0, nkeys]], channel_multiplier=1
                                        ).then_inc(zeroed, 1)
                n += 1
                if causal:
                    nc.gpsimd.affine_select(out=mask_qk[:], in_=mask_qk[:], compare_op=ALU.is_ge, fill=MASKED,
                                            base=0, pattern=[[-1, QH]], channel_multiplier=1).then_inc(zeroed, 1)
                    nc.gpsimd.affine_select(out=mask_kq[:], in_=mask_kq[:], compare_op=ALU.is_ge, fill=MASKED,
                                            base=0, pattern=[[1, QH]], channel_multiplier=-1).then_inc(zeroed, 1)
                    n += 2
                pool.wait_ge(zeroed, n)

        block = c.enter_context(nc.Block())

        class Step:

            def __init__(self, i, last):
                self.i, self.last = i, last

            def unit(self, w):
                return self.i * 8 + w

            def batch(self, w):
                return self.i * BI + w // 4

        def skip(st, w, ahead):
            return st.last and w + ahead >= 8

        def projections(st, w):
            n, mine = 0, []
            for x in range(w + 1):
                items = [] if skip(st, x, KA) else [(j, "k", j) for j in range(n_kp)]
                if not skip(st, x, 4):
                    items += [(2 + m, "v", j) for m, j in enumerate(v_plan[x % 4])]
                mine = [(*item, n + m) for m, item in enumerate(items)]
                n += len(items)
            return mine

        def iterate(eng, unit):
            for w in range(8):
                unit(Step(0, False), w)
            with eng.Fori(1, NI - 1) as i:
                for w in range(8):
                    unit(Step(i, False), w)
            for w in range(8):
                unit(Step(NI - 1, True), w)

        @block.sync
        def _(sp):
            sp.dma_start(wk[:], wk_t.rearrange("(c p) n -> p c n", p=P)).then_inc(w_in, 16)
            sp.dma_start(wv[:], wv_t.rearrange("(c p) n -> p c n", p=P)).then_inc(w_in, 16)
            sp.dma_start(bk_sb[:], bk.rearrange("(c p) -> p c", p=P), allow_slow_non_contiguous=True).then_inc(w_in, 16)
            for s in range(4):
                sp.dma_start(ks[3 * DH:3 * DH + HG, s].bitcast(F32), one_hot[:]).then_inc(ones_in, 16)

            def load_ct(b, s):
                sp.dma_start(ct[:, s], ctx_t.rearrange("(c p) b n -> p c b n", p=P)[:, :, bass.ds(b, 1), 0:nkeys]
                             .rearrange("p c b n -> p c (b n)")).then_inc(ct_in[s], 16)

            def load_qs(b, g, s):
                for part, src in ((0, qh), (1, ql), (2, qh)):
                    sp.dma_start(qs[part * DH:(part + 1) * DH, s].bitcast(F32),
                                 src[g * P:(g + 1) * P, bass.ds(b * SQ, SQ)].rearrange("(j d) n -> d j n", d=DH)
                                 ).then_inc(qs_in[s], 16)

            def stack_keys(s, n):
                sp.wait_ge(k_hi_made, n)
                sp.wait_ge(k_lo_made, n)
                for j in range(HG):
                    for part, src in ((0, k_hi), (1, k_hi), (2, k_lo)):
                        sp.dma_start(ks[part * DH:(part + 1) * DH, s, j].bitcast(F32),
                                     src[j * DH:(j + 1) * DH, s % 2].bitcast(F32)).then_inc(ks_in[s], 16)

            load_ct(0, 0)
            load_ct(1, 1)
            for g in range(4):
                load_qs(0, g, g)
            for s in range(KA):
                stack_keys(s, (s + 1) * n_kp)

            def unit(st, w):
                u = st.unit(w)
                if w % 4 == 4 - KA and not st.last:
                    sp.wait_ge(pj_made, st.i * BI * pj_batch + pj_pro + projections(st, w)[0][3])
                    load_ct(st.batch(w) + 2, (w // 4) % 2)
                if not skip(st, w, KA):
                    if not early(u, 5 - KA):
                        hold(sp, st_made, (u + KA - 3) * HG * n_exp, held)
                    stack_keys((w + KA) % 4, (u + KA + 1) * n_kp)
                if not skip(st, w, 4):
                    hold(sp, st_made, (u + 1) * HG * n_exp, held)
                    load_qs(st.batch(w) + 1, w % 4, w % 4)
                if w % 4 == 3:
                    s = (w // 4) % 2
                    sp.wait_ge(o_made, u + 1)
                    sp.dma_start(out[bass.ds(st.batch(w) * SQ, SQ), :].rearrange("(q p) n -> p q n", p=QH),
                                 o_sb[0:QH, s]).then_inc(o_out[s], 16)
            iterate(sp, unit)
            for s in range(2):
                sp.wait_ge(o_out[s], 16 * NI)

        @block.gpsimd
        def _(pool):
            def split(j, n, s, done):
                a, e = k_cuts[j]
                f = j if n_kp == 2 else s
                hold(pool, pj_read, done, held)
                nc.gpsimd.tensor_copy(k_hi[:, s, a:e], k_f[:, f, 0:e - a]).then_inc(k_hi_made, 1)
                pool.wait_ge(k_hi_made, n + 1)
                nc.gpsimd.tensor_tensor(k_lo[:, s, a:e], k_f[:, f, 0:e - a], k_hi[:, s, a:e].bitcast(F32),
                                        ALU.subtract).then_inc(k_lo_made, 1)
            for n in range(KA * n_kp):
                if n // n_kp >= 2:
                    pool.wait_ge(ks_in[n // n_kp - 2], 16 * 3 * HG)
                split(n % n_kp, n, n // n_kp % 2, nc_k + n + 1)

            def unit(st, w):
                if skip(st, w, KA):
                    return
                pool.wait_ge(ks_in[(w + KA - 2) % 4], (st.i * 2 + (w + KA - 2) // 4 + 1) * 16 * 3 * HG)
                for _, kind, j, n in projections(st, w):
                    if kind == "k":
                        split(j, (st.unit(w) + KA) * n_kp + j, (w + KA) % 2, st.i * BI * pj_batch + pj_pro + n + 1)
            iterate(pool, unit)

        @block.scalar
        def _(act):
            def read_k(j, n, bank, s, g, piece):
                a, e = k_cuts[j]
                act.wait_ge(pj_made, n + 1)
                if not early(piece, 2):
                    act.wait_ge(k_lo_made, piece - 1)
                nc.scalar.activation(k_f[:, j if n_kp == 2 else s, 0:e - a], ps_j[:, bank, 0:e - a], ACT.Identity,
                                     bias=bk_sb[:, g:g + 1]).then_inc(pj_read, 1)

            def read_v(j, n, bank, s):
                act.wait_ge(pj_made, n + 1)
                nc.scalar.copy(v[0:ck, s, j, :, 0:DH], ps_j[0:ck, bank, :].rearrange("p (h d) -> p h d", d=DH)
                               ).then_inc(pj_read, 1)

            act.wait_ge(w_in, 48)
            for j in range(nc_k):
                read_v(j, j, j % 2, 0)
            for m in range(KA * n_kp):
                read_k(m % n_kp, nc_k + m, (nc_k + m) % 2, m // n_kp % 2, m // n_kp, m)

            def exponentials(hh, s):
                if not early(hh, 2):
                    act.wait_ge(pv_made, hh - 1)
                for x, (bank, banks, cols) in enumerate(s_pieces):
                    act.wait_ge(st_made, hh * n_exp + x + 1)
                    bank = s if causal else bank
                    off = x * 4 * SQ
                    nc.scalar.activation(
                        probs[0:ck, s, off:off + banks * cols].rearrange("p (b n) -> p b n", b=banks),
                        ps_s[0:ck, bank:bank + banks, 0:cols], ACT.Exp, scale=SC).then_inc(exp_made, 1)

            exponentials(0, 0)

            def unit(st, w):
                u = st.unit(w)
                for slot in range(HG):
                    if not (skip(st, w, 1) and slot == 3):
                        exponentials(u * HG + slot + 1, (slot + 1) % 2)
                    for at, kind, j, n in projections(st, w):
                        if at != slot:
                            continue
                        number = st.i * BI * pj_batch + pj_pro + n
                        if kind == "k":
                            read_k(j, number, (pj_pro + n) % 2, (w + KA) % 2, (w + KA) % 4, (u + KA) * n_kp + j)
                        else:
                            read_v(j, number, (pj_pro + n) % 2, (w // 4 + 1) % 2)
            iterate(act, unit)

        @block.vector
        def _(dve):
            def maxima_of(u, s, heads):
                for j in heads:
                    for x, (q, a, e) in enumerate(m_cuts):
                        r = j * len(m_cuts) + x
                        dve.wait_ge(ring_made, u * n_ring + r + 1)
                        nc.vector.tensor_reduce(maxima[0:QH, s, j, x:x + 1], ps_m[0:QH, r % 2, 0:e - a],
                                                axis=AX.X, op=ALU.max, negate=True).then_inc(ring_read, 1)

            def columns_of(u, s):
                dve.wait_ge(ring_read, u * n_ring + n_ring - 2)
                for q in range(2):
                    mine = [x for x, m in enumerate(m_cuts) if m[0] == q]
                    dst = m_col[0:QH, s, q, 3 * DH:3 * DH + HG]
                    if len(mine) == 2:
                        nc.vector.tensor_tensor(dst, maxima[0:QH, s, :, mine[0]], maxima[0:QH, s, :, mine[1]], ALU.min
                                                ).then_inc(col_made, 1)
                    else:
                        nc.vector.tensor_copy(dst, maxima[0:QH, s, :, mine[0]]).then_inc(col_made, 1)

            def rows_of(u, s4):
                for q in range(2):
                    dve.wait_ge(ring_made, u * n_ring + n_ring - 1 + q)
                    nc.vector.tensor_copy(
                        qs[3 * DH:3 * DH + HG, s4, :, q * QH:(q + 1) * QH],
                        ps_m[3 * DH:3 * DH + HG, q, None, 0:QH].broadcast_to([HG, HG, QH])).then_inc(ring_read, 1)

            def output(u, b, g, s, n_b):
                dve.wait_ge(pv_made, (u + 1) * HG)
                nc.vector.reciprocal(recip[0:QH, s2(g)].rearrange("p (q j) -> p q j", q=2), ps_o[0:QH, :, :, DH]
                                     ).then_inc(recip_made, 1)
                dve.wait_ge(recip_made, u + 1)
                if g == 0 and not early(n_b, 1):
                    dve.wait_ge(o_out[s], n_b * 16)
                nc.vector.tensor_tensor(
                    o_sb[0:QH, s, :, g * P:(g + 1) * P].rearrange("p q (j d) -> p q j d", d=DH),
                    ps_o[0:QH, :, :, 0:DH],
                    recip[0:QH, s2(g)].rearrange("p (q j) -> p q j", q=2)[:, :, :, None].broadcast_to([QH, 2, HG, DH]),
                    ALU.mult).then_inc(o_made, 1)

            def s2(g):
                return g % 2

            maxima_of(0, 0, range(HG))
            columns_of(0, 0)
            rows_of(0, 0)

            def unit(st, w):
                u = st.unit(w)
                if not skip(st, w, 1):
                    maxima_of(u + 1, (w + 1) % 2, range(HG))
                    columns_of(u + 1, (w + 1) % 2)
                    rows_of(u + 1, (w + 1) % 4)
                s = w // 4
                output(u, None, w % 4, s, st.i)
            iterate(dve, unit)

        @block.tensor
        def _(pe):
            def project(kind, j, n, bank, s_k, s_v, g):
                if not early(n, 2):
                    pe.wait_ge(pj_read, n - 1)
                for k in range(KC):
                    if kind == "k":
                        a, e = k_cuts[j]
                        last = nc.tensor.matmul(ps_j[:, bank, 0:e - a], wk[:, k, g * P:(g + 1) * P],
                                                ct[:, s_k, k, a:e], start=k == 0, stop=k == KC - 1)
                    else:
                        last = nc.tensor.matmul(ps_j[0:ck, bank, :], ct[:, s_v, k, j * ck:(j + 1) * ck],
                                                wv[:, k], start=k == 0, stop=k == KC - 1)
                    if k == KC - 1:
                        last.then_inc(pj_made, 1)
                    yield

            def maxima_of(u, s4, heads):
                for j in heads:
                    for x, (q, a, e) in enumerate(m_cuts):
                        r = j * len(m_cuts) + x
                        if not (early(u, 1) and r < 2):
                            pe.wait_ge(ring_read, u * n_ring + r - 1)
                        last = nc.tensor.matmul(ps_m[0:QH, r % 2, 0:e - a],
                                                qs[0:3 * DH, s4, j, q * QH:(q + 1) * QH],
                                                ks[0:3 * DH, s4, j, a:e], start=True, stop=not causal)
                        if causal:
                            last = nc.tensor.matmul(ps_m[0:QH, r % 2, e - a - QH:e - a], ident_b[0:QH, 0:QH],
                                                    mask_qk[0:QH], start=False, stop=True)
                        last.then_inc(ring_made, 1)
                        yield

            def turn_maxima(u, s):
                for q in range(2):
                    pe.wait_ge(col_made, u * 2 + q + 1)
                    pe.wait_ge(ring_read, u * n_ring + n_ring - 3 + q)
                    nc.tensor.matmul(ps_m[0:3 * DH + HG, q, 0:QH], m_col[0:QH, s, q, 0:3 * DH + HG], ident[0:QH, 0:QH],
                                     start=True, stop=True).then_inc(ring_made, 1)

            def scores(u, s4, j):
                hh = u * HG + j
                if j == 0:
                    pe.wait_ge(ring_read, (u + 1) * n_ring)
                for x, (bank0, banks, cols) in enumerate(s_pieces):
                    if causal:
                        if not early(hh, 2):
                            pe.wait_ge(exp_made, hh - 1)
                    elif not early(hh, 1):
                        pe.wait_ge(exp_made, hh * n_exp - n_exp + x + 1)
                    mine = [y for y in s_cuts if causal or bank0 <= y[2] < bank0 + banks]
                    for y, (k, q0, bank, col, _) in enumerate(mine):
                        bank = j % 2 if causal else bank
                        dst = ps_s[0:ck, bank, col:col + SQ - q0]
                        last = nc.tensor.matmul(dst, ks[0:3 * DH + HG, s4, j, k * ck:(k + 1) * ck],
                                                qs[0:3 * DH + HG, s4, j, q0:SQ], start=True, stop=not causal)
                        if causal:
                            last = nc.tensor.matmul(ps_s[0:ck, bank, col:col + QH], ident_b[0:ck, 0:ck],
                                                    mask_kq[0:ck], start=False, stop=True)
                    last.then_inc(st_made, 1)

            def weigh(u, j, s_v, g, v_read):
                hh = u * HG + j
                if j == 0 and not early(u, 1):
                    pe.wait_ge(o_made, u)
                if j == 0 and g == 0:
                    pe.wait_ge(pj_read, v_read)
                pe.wait_ge(exp_made, (hh + 1) * n_exp)
                for q in range(2):
                    mine = [y for y in s_cuts if q * QH >= y[1]]
                    for y, (k, q0, _, _, col) in enumerate(mine):
                        p0 = col + q * QH - q0
                        last = nc.tensor.matmul(ps_o[0:QH, q, j, 0:DH + 1], probs[0:ck, j % 2, p0:p0 + QH],
                                                v[0:ck, s_v, k, g * HG + j], start=y == 0, stop=y == len(mine) - 1)
                last.then_inc(pv_made, 1)

            pe.wait_ge(w_in, 48)
            pe.wait_ge(ones_in, 64)
            pe.wait_ge(ct_in[0], 16)
            for n, (kind, j, g) in enumerate([("v", j, 0) for j in range(nc_k)]
                                             + [("k", j, u) for u in range(KA) for j in range(n_kp)]):
                for _ in project(kind, j, n, n % 2, 0, 0, g):
                    pass
            pe.wait_ge(qs_in[0], 48)
            pe.wait_ge(ks_in[0], 16 * 3 * HG)
            for _ in maxima_of(0, 0, range(HG)):
                pass
            turn_maxima(0, 0)
            scores(0, 0, 0)

            def unit(st, w):
                u = st.unit(w)
                for slot in range(HG):
                    if not (skip(st, w, 1) and slot == 3):
                        uu, ww, jj = (u, w, slot + 1) if slot < 3 else (u + 1, w + 1, 0)
                        scores(uu, ww % 4, jj)
                    works = []
                    for at, kind, j, n in projections(st, w):
                        if at != slot:
                            continue
                        batch = (w + KA) // 4 if kind == "k" else w // 4 + 1
                        s_b = batch % 2
                        pe.wait_ge(ct_in[s_b], (st.i + batch // 2) * 16 + 16)
                        works.append(project(kind, j, st.i * BI * pj_batch + pj_pro + n, (pj_pro + n) % 2, s_b, s_b,
                                             (w + KA) % 4))
                    if slot < 2 and not skip(st, w, 1):
                        if slot == 0:
                            pe.wait_ge(qs_in[(w + 1) % 4], (st.i * 2 + (w + 1) // 4 + 1) * 48)
                            pe.wait_ge(ks_in[(w + 1) % 4], (st.i * 2 + (w + 1) // 4 + 1) * 16 * 3 * HG)
                        works.append(maxima_of(u + 1, (w + 1) % 4, range(2 * slot, 2 * slot + 2)))
                    if slot == 2 and not skip(st, w, 1):
                        turn_maxima(u + 1, (w + 1) % 2)
                    take_turns(works)
                    weigh(u, slot, w // 4, w % 4, st.i * BI * pj_batch + pj_pro + w // 4 * pj_batch)

            def take_turns(works):
                works = list(works)
                while works:
                    for x in list(works):
                        for _ in range(2 if x.__name__ == "maxima_of" else 1):
                            if next(x, "end") == "end":
                                works.remove(x)
                                break
            iterate(pe, unit)


def hold(eng, sem, value, held):
    eng.wait_ge(sem, value)
    eng.sem_inc(held, 1)


class Link:

    def __init__(self, eng, sem, per):
        self.eng, self.sem, self.per, self.base, self.k = eng, sem, per, 0, 0

    def start(self, t):
        assert self.k in (0, self.per), self.k
        self.base, self.k = t * self.per, 0

    def __call__(self, ins, held=None):
        self.k += 1
        ins.then_inc(self.sem, 1)
        self.eng.wait_ge(self.sem, self.base + self.k)
        if held is not None:
            self.eng.sem_inc(held, 1)


def out_project(nc, tag, ident, a, bv, wo_t, bo, x, out):
    with nc.cleanup_on_exit(), ExitStack() as c:
        def sb(name, shape, dt=F32):
            return c.enter_context(nc.sbuf_tensor(f"{tag}_{name}", shape, dt))

        def sem(name):
            return nc.alloc_semaphore(f"{tag}_{name}")

        w = sb("w", [P, KC, D])
        bv_sb = sb("bv", [P, KC])
        bo_sb = sb("bo", [P, D])
        ain = sb("ain", [P, 2, D])
        xin = sb("xin", [P, 4, D])
        xb = sb("xb", [P, 2, D])
        at = sb("at", [P, 2, KC, P])
        y = sb("y", [P, 2, D])
        ps_t = c.enter_context(nc.psum_tensor(f"{tag}_ps_t", [P, 2, KC, P], F32))
        ps_y = c.enter_context(nc.psum_tensor(f"{tag}_ps_y", [P, 2, D], F32))
        w_in = sem("w_in")
        a_in = [sem("a_in0"), sem("a_in1")]
        x_in = [sem("x_in0"), sem("x_in1")]
        y_out = [sem("y_out0"), sem("y_out1")]
        transposed, at_made, xb_made, ps_made, y_made = map(sem, ("transposed", "at_made", "xb_made", "ps_made", "y_made"))
        block = c.enter_context(nc.Block())

        def seen(t, s):
            return t // 2 + 1 if isinstance(t, int) else (t - s) // 2 + 1

        @block.sync
        def _(sp):
            sp.dma_start(w[:], wo_t.rearrange("(c p) n -> p c n", p=P)).then_inc(w_in, 16)
            sp.dma_start(bv_sb[:], bv.rearrange("(c p) -> p c", p=P), allow_slow_non_contiguous=True).then_inc(w_in, 16)
            sp.dma_start(bo_sb[:], bo[None, :].broadcast_to([P, D])).then_inc(w_in, 16)

            def load(t, s):
                if not early(t, 2):
                    sp.wait_ge(transposed, t - 1)
                    sp.wait_ge(xb_made, t - 1)
                sp.dma_start(ain[:, s], a[bass.ds(t * P, P), :]).then_inc(a_in[s], 16)
                sp.dma_start(xin[:, s], x[bass.ds(t * P, P), :]).then_inc(x_in[s], 16)

            def store(t, s):
                sp.wait_ge(y_made, t + 1)
                sp.dma_start(out[bass.ds(t * P, P), :], y[:, s]).then_inc(y_out[s], 16)

            load(0, 0)
            load(1, 1)
            with sp.Fori(0, NT // 2 - 1) as i:
                for s in range(2):
                    load(2 * i + s + 2, s)
                    store(2 * i + s, s)
            store(NT - 2, 0)
            store(NT - 1, 1)
            for s in range(2):
                sp.wait_ge(y_out[s], 16 * (NT // 2))

        @block.gpsimd
        def _(pool):
            pool.wait_ge(w_in, 48)

            def pair(i, first):
                for s in range(2):
                    pool.wait_ge(x_in[s], 16 * i + 16)
                    if not first:
                        pool.wait_ge(y_made, 2 * i + s - 1)
                    nc.gpsimd.tensor_tensor(xb[:, s], xin[:, s], bo_sb[:], ALU.add).then_inc(xb_made, 1)
            pair(0, True)
            with pool.Fori(1, NT // 2) as i:
                pair(i, False)

        @block.scalar
        def _(act):
            act.wait_ge(w_in, 48)

            def step(t, s):
                act.wait_ge(transposed, t + 1)
                if not early(t, 2):
                    act.wait_ge(ps_made, t - 1)
                for k in range(KC):
                    last = nc.scalar.activation(at[:, s, k], ps_t[:, s, k], ACT.Identity, bias=bv_sb[:, k:k + 1])
                last.then_inc(at_made, 1)
            over_tiles(act, step)

        @block.vector
        def _(dve):
            def pair(i, first):
                for s in range(2):
                    t = 2 * i + s
                    dve.wait_ge(ps_made, t + 1)
                    dve.wait_ge(xb_made, t + 1)
                    if not first:
                        dve.wait_ge(y_out[s], 16 * i)
                    nc.vector.tensor_tensor(y[:, s], ps_y[:, s], xb[:, s], ALU.add).then_inc(y_made, 1)
            pair(0, True)
            with dve.Fori(1, NT // 2) as i:
                pair(i, False)

        @block.tensor
        def _(pe):
            def turn(i, s, first):
                pe.wait_ge(a_in[s], 16 * i + 16)
                if not first:
                    pe.wait_ge(at_made, 2 * i + s - 1)
                for k in range(KC):
                    last = nc.tensor.transpose(ps_t[:, s, k], ain[:, s, k * P:(k + 1) * P], ident[:])
                last.then_inc(transposed, 1)

            def project(i, s, first):
                pe.wait_ge(at_made, 2 * i + s + 1)
                if not first:
                    pe.wait_ge(y_made, 2 * i + s - 1)
                for k in range(KC):
                    last = nc.tensor.matmul(ps_y[:, s], at[:, s, k], w[:, k], start=k == 0, stop=k == KC - 1)
                last.then_inc(ps_made, 1)

            pe.wait_ge(w_in, 48)
            turn(0, 0, True)
            turn(0, 1, True)
            project(0, 0, True)
            turn(1, 0, False)
            project(0, 1, True)
            turn(1, 1, False)
            with pe.Fori(1, NT // 2 - 1) as i:
                for s in range(2):
                    project(i, s, False)
                    turn(i + 1, s, False)
            project(NT // 2 - 1, 0, False)
            project(NT // 2 - 1, 1, False)


def quantized_ffn(nc, tag, ident, x, w8_t, w_scale, bias, out):
    FP8_MAX = 448.0
    U8 = mybir.dt.uint8
    with nc.cleanup_on_exit(), ExitStack() as c:
        def sb(name, shape, dt=F32):
            return c.enter_context(nc.sbuf_tensor(f"{tag}_{name}", shape, dt))

        def sem(name):
            return nc.alloc_semaphore(f"{tag}_{name}")

        w8 = sb("w8", [P, KC, D], U8)
        code = sb("code", [P, KC, D], I32)
        field = sb("field", [P, KC, D], I32)
        tmp = sb("tmp", [P, KC, D], F32)
        wv_ = sb("wval", [P, KC, D], F32)
        w = sb("w", [P, KC, D], BF16)
        ident_b = sb("ident_b", [P, P], BF16)
        ws = sb("ws", [P, 1])
        b_sb = sb("b", [P, D])
        xin = sb("xin", [P, 2, D])
        xb = sb("xb", [P, 2, D])
        stats = sb("stats", [P, 2, 6])
        mv = sb("mv", [P, 2, 2])
        ve = sb("ve", [P, 2, 1])
        rstd = sb("rstd", [P, 2, 1])
        power = sb("power", [P, 1])
        xn = sb("xn", [P, 2, D])
        amax = sb("amax", [P, 2, 1])
        xs = sb("xs", [P, 2, 1])
        inv = sb("inv", [P, 2, 1])
        scale = sb("scale", [P, 2, 1])
        v = sb("v", [P, 2, D])
        magic = sb("magic", [P, 2, D])
        vm = sb("vm", [P, 2, D])
        q = sb("q", [P, 2, D], BF16)
        qt = sb("qt", [P, 2, KC, P], BF16)
        y = sb("y", [P, 2, D])
        ps_t = c.enter_context(nc.psum_tensor(f"{tag}_ps_t", [P, 2, 2 * KC, P], BF16))
        ps_y = c.enter_context(nc.psum_tensor(f"{tag}_ps_y", [P, 2, D], F32))
        w_in, held, power_set, wchain = sem("w_in"), sem("held"), sem("power_set"), sem("wchain")
        x_in = [sem("x_in0"), sem("x_in1")]
        y_out = [sem("y_out0"), sem("y_out1")]
        chain, ve_made, rstd_made, xb_made, q_made, transposed, qt_made, ps_made, y_made = map(
            sem, ("chain", "ve_made", "rstd_made", "xb_made", "q_made", "transposed", "qt_made", "ps_made", "y_made"))
        block = c.enter_context(nc.Block())

        @block.sync
        def _(sp):
            sp.dma_start(w8[:], w8_t.rearrange("(c p) n -> p c n", p=P)).then_inc(w_in, 16)
            sp.dma_start(ws[:], w_scale[None, :].broadcast_to([P, 1])).then_inc(w_in, 16)
            sp.dma_start(b_sb[:], bias[None, :].broadcast_to([P, D])).then_inc(w_in, 16)

            def load(i, s, first):
                if not first:
                    sp.wait_ge(q_made, 2 * i + s - 1)
                    sp.wait_ge(xb_made, 2 * i + s - 1)
                sp.dma_start(xin[:, s], x[bass.ds((2 * i + s) * P, P), :]).then_inc(x_in[s], 16)

            def store(i, s):
                sp.wait_ge(y_made, 2 * i + s + 1)
                sp.dma_start(out[bass.ds((2 * i + s) * P, P), :], y[:, s]).then_inc(y_out[s], 16)

            load(0, 0, True)
            load(0, 1, True)
            with sp.Fori(0, NT // 2 - 1) as i:
                for s in range(2):
                    load(i + 1, s, False)
                    store(i, s)
            for s in range(2):
                store(NT // 2 - 1, s)
            for s in range(2):
                sp.wait_ge(y_out[s], 16 * (NT // 2))

        @block.gpsimd
        def _(pool):
            nc.gpsimd.memset(power[:], -0.5).then_inc(power_set, 1)
            nc.gpsimd.tensor_copy(ident_b[:], ident[:]).then_inc(power_set, 1)
            pool.wait_ge(power_set, 2)
            pool.wait_ge(w_in, 48)

            def step(i, s, first):
                t = 2 * i + s
                pool.wait_ge(ve_made, t + 1)
                if not first:
                    pool.wait_ge(q_made, t - 1)
                nc.gpsimd.tensor_tensor(rstd[:, s], ve[:, s], power[:], ALU.pow).then_inc(rstd_made, 1)
                if not first:
                    pool.wait_ge(y_made, t - 1)
                nc.gpsimd.tensor_tensor(xb[:, s], xin[:, s], b_sb[:], ALU.add).then_inc(xb_made, 1)
            for s in range(2):
                step(0, s, True)
            with pool.Fori(1, NT // 2) as i:
                for s in range(2):
                    step(i, s, False)

        @block.scalar
        def _(act):
            def step(i, s, first):
                t = 2 * i + s
                act.wait_ge(transposed, t + 1)
                if not first:
                    act.wait_ge(ps_made, t - 1)
                nc.scalar.copy(qt[:, s], ps_t[:, s, 0:KC]).then_inc(qt_made, 1)
            for s in range(2):
                step(0, s, True)
            with act.Fori(1, NT // 2) as i:
                for s in range(2):
                    step(i, s, False)

        @block.vector
        def _(dve):
            dve.wait_ge(w_in, 48)
            wl = Link(dve, wchain, 12)
            wl(nc.vector.tensor_copy(code[:], w8[:]))
            wl(nc.vector.tensor_scalar(field[:], code[:], 3, 15, ALU.logical_shift_right, ALU.bitwise_and))
            wl(nc.vector.tensor_scalar(tmp[:], field[:], 0.5, 8.0, ALU.is_ge, ALU.mult))
            wl(nc.vector.tensor_scalar(field[:], field[:], 1.0, 117.0, ALU.max, ALU.add))
            wl(nc.vector.tensor_scalar(field[:], field[:], 23, None, ALU.logical_shift_left))
            wl(nc.vector.tensor_copy(wv_[:], field[:].bitcast(F32)))
            wl(nc.vector.tensor_scalar(field[:], code[:], 7, None, ALU.bitwise_and))
            wl(nc.vector.tensor_tensor(tmp[:], tmp[:], field[:], ALU.add))
            wl(nc.vector.tensor_tensor(tmp[:], tmp[:], wv_[:], ALU.mult))
            wl(nc.vector.tensor_scalar(field[:], code[:], 7, None, ALU.logical_shift_right))
            wl(nc.vector.tensor_scalar(wv_[:], field[:], -2.0, 1.0, ALU.mult, ALU.add))
            wl(nc.vector.tensor_tensor(w[:], tmp[:], wv_[:], ALU.mult))
            link = Link(dve, chain, 11)

            def quantize(i, s, first):
                t = 2 * i + s
                link.start(t)
                dve.wait_ge(x_in[s], 16 * i + 16)
                link(nc.vector.bn_stats(stats[:, s], xin[:, s]), held)
                link(nc.vector.bn_aggr(mv[:, s], stats[:, s]))
                nc.vector.tensor_scalar(ve[:, s], mv[:, s, 1:2], EPS, None, ALU.add).then_inc(ve_made, 1)
                dve.wait_ge(rstd_made, t + 1)
                link(nc.vector.tensor_scalar(xn[:, s], xin[:, s], mv[:, s, 0:1], rstd[:, s], ALU.subtract, ALU.mult))
                link(nc.vector.tensor_reduce(amax[:, s], xn[:, s], axis=AX.X, op=ALU.max, apply_absolute_value=True))
                link(nc.vector.tensor_scalar(xs[:, s], amax[:, s], 1e-12, 1.0 / FP8_MAX, ALU.max, ALU.mult))
                link(nc.vector.reciprocal(inv[:, s], xs[:, s]))
                if not first:
                    dve.wait_ge(y_made, t - 1)
                link(nc.vector.tensor_scalar(scale[:, s], xs[:, s], ws[:], None, ALU.mult))
                link(nc.vector.tensor_scalar(v[:, s], xn[:, s], inv[:, s], None, ALU.mult))
                link(nc.vector.tensor_scalar(magic[:, s].bitcast(I32), v[:, s].bitcast(I32), 0x7F800000, None,
                                             ALU.bitwise_and))
                link(nc.vector.tensor_scalar(magic[:, s], magic[:, s], 2.0 ** -6, 1.5 * 2.0 ** 20, ALU.max, ALU.mult))
                link(nc.vector.tensor_tensor(vm[:, s], v[:, s], magic[:, s], ALU.add))
                if not first:
                    dve.wait_ge(transposed, t - 1)
                nc.vector.tensor_tensor(q[:, s], vm[:, s], magic[:, s], ALU.subtract).then_inc(q_made, 1)

            def finish(i, s, first):
                t = 2 * i + s
                dve.wait_ge(ps_made, t + 1)
                dve.wait_ge(xb_made, t + 1)
                if not first:
                    dve.wait_ge(y_out[s], 16 * i)
                nc.vector.scalar_tensor_tensor(y[:, s], ps_y[:, s], scale[:, s], xb[:, s], ALU.mult, ALU.add
                                               ).then_inc(y_made, 1)

            quantize(0, 0, True)
            quantize(0, 1, True)
            for s in range(2):
                finish(0, s, True)
                quantize(1, s, False)
            with dve.Fori(1, NT // 2 - 1) as i:
                for s in range(2):
                    finish(i, s, False)
                    quantize(i + 1, s, False)
            for s in range(2):
                finish(NT // 2 - 1, s, False)

        @block.tensor
        def _(pe):
            pe.wait_ge(power_set, 2)
            pe.wait_ge(wchain, 12)

            def step(i, s, first):
                t = 2 * i + s
                pe.wait_ge(q_made, t + 1)
                if not first:
                    pe.wait_ge(qt_made, t - 1)
                for k in range(KC):
                    last = nc.tensor.transpose(ps_t[:, s, k], q[:, s, k * P:(k + 1) * P], ident_b[:])
                last.then_inc(transposed, 1)
                pe.wait_ge(qt_made, t + 1)
                if not first:
                    pe.wait_ge(y_made, t - 1)
                for k in range(KC):
                    last = nc.tensor.matmul(ps_y[:, s], qt[:, s, k], w[:, k], start=k == 0, stop=k == KC - 1)
                last.then_inc(ps_made, 1)
            for s in range(2):
                step(0, s, True)
            with pe.Fori(1, NT // 2) as i:
                for s in range(2):
                    step(i, s, False)


E_, I_, KTOP = 128, 128, 8
NG, GE, TG = 8, 16, 4
NS = 2
TILES = N * KTOP // P + E_
BIG = 3.0e38


class RouteState:

    def __init__(self, nc, c):
        def sb(name, shape, dt=F32):
            return c.enter_context(nc.sbuf_tensor(f"r_{name}", shape, dt))
        self.mask = sb("mask", [P, NT, E_], BF16)
        self.cand = sb("cand", [P, NT, E_])
        self.top = sb("top", [P, NT, 8])
        self.rank = sb("rank", [P, NT, E_])
        self.before = sb("before", [P, NT + 1, E_], BF16)
        self.first = sb("first", [P, E_])
        self.eid = sb("eid", [1, TILES], I32)
        self.lofs = sb("lofs", [1, TILES], I32)
        self.ends = sb("ends", [1, E_], I32)


def route(nc, tag, ident, st, x, wg_t, ws_gu, ws_d, xf, base, lists):
    with nc.cleanup_on_exit(), ExitStack() as c:
        def sb(name, shape, dt=F32):
            return c.enter_context(nc.sbuf_tensor(f"{tag}_{name}", shape, dt))

        def sem(name):
            return nc.alloc_semaphore(f"{tag}_{name}")

        def ps(name, shape):
            return c.enter_context(nc.psum_tensor(f"{tag}_{name}", shape, F32))

        wg = sb("wg", [P, KC, E_])
        wgu = sb("wgu", [P, NS, KC, 2 * I_])
        wd = sb("wd", [P, NS, D])
        xin = sb("xin", [P, 2, D])
        xres = sb("xres", [P, 2, D])
        token_i = sb("token_i", [P, 2, 1], I32)
        stats = sb("stats", [P, 2, 6])
        mv = sb("mv", [P, 2, 2])
        ve = sb("ve", [P, 2, 1])
        rstd = sb("rstd", [P, 2, 1])
        power = sb("power", [P, 1])
        xn = sb("xn", [P, 2, D])
        xnt = sb("xnt", [P, 2, KC, P])
        silu = sb("silu", [P, 2, NS, P])
        hid = sb("hid", [P, 2, NS, P])
        lg = sb("lg", [P, 2, NG, GE + TG])
        top_g = sb("top_g", [P, NG, 8])
        take_g = sb("take_g", [P, NG, 8])
        rep_g = sb("rep_g", [P, NG, GE + TG])
        rep = sb("rep", [P, E_])
        cand = sb("cand", [P, E_])
        top = sb("top", [P, 8])
        slot = sb("slot", [P, 2, E_])
        ebase = sb("ebase", [P, E_])
        top_s = sb("top_s", [P, 8])
        slot_i = sb("slot_i", [P, 2, 8], I32)
        token = sb("token", [P, NT], I32)
        zeros = sb("zeros", [P, SQ * B], I32)
        tri = sb("tri", [P, P], BF16)
        ones = sb("ones", [P, P], BF16)
        y = sb("y", [P, 2, D])
        ps_t = ps("ps_t", [P, 2, KC, P])
        ps_l = ps("ps_l", [P, 512])
        ps_r = ps("ps_r", [P, 512])
        ps_g = ps("ps_g", [P, 2, 2 * NS, P])
        ps_y = ps("ps_y", [P, 2, D])
        w_in, const_made, held = sem("w_in"), sem("const_made"), sem("held")
        x_in = [sem("x_in0"), sem("x_in1")]
        xr_in = [sem("xr_in0"), sem("xr_in1")]
        xf_out = [sem("xf_out0"), sem("xf_out1")]
        y_out = [sem("y_out0"), sem("y_out1")]
        zero_out, list_out = sem("zero_out"), [sem("list_out0"), sem("list_out1")]
        chain, ve_made, rstd_made, normed, transposed, xnt_made = map(
            sem, ("chain", "ve_made", "rstd_made", "normed", "transposed", "xnt_made"))
        logits_made, lg_made, mask_made, before_made, rank_made, rank_read = map(
            sem, ("logits_made", "lg_made", "mask_made", "before_made", "rank_made", "rank_read"))
        gu_made, silu_made, hid_made, y_ps_made, y_made, slot_made, rchain, pchain, token_made = map(
            sem, ("gu_made", "silu_made", "hid_made", "y_ps_made", "y_made", "slot_made", "rchain", "pchain", "token_made"))
        block = c.enter_context(nc.Block())
        lists_rows = lists[:, :].rearrange("(e n) o -> e (n o)", n=N)

        @block.sync
        def _(sp):
            sp.dma_start(wg[:], wg_t.rearrange("(c p) n -> p c n", p=P)).then_inc(w_in, 16)
            for m in range(NS):
                sp.dma_start(wgu[:, m], ws_gu[m].rearrange("(c p) n -> p c n", p=P)).then_inc(w_in, 16)
                sp.dma_start(wd[:, m], ws_d[m]).then_inc(w_in, 16)
            sp.wait_ge(const_made, 1)
            sp.dma_start(lists_rows, zeros[:]).then_inc(zero_out, 16)

            def load_x(i, s, first):
                if not first:
                    sp.wait_ge(normed, 2 * i + s - 1)
                sp.dma_start(xin[:, s], x[bass.ds((2 * i + s) * P, P), :]).then_inc(x_in[s], 16)

            def load_xres(i, s, first):
                if not first:
                    sp.wait_ge(y_made, 2 * i + s - 1)
                sp.dma_start(xres[:, s], x[bass.ds((2 * i + s) * P, P), :]).then_inc(xr_in[s], 16)

            def store_xf(i, s):
                sp.wait_ge(normed, 2 * i + s + 1)
                sp.dma_start(xf[bass.ds((2 * i + s) * P, P), :], xn[:, s]).then_inc(xf_out[s], 16)

            def store_y(i, s):
                sp.wait_ge(y_made, 2 * i + s + 1)
                sp.dma_start(base[bass.ds((2 * i + s) * P, P), :], y[:, s]).then_inc(y_out[s], 16)

            for s in range(2):
                load_x(0, s, True)
                load_xres(0, s, True)
            for s in range(2):
                store_xf(0, s)
                load_x(1, s, False)

            def both(i, last):
                for s in range(2):
                    store_xf(i + 1, s)
                    if not last:
                        load_x(i + 2, s, False)
                    store_y(i, s)
                    load_xres(i + 1, s, False)
            with sp.Fori(0, NT // 2 - 2) as i:
                both(i, False)
            both(NT // 2 - 2, True)
            for s in range(2):
                store_y(NT // 2 - 1, s)
            for s in range(2):
                sp.wait_ge(y_out[s], 16 * (NT // 2))
                sp.wait_ge(xf_out[s], 16 * (NT // 2))

        @block.gpsimd
        def _(pool):
            nc.gpsimd.memset(zeros[:], 0).then_inc(const_made, 1)
            nc.gpsimd.memset(power[:], -0.5).then_inc(const_made, 1)
            nc.gpsimd.memset(ones[:], 1.0).then_inc(const_made, 1)
            nc.gpsimd.memset(tri[:], 1.0).then_inc(const_made, 1)
            nc.gpsimd.memset(lg[:], BIG).then_inc(const_made, 1)
            nc.gpsimd.memset(take_g[:], BIG).then_inc(const_made, 1)
            nc.gpsimd.memset(st.before[:, 0], 0.0).then_inc(const_made, 1)
            nc.gpsimd.iota(ebase[:], pattern=[[N, E_]], base=1, channel_multiplier=0,
                           allow_small_or_imprecise_dtypes=True).then_inc(const_made, 1)
            nc.gpsimd.iota(token[:], pattern=[[P, NT]], base=0, channel_multiplier=1).then_inc(const_made, 1)
            pool.wait_ge(const_made, 9)
            nc.gpsimd.affine_select(out=tri[:], in_=tri[:], compare_op=ALU.is_ge, fill=0.0, base=-1,
                                    pattern=[[1, P]], channel_multiplier=-1).then_inc(const_made, 1)
            pool.wait_ge(const_made, 10)

            def rstd_of(i, s, first):
                t = 2 * i + s
                pool.wait_ge(ve_made, t + 1)
                if not first:
                    pool.wait_ge(normed, t - 1)
                nc.gpsimd.tensor_tensor(rstd[:, s], ve[:, s], power[:], ALU.pow).then_inc(rstd_made, 1)

            def scatter(i, s):
                t = 2 * i + s
                if not (isinstance(t, int) and t < 2):
                    pool.wait_ge(list_out[s], 16 * KTOP * i)
                nc.gpsimd.tensor_copy(token_i[:, s], token[:, bass.ds(t, 1)]).then_inc(token_made, 1)
                pool.wait_ge(token_made, t + 1)
                hold(pool, slot_made, t + 1, held)
                for k in range(KTOP):
                    nc.gpsimd.indirect_dma_start(
                        lists[:, :], bass.IndirectOffsetOnAxis(ap=slot_i[:, s, k:k + 1], axis=0),
                        token_i[:, s], None).then_inc(list_out[s], 16)

            rstd_of(0, 0, True)
            rstd_of(0, 1, True)
            pool.wait_ge(zero_out, 16)
            rstd_of(1, 0, False)
            rstd_of(1, 1, False)
            scatter(0, 0)

            def both(i):
                rstd_of(i + 1, 0, False)
                scatter(i - 1, 1)
                rstd_of(i + 1, 1, False)
                scatter(i, 0)
            both(1)
            with pool.Fori(2, NT // 2 - 1) as i:
                both(i)
            scatter(NT // 2 - 2, 1)
            scatter(NT // 2 - 1, 0)
            scatter(NT // 2 - 1, 1)
            for s in range(2):
                pool.wait_ge(list_out[s], 16 * KTOP * (NT // 2))
            pool.wait_ge(before_made, NT)

        @block.scalar
        def _(act):
            act.wait_ge(const_made, 10)

            def turned(i, s, first):
                t = 2 * i + s
                act.wait_ge(transposed, t + 1)
                if not first:
                    act.wait_ge(gu_made, t - 1)
                nc.scalar.copy(xnt[:, s], ps_t[:, s]).then_inc(xnt_made, 1)

            def logits(i, s, first):
                t = 2 * i + s
                act.wait_ge(logits_made, t + 1)
                if not first:
                    act.wait_ge(mask_made, t - 1)
                nc.scalar.copy(lg[:, s, :, 0:GE], ps_l[:, 0:E_].rearrange("p (g e) -> p g e", g=NG)
                               ).then_inc(lg_made, 1)

            def gate(i, s, first):
                t = 2 * i + s
                act.wait_ge(gu_made, t + 1)
                if not first:
                    act.wait_ge(hid_made, t - 1)
                nc.scalar.activation(silu[:, s], ps_g[:, s, 0:NS], ACT.Silu).then_inc(silu_made, 1)

            def ranks(i, s):
                t = 2 * i + s
                act.wait_ge(rank_made, t + 1)
                nc.scalar.copy(st.rank[:, bass.ds(t, 1)], ps_r[:, None, 0:E_]).then_inc(rank_read, 1)

            turned(0, 0, True)
            logits(0, 0, True)
            gate(0, 0, True)
            turned(0, 1, True)
            logits(0, 1, True)
            gate(0, 1, True)
            ranks(0, 0)
            with act.Fori(1, NT // 2) as i:
                turned(i, 0, False)
                logits(i, 0, False)
                gate(i, 0, False)
                ranks(i - 1, 1)
                turned(i, 1, False)
                logits(i, 1, False)
                gate(i, 1, False)
                ranks(i, 0)
            ranks(NT // 2 - 1, 1)
            act.wait_ge(rank_read, NT)

        @block.vector
        def _(dve):
            dve.wait_ge(const_made, 10)
            nl = Link(dve, chain, 2)
            rl = Link(dve, rchain, 10)
            pl = Link(dve, pchain, 3)

            def statistics(i, s):
                t = 2 * i + s
                nl.start(t)
                dve.wait_ge(x_in[s], 16 * i + 16)
                nl(nc.vector.bn_stats(stats[:, s], xin[:, s]), held)
                nl(nc.vector.bn_aggr(mv[:, s], stats[:, s]))
                nc.vector.tensor_scalar(ve[:, s], mv[:, s, 1:2], EPS, None, ALU.add).then_inc(ve_made, 1)

            def norm(i, s, first):
                t = 2 * i + s
                dve.wait_ge(rstd_made, t + 1)
                if not first:
                    dve.wait_ge(transposed, t - 1)
                    dve.wait_ge(xf_out[s], 16 * i)
                nc.vector.tensor_scalar(xn[:, s], xin[:, s], mv[:, s, 0:1], rstd[:, s], ALU.subtract, ALU.mult
                                        ).then_inc(normed, 1)

            def hidden(i, s, first):
                t = 2 * i + s
                dve.wait_ge(silu_made, t + 1)
                if not first:
                    dve.wait_ge(y_ps_made, t - 1)
                nc.vector.tensor_tensor(hid[:, s], silu[:, s], ps_g[:, s, NS:2 * NS], ALU.mult).then_inc(hid_made, 1)

            def choose(i, s, first):
                t = 2 * i + s
                rl.start(t)
                hold(dve, lg_made, t + 1, held)
                for g in range(NG):
                    last = nc.vector.max(top_g[:, g], lg[:, s, g, 0:GE])
                rl(last)
                rl(nc.vector.tensor_copy(take_g[:, :, 0:TG], top_g[:, :, 0:TG]), held)
                for g in range(NG):
                    last = nc.vector.match_replace(rep_g[:, g], take_g[:, g], lg[:, s, g], -BIG)
                rl(last)
                rl(nc.vector.tensor_scalar(rep_g[:, :, 0:GE], rep_g[:, :, 0:GE], -BIG, 1.0, ALU.is_equal, ALU.subtract))
                rl(nc.vector.scalar_tensor_tensor(cand[:].rearrange("p (g e) -> p g e", g=NG), rep_g[:, :, 0:GE],
                                                  1.0e30, lg[:, s, :, 0:GE], ALU.mult, ALU.add), held)
                rl(nc.vector.max(top[:], cand[:]), held)
                rl(nc.vector.match_replace(rep[:], top[:], cand[:], -BIG))
                nc.vector.tensor_scalar(st.mask[:, bass.ds(t, 1)], rep[:, None, :], -BIG, None, ALU.is_equal
                                        ).then_inc(mask_made, 1)
                rl(nc.vector.tensor_copy(st.top[:, bass.ds(t, 1)], top[:, None, :]))
                dve.wait_ge(mask_made, t + 1)
                if not (isinstance(i, int) and t == 0):
                    dve.wait_ge(before_made, t)
                nc.vector.tensor_tensor(st.before[:, bass.ds(t + 1, 1)], st.before[:, bass.ds(t, 1)],
                                        st.mask[:, bass.ds(t, 1)], ALU.add).then_inc(before_made, 1)
                rl(nc.vector.tensor_scalar(rep[:], rep[:], -BIG, 1.0, ALU.is_equal, ALU.subtract))
                rl(nc.vector.scalar_tensor_tensor(st.cand[:, bass.ds(t, 1)], rep[:, None, :], 1.0e30, cand[:, None, :],
                                                  ALU.mult, ALU.add))

            def place(i, s, first):
                t = 2 * i + s
                pl.start(t)
                dve.wait_ge(rank_read, t + 1)
                pl(nc.vector.tensor_tensor(slot[:, s, None, :], st.rank[:, bass.ds(t, 1)], ebase[:, None, :], ALU.add))
                pl(nc.vector.tensor_tensor(slot[:, s, None, :], slot[:, s, None, :], st.mask[:, bass.ds(t, 1)], ALU.mult),
                   held)
                pl(nc.vector.max(top_s[:], slot[:, s]))
                if not first:
                    dve.wait_ge(list_out[s], 16 * KTOP * i)
                nc.vector.tensor_scalar(slot_i[:, s], top_s[:], -1.0, None, ALU.add).then_inc(slot_made, 1)

            def finish(i, s, first):
                t = 2 * i + s
                dve.wait_ge(y_ps_made, t + 1)
                dve.wait_ge(xr_in[s], 16 * i + 16)
                if not first:
                    dve.wait_ge(y_out[s], 16 * i)
                nc.vector.scalar_tensor_tensor(y[:, s], ps_y[:, s], 1.0 / NS, xres[:, s], ALU.mult, ALU.add
                                               ).then_inc(y_made, 1)

            for s in range(2):
                statistics(0, s)
                norm(0, s, True)

            def tile(i, s, first, last, before):
                if not last:
                    statistics(i + 1, s)
                choose(i, s, first)
                hidden(i, s, first)
                if before:
                    place(*before)
                    finish(*before)
                if not last:
                    norm(i + 1, s, False)

            tile(0, 0, True, False, None)
            tile(0, 1, True, False, (0, 0, True))
            tile(1, 0, False, False, (0, 1, True))
            tile(1, 1, False, False, (1, 0, False))
            with dve.Fori(2, NT // 2 - 1) as i:
                tile(i, 0, False, False, (i - 1, 1, False))
                tile(i, 1, False, False, (i, 0, False))
            last = NT // 2 - 1
            tile(last, 0, False, True, (last - 1, 1, False))
            tile(last, 1, False, True, (last, 0, False))
            place(last, 1, False)
            finish(last, 1, False)

        @block.tensor
        def _(pe):
            def turn(i, s, first):
                t = 2 * i + s
                pe.wait_ge(normed, t + 1)
                if not first:
                    pe.wait_ge(xnt_made, t - 1)
                for k in range(KC):
                    last = nc.tensor.transpose(ps_t[:, s, k], xn[:, s, k * P:(k + 1) * P], ident[:])
                last.then_inc(transposed, 1)

            def products(i, s, first):
                t = 2 * i + s
                pe.wait_ge(xnt_made, t + 1)
                if not (first and s == 0):
                    pe.wait_ge(lg_made, t)
                for k in range(KC):
                    last = nc.tensor.matmul(ps_l[:, 0:E_], xnt[:, s, k], wg[:, k], start=k == 0, stop=k == KC - 1)
                last.then_inc(logits_made, 1)
                if not first:
                    pe.wait_ge(hid_made, t - 1)
                for half in range(2):
                    for m in range(NS):
                        for k in range(KC):
                            last = nc.tensor.matmul(ps_g[:, s, half * NS + m], wgu[:, m, k, half * I_:(half + 1) * I_],
                                                    xnt[:, s, k], start=k == 0, stop=k == KC - 1)
                last.then_inc(gu_made, 1)

            def down(i, s, first):
                t = 2 * i + s
                pe.wait_ge(hid_made, t + 1)
                if not first:
                    pe.wait_ge(y_made, t - 1)
                for m in range(NS):
                    last = nc.tensor.matmul(ps_y[:, s], hid[:, s, m], wd[:, m], start=m == 0, stop=m == NS - 1)
                last.then_inc(y_ps_made, 1)

            def count(i, s, first):
                t = 2 * i + s
                pe.wait_ge(mask_made, t + 1)
                if not (first and s == 0):
                    pe.wait_ge(rank_read, t)
                    pe.wait_ge(before_made, t)
                nc.tensor.matmul(ps_r[:, 0:E_], tri[:], st.mask[:, bass.ds(t, 1)].rearrange("p o e -> p (o e)"),
                                 start=True, stop=False)
                nc.tensor.matmul(ps_r[:, 0:E_], ones[:], st.before[:, bass.ds(t, 1)].rearrange("p o e -> p (o e)"),
                                 start=False, stop=True).then_inc(rank_made, 1)

            pe.wait_ge(const_made, 10)
            pe.wait_ge(w_in, 16 * (1 + 2 * NS))
            turn(0, 0, True)
            products(0, 0, True)
            turn(0, 1, True)
            products(0, 1, True)
            count(0, 0, True)
            down(0, 0, True)

            def both(i):
                turn(i, 0, False)
                products(i, 0, False)
                count(i - 1, 1, False)
                down_(i - 1, 1)
                turn(i, 1, False)
                products(i, 1, False)
                count(i, 0, False)
                down(i, 0, False)

            def down_(i, s):
                down(i, s, isinstance(i, int) and i == 0)

            both(1)
            with pe.Fori(2, NT // 2) as i:
                both(i)
            count(NT // 2 - 1, 1, False)
            down(NT // 2 - 1, 1, False)


def tables(nc, tag, ident, st):
    with nc.cleanup_on_exit(), ExitStack() as c:
        def sb(name, shape, dt=F32):
            return c.enter_context(nc.sbuf_tensor(f"{tag}_{name}", shape, dt))

        def sem(name):
            return nc.alloc_semaphore(f"{tag}_{name}")

        def ps(name, shape):
            return c.enter_context(nc.psum_tensor(f"{tag}_{name}", shape, F32))

        onesb = sb("onesb", [P, P], BF16)
        cnt = sb("cnt", [P, E_])
        ntile = sb("ntile", [P, E_])
        zero = sb("zero", [P, E_])
        ends = sb("ends", [P, E_])
        cols = sb("cols", [P, 2, P])
        number = sb("number", [P, TILES])
        past = sb("past", [P, TILES])
        sums_w = sb("sums_w", [P, 2])
        row = sb("row", [1, TILES])
        row2 = sb("row2", [1, TILES])
        ps_c = ps("ps_c", [P, 512])
        ps_t = ps("ps_t", [P, 2, 512])
        ps_e = ps("ps_e", [P, 2, 512])
        const_made, pe_made, link_s = map(sem, ("const_made", "pe_made", "link"))
        block = c.enter_context(nc.Block())

        @block.gpsimd
        def _(pool):
            nc.gpsimd.memset(onesb[:], 1.0).then_inc(const_made, 1)
            nc.gpsimd.memset(zero[:], 0.0).then_inc(const_made, 1)
            nc.gpsimd.memset(sums_w[:], 1.0).then_inc(const_made, 1)
            nc.gpsimd.iota(number[:], pattern=[[1, TILES]], base=0, channel_multiplier=0,
                           allow_small_or_imprecise_dtypes=True).then_inc(const_made, 1)

        @block.tensor
        def _(pe):
            pe.wait_ge(const_made, 4)
            nc.tensor.matmul(ps_c[:, 0:E_], onesb[:], st.before[:, NT], start=True, stop=True).then_inc(pe_made, 1)
            pe.wait_ge(link_s, 5)
            nc.tensor.transpose(ps_t[:, 0, 0:P], ends[:], ident[:]).then_inc(pe_made, 1)
            nc.tensor.transpose(ps_t[:, 1, 0:P], ntile[:], ident[:]).then_inc(pe_made, 1)
            pe.wait_ge(link_s, 11)
            nc.tensor.matmul(ps_e[0:1, 0, 0:TILES], sums_w[:, 0:1], past[:], start=True, stop=True).then_inc(pe_made, 1)
            nc.tensor.matmul(ps_e[0:1, 1, 0:TILES], sums_w[:, 1:2], past[:], start=True, stop=True).then_inc(pe_made, 1)

        @block.vector
        def _(dve):
            link = Link(dve, link_s, 16)
            dve.wait_ge(pe_made, 1)
            link(nc.vector.tensor_copy(cnt[:], ps_c[:, 0:E_]))
            link(nc.vector.tensor_scalar(ntile[:], cnt[:], 1.0 / P, 127.0 / P - 0.5 + 1.0 / 256, ALU.mult, ALU.add))
            link(nc.vector.tensor_scalar(ntile[:], ntile[:], 12582912.0, None, ALU.add))
            link(nc.vector.tensor_scalar(ntile[:], ntile[:], -12582912.0, 1.0, ALU.add, ALU.max))
            dve.wait_ge(const_made, 4)
            link(nc.vector.tensor_tensor_scan(ends[:], ntile[:], zero[:], 0.0, ALU.add, ALU.add))
            link(nc.vector.tensor_tensor(st.first[:], ends[:], ntile[:], ALU.subtract))
            link(nc.vector.tensor_scalar(st.first[:], st.first[:], float(P), 1.0, ALU.mult, ALU.add))
            link(nc.vector.tensor_copy(st.ends[:], ends[0:1]))
            dve.wait_ge(pe_made, 3)
            link(nc.vector.tensor_copy(cols[:], ps_t[:, :, 0:P]))
            link(nc.vector.tensor_scalar(sums_w[:, 1:2], cols[:, 1, 0:1], -float(P), float(N), ALU.mult, ALU.add))
            link(nc.vector.tensor_scalar(past[:], number[:], cols[:, 0, 0:1], None, ALU.is_ge))
            dve.wait_ge(pe_made, 5)
            link(nc.vector.tensor_scalar(row[:], ps_e[0:1, 0, 0:TILES], float(E_ - 1), None, ALU.min))
            link(nc.vector.tensor_copy(st.eid[:], row[:]))
            link(nc.vector.tensor_scalar(row2[:], number[0:1], float(P), None, ALU.mult))
            link(nc.vector.tensor_tensor(row2[:], row2[:], ps_e[0:1, 1, 0:TILES], ALU.add))
            link(nc.vector.tensor_scalar(st.lofs[:], row2[:], float(E_ * N - P), None, ALU.min))


def experts(nc, tag, ident, st, xf, w_gu, w_d, lists, yo):
    WR, GR, LR = 4, 4, 8
    with nc.cleanup_on_exit(), ExitStack() as c:
        def sb(name, shape, dt=F32):
            return c.enter_context(nc.sbuf_tensor(f"{tag}_{name}", shape, dt))

        def sem(name):
            return nc.alloc_semaphore(f"{tag}_{name}")

        def ps(name, shape):
            return c.enter_context(nc.psum_tensor(f"{tag}_{name}", shape, F32))

        wgu = sb("wgu", [P, WR * KC * 2 * I_])
        wd = sb("wd", [P, WR * D])
        ids = sb("ids", [P, LR, 1], I32)
        xg = sb("xg", [P, GR, D])
        xt = sb("xt", [P, 2, KC, P])
        silu = sb("silu", [P, 2, I_])
        hid = sb("hid", [P, 2, I_])
        hid_t = sb("hid_t", [P, 2, P])
        y = sb("y", [P, 4, D])
        ps_t = ps("ps_t", [P, 2, KC, P])
        ps_g = ps("ps_g", [P, 2, 512])
        ps_h = ps("ps_h", [P, 2, 512])
        ps_y = ps("ps_y", [P, 2, D])
        held = sem("held")
        weights_ready = sem("weights_ready")
        w_in = [sem(f"w_in{s}") for s in range(WR)]
        ids_in = [sem(f"ids_in{s}") for s in range(LR)]
        xg_in = [sem(f"xg_in{s}") for s in range(GR)]
        y_out = [sem(f"y_out{s}") for s in range(4)]
        transposed, xt_made, gu_made, silu_made, hid_made, turned, hid_t_made, y_ps_made, y_made = map(
            sem, ("transposed", "xt_made", "gu_made", "silu_made", "hid_made", "turned", "hid_t_made", "y_ps_made",
                  "y_made"))
        block = c.enter_context(nc.Block())

        @block.sync
        def _(sp):
            def load(e, s):
                sp.dma_start(wgu[:, s * KC * 2 * I_:(s + 1) * KC * 2 * I_].rearrange("p (c n) -> p c n", c=KC),
                             w_gu[bass.ds(e * D, D), :].rearrange("(c p) n -> p c n", p=P)).then_inc(w_in[s], 16)
                sp.dma_start(wd[:, s * D:(s + 1) * D], w_d[bass.ds(e * I_, I_), :]).then_inc(w_in[s], 16)
            def arrived(i, s):
                sp.wait_ge(w_in[s], 32 * (i + 1))
                sp.sem_inc(weights_ready, 1)

            for s in range(WR):
                load(s, s)
            arrived(0, 0)
            arrived(0, 1)
            with sp.Fori(1, E_ // WR) as i:
                for s in range(WR):
                    arrived(*((i - 1, s + 2) if s + 2 < WR else (i, s + 2 - WR)))
                    end = sp.value_load(st.ends[0:1, bass.ds((i - 1) * WR + s, 1)], min_val=0, max_val=TILES)
                    sp.wait_ge(y_ps_made, end + 1)
                    load(i * WR + s, s)
            for s in range(2, WR):
                arrived(E_ // WR - 1, s)

        @block.gpsimd
        def _(pool):
            def gather(m, j, first):
                g = j % GR
                hold(pool, ids_in[j], 16 * m + 16, held)
                if not (first and j < GR):
                    hold(pool, transposed, 8 * m + j - GR + 1, held)
                nc.gpsimd.indirect_dma_start(xg[:, g], None, xf[:, :], bass.IndirectOffsetOnAxis(ap=ids[:, j], axis=0)
                                             ).then_inc(xg_in[g], 16)

            for s in range(LR // 2):
                at = pool.value_load(st.lofs[0:1, s:s + 1], min_val=0, max_val=E_ * N - P)
                nc.gpsimd.dma_start(ids[:, s], lists[bass.ds(at, P), :]).then_inc(ids_in[s], 16)

            def eight(m, first, last):
                for j in range(8):
                    gather(m, j, first)
                    ahead = j + LR // 2
                    if last and ahead >= 8:
                        continue
                    if not (first and ahead < 8):
                        pool.wait_ge(xg_in[ahead % GR], 16 * (2 * m + ahead // GR - 2 + 1))
                    at = pool.value_load(st.lofs[0:1, bass.ds(m * 8 + ahead, 1)], min_val=0, max_val=E_ * N - P)
                    nc.gpsimd.dma_start(ids[:, ahead % LR], lists[bass.ds(at, P), :]).then_inc(ids_in[ahead % LR], 16)
            eight(0, True, False)
            with pool.Fori(1, TILES // 8 - 1) as m:
                eight(m, False, False)
            eight(TILES // 8 - 1, False, True)

        @block.scalar
        def _(act):
            def store(i, s):
                act.wait_ge(y_made, i * 4 + s + 1)
                act.dma_start(yo[bass.ds((i * 4 + s) * P, P), :], y[:, s]).then_inc(y_out[s], 16)

            def copy_x(t, b, first):
                act.wait_ge(transposed, t + 1)
                if not first:
                    act.wait_ge(gu_made, t - 1)
                nc.scalar.copy(xt[:, b], ps_t[:, b]).then_inc(xt_made, 1)

            def gate(t, b, first):
                act.wait_ge(gu_made, t + 1)
                if not first:
                    act.wait_ge(hid_made, t - 1)
                nc.scalar.activation(silu[:, b], ps_g[:, b, 0:I_], ACT.Silu).then_inc(silu_made, 1)

            copy_x(0, 0, True)

            def four(i, first, last):
                for s in range(4):
                    t = i * 4 + s
                    gate(t, s % 2, first and s < 2)
                    if not (last and s == 3):
                        copy_x(t + 1, (s + 1) % 2, first and s < 1)
                    if not (first and s < 2):
                        store(*((i, s - 2) if s >= 2 else (i - 1, s + 2)))
            four(0, True, False)
            with act.Fori(1, TILES // 4 - 1) as i:
                four(i, False, False)
            four(TILES // 4 - 1, False, True)
            store(TILES // 4 - 1, 2)
            store(TILES // 4 - 1, 3)
            for s in range(4):
                act.wait_ge(y_out[s], 16 * (TILES // 4))

        @block.vector
        def _(dve):
            def multiply(t, b, first):
                dve.wait_ge(silu_made, t + 1)
                if not first:
                    dve.wait_ge(turned, t - 1)
                nc.vector.tensor_tensor(hid[:, b], silu[:, b], ps_g[:, b, I_:2 * I_], ALU.mult).then_inc(hid_made, 1)

            def copy_h(t, b, first):
                dve.wait_ge(turned, t + 1)
                if not first:
                    dve.wait_ge(y_ps_made, t)
                nc.vector.tensor_copy(hid_t[:, b], ps_h[:, b, 0:P]).then_inc(hid_t_made, 1)

            def copy_y(i, s, first):
                t = i * 4 + s
                dve.wait_ge(y_ps_made, t + 2)
                if not first:
                    dve.wait_ge(y_out[s], 16 * i)
                nc.vector.tensor_copy(y[:, s], ps_y[:, s % 2]).then_inc(y_made, 1)

            def four(i, first):
                for s in range(4):
                    t = i * 4 + s
                    multiply(t, s % 2, first and s < 2)
                    if not (first and s == 0):
                        copy_y(*((i, s - 1, first) if s else (i - 1, 3, False)))
                    copy_h(t, s % 2, first and s < 2)
            four(0, True)
            multiply(4, 0, False)
            dve.wait_ge(y_ps_made, 5)
            nc.vector.tensor_copy(y[:, 3], ps_y[:, 1]).then_inc(y_made, 1)
            copy_h(4, 0, False)
            for s in range(1, 4):
                multiply(4 + s, s % 2, False)
                copy_y(1, s - 1, False)
                copy_h(4 + s, s % 2, False)
            with dve.Fori(2, TILES // 4) as i:
                four(i, False)
            copy_y(TILES // 4 - 1, 3, False)

        @block.tensor
        def _(pe):
            def turn(t, s, n, first):
                pe.wait_ge(xg_in[s], 16 * n)
                if not first:
                    pe.wait_ge(xt_made, t - 1)
                for k in range(KC):
                    last = nc.tensor.transpose(ps_t[:, s % 2, k], xg[:, s, k * P:(k + 1) * P], ident[:])
                last.then_inc(transposed, 1)

            def weights_of(t):
                e = pe.value_load(st.eid[0:1, bass.ds(t, 1)], min_val=0, max_val=E_ - 1)
                pe.wait_ge(weights_ready, e + 1)
                slot = pe.snap(e & (WR - 1))
                return pe.snap(slot * (KC * 2 * I_)), pe.snap(slot * D)

            def gate_up(t, b, at, first):
                if not first:
                    pe.wait_ge(hid_made, t - 1)
                pe.wait_ge(xt_made, t + 1)
                for k in range(KC):
                    last = nc.tensor.matmul(ps_g[:, b, 0:2 * I_], xt[:, b, k], wgu[:, bass.ds(at + k * 2 * I_, 2 * I_)],
                                            start=k == 0, stop=k == KC - 1)
                last.then_inc(gu_made, 1)

            def turn_hidden(t, b, first):
                pe.wait_ge(hid_made, t + 1)
                if not first:
                    pe.wait_ge(hid_t_made, t - 1)
                nc.tensor.transpose(ps_h[:, b, 0:P], hid[:, b], ident[:]).then_inc(turned, 1)

            def down(t, b, at, first):
                if not first:
                    pe.wait_ge(y_made, t - 1)
                pe.wait_ge(hid_t_made, t + 1)
                nc.tensor.matmul(ps_y[:, b], hid_t[:, b], wd[:, bass.ds(at, D)], start=True, stop=True
                                 ).then_inc(y_ps_made, 1)

            pe.sem_inc(y_ps_made, 1)
            turn(0, 0, 1, True)

            def eight(i, first, last):
                at = weights_of(i * 8)
                for s in range(8):
                    t = i * 8 + s
                    gate_up(t, s % 2, at[0], first and s < 2)
                    if not (last and s == 7):
                        turn(t + 1, (s + 1) % 4, i * 2 + (s + 1) // 4 + 1, first and s < 1)
                    if s:
                        down(t - 1, (s - 1) % 2, before, first and s < 3)
                    before = at[1]
                    if s < 7:
                        at = weights_of(t + 1)
                    turn_hidden(t, s % 2, first and s < 2)
                down(i * 8 + 7, 1, before, False)
            eight(0, True, False)
            with pe.Fori(1, TILES // 8 - 1) as i:
                eight(i, False, False)
            eight(TILES // 8 - 1, False, True)


def combine(nc, tag, st, base, yo, out):
    with nc.cleanup_on_exit(), ExitStack() as c:
        def sb(name, shape, dt=F32):
            return c.enter_context(nc.sbuf_tensor(f"{tag}_{name}", shape, dt))

        def sem(name):
            return nc.alloc_semaphore(f"{tag}_{name}")

        place = sb("place", [P, 2, 8], I32)
        rows = sb("rows", [P, 2, KTOP, D])
        bin_ = sb("bin", [P, 2, D])
        acc = sb("acc", [P, 2, D])
        nmax = sb("nmax", [P, NT])
        ex = sb("ex", [P, 2, E_])
        total = sb("total", [P, 2])
        rtotal = sb("rtotal", [P, 1])
        pos = sb("pos", [P, E_])
        top = sb("top", [P, 8])
        junk = sb("junk", [P, 8, E_])
        w8 = sb("w8", [P, 8])
        weight = sb("weight", [P, 2, 8])
        y = sb("y", [P, 2, D])
        b_in = [sem("b_in0"), sem("b_in1")]
        rows_in = [sem("rows_in0"), sem("rows_in1")]
        y_out = [sem("y_out0"), sem("y_out1")]
        place_made, chain, y_made, held = sem("place_made"), sem("chain"), sem("y_made"), sem("held")
        nmax_made, ex_made, picks, tile_link = sem("nmax_made"), sem("ex_made"), sem("picks"), sem("tile_link")
        weight_made = sem("weight_made")
        block = c.enter_context(nc.Block())

        @block.sync
        def _(sp):
            def load(i, s, first):
                if not first:
                    sp.wait_ge(y_made, 2 * i + s - 1)
                sp.dma_start(bin_[:, s], base[bass.ds((2 * i + s) * P, P), :]).then_inc(b_in[s], 16)

            def store(i, s):
                sp.wait_ge(y_made, 2 * i + s + 1)
                sp.dma_start(out[bass.ds((2 * i + s) * P, P), :], y[:, s]).then_inc(y_out[s], 16)
            load(0, 0, True)
            load(0, 1, True)
            with sp.Fori(0, NT // 2 - 1) as i:
                for s in range(2):
                    store(i, s)
                    load(i + 1, s, False)
            for s in range(2):
                store(NT // 2 - 1, s)
            for s in range(2):
                sp.wait_ge(y_out[s], 16 * (NT // 2))

        @block.gpsimd
        def _(pool):
            def gather(i, s, first):
                t = 2 * i + s
                if not first:
                    hold(pool, y_made, t - 1, held)
                hold(pool, place_made, t + 1, held)
                for k in range(KTOP):
                    nc.gpsimd.indirect_dma_start(rows[:, s, k], None, yo[:, :],
                                                 bass.IndirectOffsetOnAxis(ap=place[:, s, k:k + 1], axis=0)
                                                 ).then_inc(rows_in[s], 16)
            for s in range(2):
                gather(0, s, True)
            with pool.Fori(1, NT // 2) as i:
                for s in range(2):
                    gather(i, s, False)

        @block.scalar
        def _(act):
            act.wait_ge(nmax_made, 1)

            def exponentials(i, s, first):
                t = 2 * i + s
                if not first:
                    act.wait_ge(weight_made, t - 1)
                nc.scalar.activation(ex[:, s], st.cand[:, bass.ds(t, 1)].rearrange("p o e -> p (o e)"), ACT.Exp,
                                     bias=nmax[:, bass.ds(t, 1)], accum_out=total[:, s:s + 1]).then_inc(ex_made, 1)
            for s in range(2):
                exponentials(0, s, True)
            with act.Fori(1, NT // 2) as i:
                for s in range(2):
                    exponentials(i, s, False)

        @block.vector
        def _(dve):
            link = Link(dve, chain, KTOP - 1)
            tl = Link(dve, tile_link, 4)
            nc.vector.tensor_scalar(nmax[:], st.top[:, :, 0], -1.0, None, ALU.mult).then_inc(nmax_made, 1)

            def choose(i, s, first):
                t = 2 * i + s
                tl.start(t)
                if not (first and s == 0):
                    dve.wait_ge(picks, (KTOP + 1) * t)
                tl(nc.vector.tensor_tensor(pos[:, None, :], st.rank[:, bass.ds(t, 1)], st.first[:, None, :], ALU.add))
                tl(nc.vector.tensor_tensor(pos[:, None, :], pos[:, None, :], st.mask[:, bass.ds(t, 1)], ALU.mult),
                   held)
                tl(nc.vector.max(top[:], pos[:]))
                if not first:
                    dve.wait_ge(rows_in[s], 16 * KTOP * i)
                nc.vector.tensor_scalar(place[:, s], top[:], -1.0, None, ALU.add).then_inc(place_made, 1)
                dve.wait_ge(ex_made, t + 1)
                tl(nc.vector.reciprocal(rtotal[:], total[:, s:s + 1]))
                for k in range(KTOP):
                    nc.vector.scalar_tensor_tensor(junk[:, k], pos[:], top[:, k:k + 1], ex[:, s], ALU.is_equal,
                                                   ALU.mult, accum_out=w8[:, k:k + 1]).then_inc(picks, 1)
                dve.wait_ge(picks, (KTOP + 1) * t + KTOP)
                nc.vector.tensor_scalar(weight[:, s], w8[:], rtotal[:], None, ALU.mult).then_inc(weight_made, 1)
                dve.sem_inc(picks, 1)

            def add(i, s, first):
                t = 2 * i + s
                link.start(t)
                dve.wait_ge(weight_made, t + 1)
                dve.wait_ge(b_in[s], 16 * i + 16)
                dve.wait_ge(rows_in[s], 16 * KTOP * i + 16 * KTOP)
                if not (first and s == 0):
                    dve.wait_ge(y_made, t)
                if not first:
                    dve.wait_ge(y_out[s], 16 * i)
                for k in range(KTOP):
                    src = bin_[:, s] if k == 0 else acc[:, (k - 1) % 2]
                    dst = y[:, s] if k == KTOP - 1 else acc[:, k % 2]
                    ins = nc.vector.scalar_tensor_tensor(
                        dst, rows[:, s, k], weight[:, s, k:k + 1], src,
                        ALU.mult, ALU.add)
                    if k < KTOP - 1:
                        link(ins)
                ins.then_inc(y_made, 1)
            for s in range(2):
                choose(0, s, True)
            for s in range(2):
                add(0, s, True)
                choose(1, s, False)
            with dve.Fori(1, NT // 2 - 1) as i:
                for s in range(2):
                    add(i, s, False)
                    choose(i + 1, s, False)
            for s in range(2):
                add(NT // 2 - 1, s, False)


def two_layers(nc, a, out):
    def dram(name, shape, dt=F32):
        return nc.dram_tensor(name, shape, dt, kind="Internal").ap()

    qh, ql = dram("q_high", [D, N]), dram("q_low", [D, N])
    att, x1, xf = dram("attended", [N, D]), dram("x_1", [N, D]), dram("x_normed", [N, D])
    base, x2, x3 = dram("x_shared", [N, D]), dram("x_2", [N, D]), dram("x_3", [N, D])
    lists = dram("token_lists", [E_ * N, 1], I32)
    yo = dram("expert_rows", [TILES * P, D])
    with ExitStack() as c:
        ident = make_identity(nc, c, "identity")
        norm_query(nc, "q0", ident, a["x"], a["L0_xattn_W_Q"], a["L0_xattn_b_Q"], qh, ql)
        attend(nc, "a0", ident, qh, ql, a["ctx_1024"], a["L0_xattn_W_K"], a["L0_xattn_b_K"], a["L0_xattn_W_V"], att,
               a["ctx_1024"].shape[2], False)
        out_project(nc, "o0", ident, att, a["L0_xattn_b_V"], a["L0_xattn_W_O"], a["L0_xattn_b_O"], a["x"], x1)
        with ExitStack() as cc:
            st = RouteState(nc, cc)
            route(nc, "rt", ident, st, x1, a["L0_ffn_Wg"], a["L0_ffn_Ws_gate_up"], a["L0_ffn_Ws_down"], xf, base, lists)
            tables(nc, "tb", ident, st)
            experts(nc, "ex", ident, st, xf, a["L0_ffn_W_gate_up"].rearrange("e k n -> (e k) n"),
                    a["L0_ffn_W_down"].rearrange("e k n -> (e k) n"), lists, yo)
            combine(nc, "cb", st, base, yo, x2)
        norm_query(nc, "q1", ident, x2, a["L1_xattn_Wq"], a["L1_xattn_bq"], qh, ql)
        attend(nc, "a1", ident, qh, ql, a["ctx_1024"], a["L1_xattn_Wk"], a["L1_xattn_bk"], a["L1_xattn_Wv"], att,
               SQ, True)
        out_project(nc, "o1", ident, att, a["L1_xattn_bv"], a["L1_xattn_Wo"], a["L1_xattn_bo"], x2, x3)
        quantized_ffn(nc, "f1", ident, x3, a["L1_ffn_weight"].bitcast(mybir.dt.uint8), a["L1_ffn_weight_scale"],
                      a["L1_ffn_bias"], out)


_TURNED = ("L0_xattn_W_Q", "L0_xattn_W_K", "L0_xattn_W_V", "L0_xattn_W_O", "L0_ffn_Wg",
           "L1_xattn_Wq", "L1_xattn_Wk", "L1_xattn_Wv", "L1_xattn_Wo", "L1_ffn_weight")


def kernel(**inputs):
    import numpy as np
    import concourse.bacc as bacc
    from concourse.bass_utils import run_bass_kernel_spmd

    nc = bacc.Bacc("TRN2", target_bir_lowering=False, num_devices=1)
    arrays, args = {}, {}
    for name, value in inputs.items():
        v = np.asarray(value)
        if name in _TURNED:
            v = v.T
        if name == "ctx_1024":
            v = v.transpose(2, 0, 1)
        if name == "x":
            v = v.reshape(N, D)
        v = np.ascontiguousarray(v.reshape(1) if v.ndim == 0 else v)
        arrays[f"in_{name}"] = v
        args[name] = nc.dram_tensor(f"in_{name}", v.shape, mybir.dt.from_np(v.dtype), kind="ExternalInput").ap()
    out = nc.dram_tensor("out", (N, D), F32, kind="ExternalOutput").ap()
    two_layers(nc, args, out)
    r = run_bass_kernel_spmd(nc, [arrays], core_ids=[0])
    return r.results[0]["out"].reshape(B, SQ, D)
```

```python
from contextlib import ExitStack

import concourse.bass as bass
from concourse import mybir
from concourse.alu_op_type import AluOpType as ALU

F32 = mybir.dt.float32
F32R = mybir.dt.float32r
BF16 = mybir.dt.bfloat16
I32 = mybir.dt.int32
U32 = mybir.dt.uint32
ACT = mybir.ActivationFunctionType
AX = mybir.AxisListType

P = 128
B, SQ, D = 16, 224, 512
N = B * SQ
NT = N // P
KC = D // P
H, DH = 16, 32
G = D // P
HG = P // DH
QH = SQ // 2
SC = float(DH) ** -0.5
EPS = 1e-5
MASKED = -1e30


def early(t, n):
    return isinstance(t, int) and t < n


def over_tiles(eng, step, n=NT):
    step(0, 0)
    step(1, 1)
    with eng.Fori(1, n // 2) as i:
        step(2 * i, 0)
        step(2 * i + 1, 1)


def make_identity(nc, c, name):
    ident = c.enter_context(nc.sbuf_tensor(name, [P, P], F32))
    with nc.cleanup_on_exit(), ExitStack() as s:
        zeroed = nc.alloc_semaphore(name + "_zeroed")
        block = s.enter_context(nc.Block())

        @block.gpsimd
        def _(pool):
            nc.gpsimd.memset(ident[:], 0.0).then_inc(zeroed, 1)
            pool.wait_ge(zeroed, 1)
            nc.gpsimd.affine_select(out=ident[:], in_=ident[:], compare_op=ALU.not_equal, fill=1.0,
                                    base=0, pattern=[[-1, P]], channel_multiplier=1).then_inc(zeroed, 1)
            pool.wait_ge(zeroed, 2)
    return ident


def norm_query(nc, tag, ident, x, w_t, bias, qh, ql):
    with nc.cleanup_on_exit(), ExitStack() as c:
        def sb(name, shape, dt=F32):
            return c.enter_context(nc.sbuf_tensor(f"{tag}_{name}", shape, dt))

        def sem(name):
            return nc.alloc_semaphore(f"{tag}_{name}")

        w = sb("w", [P, KC, D])
        b = sb("b", [P, KC])
        xin = sb("xin", [P, 4, D])
        stats = sb("stats", [P, 2, 6])
        mv = sb("mv", [P, 2, 2])
        ve = sb("ve", [P, 2, 1])
        rstd = sb("rstd", [P, 2, 1])
        power = sb("power", [P, 1])
        xn = sb("xn", [P, 2, D])
        xnt = sb("xnt", [P, 2, KC, P])
        qf = sb("qf", [P, 2, KC, P])
        q_hi = sb("q_hi", [P, 2, KC, P], F32R)
        q_lo = sb("q_lo", [P, 2, KC, P], F32R)
        ps_t = c.enter_context(nc.psum_tensor(f"{tag}_ps_t", [P, 2, KC, P], F32))
        ps_q = c.enter_context(nc.psum_tensor(f"{tag}_ps_q", [P, 2, KC, P], F32))
        w_in, power_set, held = sem("w_in"), sem("power_set"), sem("held")
        x_in = [sem(f"x_in{s}") for s in range(4)]
        q_out = [sem("q_out0"), sem("q_out1")]
        stats_made, mv_made, ve_made, rstd_made, normed = map(sem, ("stats_made", "mv_made", "ve_made", "rstd_made", "normed"))
        transposed, xnt_made, q_made, qf_made, hi_made, lo_made = map(
            sem, ("transposed", "xnt_made", "q_made", "qf_made", "hi_made", "lo_made"))
        block = c.enter_context(nc.Block())

        @block.sync
        def _(sp):
            sp.dma_start(w[:], w_t.rearrange("(c p) n -> p c n", p=P)).then_inc(w_in, 16)
            sp.dma_start(b[:], bias.rearrange("(c p) -> p c", p=P), allow_slow_non_contiguous=True).then_inc(w_in, 16)

            def load(t, s):
                if not early(t, 4):
                    sp.wait_ge(normed, t - 3)
                sp.dma_start(xin[:, s, :], x[bass.ds(t * P, P), :]).then_inc(x_in[s], 16)

            def store(t, s):
                sp.wait_ge(hi_made, t + 1)
                sp.wait_ge(lo_made, t + 1)
                for q, d in ((q_hi, qh), (q_lo, ql)):
                    sp.dma_start(d.rearrange("(c p) n -> p c n", p=P)[:, :, bass.ds(t * P, P)],
                                 q[:, s].bitcast(F32)).then_inc(q_out[s], 16)

            for s in range(4):
                load(s, s)
            with sp.Fori(0, NT // 4 - 1) as i:
                for s in range(4):
                    load(4 * i + s + 4, s)
                    store(4 * i + s, s % 2)
            for s in range(4):
                store(NT - 4 + s, s % 2)
            for s in range(2):
                sp.wait_ge(q_out[s], 32 * (NT // 2))

        @block.vector
        def _(dve):
            def norm(i, r):
                t, s = 4 * i + r, r % 2
                dve.wait_ge(x_in[r % 4], 16 * (i + r // 4 + 1))
                if not early(t, 2):
                    dve.wait_ge(rstd_made, t - 1)
                nc.vector.bn_stats(stats[:, s], xin[:, r % 4]).then_inc(stats_made, 1)
                hold(dve, stats_made, t + 1, held)
                nc.vector.bn_aggr(mv[:, s], stats[:, s]).then_inc(mv_made, 1)
                dve.wait_ge(mv_made, t + 1)
                nc.vector.tensor_scalar(ve[:, s], mv[:, s, 1:2], EPS, None, ALU.add).then_inc(ve_made, 1)

            def scale(i, r):
                t, s = 4 * i + r, r % 2
                dve.wait_ge(rstd_made, t + 1)
                if not early(t, 2):
                    dve.wait_ge(transposed, t - 1)
                nc.vector.tensor_scalar(xn[:, s], xin[:, r % 4], mv[:, s, 0:1], rstd[:, s], ALU.subtract, ALU.mult
                                        ).then_inc(normed, 1)

            def bias_add(t, s):
                dve.wait_ge(q_made, t + 1)
                if not early(t, 2):
                    dve.wait_ge(hi_made, t - 1)
                    dve.wait_ge(lo_made, t - 1)
                nc.vector.tensor_tensor(qf[:, s], ps_q[:, s], b[:, :, None].broadcast_to([P, KC, P]),
                                        ALU.add).then_inc(qf_made, 1)

            def low(t, s):
                dve.wait_ge(hi_made, t + 1)
                if not early(t, 2):
                    dve.wait_ge(q_out[s], (t - s) * 16)
                nc.vector.tensor_tensor(q_lo[:, s], qf[:, s], q_hi[:, s].bitcast(F32), ALU.subtract
                                        ).then_inc(lo_made, 1)

            dve.wait_ge(w_in, 32)
            norm(0, 0)
            scale(0, 0)
            norm(0, 1)
            scale(0, 1)

            def four(i, last):
                for s in range(4):
                    if not (last and s >= 2):
                        norm(i, s + 2)
                        scale(i, s + 2)
                    bias_add(4 * i + s, s % 2)
                    low(4 * i + s, s % 2)
            four(0, False)
            with dve.Fori(1, NT // 4 - 1) as i:
                four(i, False)
            four(NT // 4 - 1, True)

        @block.gpsimd
        def _(pool):
            nc.gpsimd.memset(power[:], -0.5).then_inc(power_set, 1)
            pool.wait_ge(power_set, 1)

            def step(t, s):
                pool.wait_ge(ve_made, t + 1)
                if not early(t, 2):
                    pool.wait_ge(normed, t - 1)
                nc.gpsimd.tensor_tensor(rstd[:, s], ve[:, s], power[:], ALU.pow).then_inc(rstd_made, 1)
            over_tiles(pool, step)

        @block.scalar
        def _(act):
            def copy_t(t, s):
                act.wait_ge(transposed, t + 1)
                if not early(t, 2):
                    act.wait_ge(q_made, t - 1)
                nc.scalar.copy(xnt[:, s], ps_t[:, s]).then_inc(xnt_made, 1)

            def high(t, s):
                act.wait_ge(qf_made, t + 1)
                if not early(t, 2):
                    act.wait_ge(q_out[s], (t - s) * 16)
                nc.scalar.copy(q_hi[:, s], qf[:, s]).then_inc(hi_made, 1)

            copy_t(0, 0)
            copy_t(1, 1)

            def both(i):
                for s in range(2):
                    high(2 * i + s, s)
                    copy_t(2 * i + s + 2, s)
            both(0)
            with act.Fori(1, NT // 2 - 1) as i:
                both(i)
            high(NT - 2, 0)
            high(NT - 1, 1)

        @block.tensor
        def _(pe):
            def turn(t, s):
                pe.wait_ge(normed, t + 1)
                if not early(t, 2):
                    pe.wait_ge(xnt_made, t - 1)
                for k in range(KC):
                    last = nc.tensor.transpose(ps_t[:, s, k], xn[:, s, k * P:(k + 1) * P], ident[:])
                last.then_inc(transposed, 1)

            def project(t, s):
                pe.wait_ge(xnt_made, t + 1)
                if not early(t, 2):
                    pe.wait_ge(qf_made, t - 1)
                for o in range(KC):
                    for k in range(KC):
                        last = nc.tensor.matmul(ps_q[:, s, o], w[:, k, o * P:(o + 1) * P], xnt[:, s, k],
                                                start=k == 0, stop=k == KC - 1)
                last.then_inc(q_made, 1)

            turn(0, 0)
            pe.wait_ge(w_in, 32)
            turn(1, 1)

            def both(i):
                for s in range(2):
                    project(2 * i + s, s)
                    turn(2 * i + s + 2, s)
            both(0)
            with pe.Fori(1, NT // 2 - 1) as i:
                both(i)
            project(NT - 2, 0)
            project(NT - 1, 1)


def attend(nc, tag, ident, qh, ql, ctx_t, wk_t, bk, wv_t, out, nkeys, causal):
    ck = 112 if causal else 125
    nc_k = nkeys // ck
    k_cuts = [(0, nkeys)] if causal else [(0, 375), (375, 750)]
    m_cuts = [(0, 0, QH), (1, 0, SQ)] if causal else [(q, a, e) for q in range(2) for a, e in ((0, 376), (376, 750))]
    if causal:
        s_cuts = [(0, 0, 0, 0, 0), (1, QH, 0, SQ, SQ)]
        s_pieces = [(0, 1, SQ + QH)]
        p_cols = SQ + QH
    else:
        s_cuts = [(k, 0, k // 2, (k % 2) * SQ, k * SQ) for k in range(nc_k)]
        s_pieces = [(0, 2, 2 * SQ), (2, 1, 2 * SQ)]
        p_cols = nc_k * SQ
    n_exp = len(s_pieces)
    v_plan = [[0], [1], [], []] if causal else [[0, 1], [2, 3], [4], [5]]
    n_kp = len(k_cuts)
    pj_batch = 4 * n_kp + nc_k
    KA = 3
    pj_pro = nc_k + KA * n_kp
    n_ring = HG * len(m_cuts) + 2
    assert pj_batch % 2 == 0 and n_ring % 2 == 0
    BI = 2
    NI = B // BI
    OC = 104

    with nc.cleanup_on_exit(), ExitStack() as c:
        def sb(name, shape, dt=F32):
            return c.enter_context(nc.sbuf_tensor(f"{tag}_{name}", shape, dt))

        def ps(name, shape):
            return c.enter_context(nc.psum_tensor(f"{tag}_{name}", shape, F32))

        def sem(name):
            return nc.alloc_semaphore(f"{tag}_{name}")

        wk = sb("wk", [P, KC, D])
        wv = sb("wv", [P, KC, D])
        bk_sb = sb("bk", [P, G])
        ct = sb("ct", [P, 2, KC, nkeys])
        qs = sb("qs", [P, 4, HG, SQ], F32R)
        ks = sb("ks", [P, 4, HG, nkeys], F32R)
        k_f = sb("k_f", [P, 2, 376])
        k_hi = sb("k_hi", [P, 2, nkeys], F32R)
        k_lo = sb("k_lo", [P, 2, nkeys], F32R)
        v = sb("v", [P, 2, nc_k, H, DH + 1])
        probs = sb("probs", [P, 2, p_cols])
        maxima = sb("maxima", [P, 2, HG, len(m_cuts)])
        m_col = sb("m_col", [P, 2, 2, P])
        one_hot = sb("one_hot", [HG, HG, nkeys])
        o_t = sb("o_t", [P, HG * QH])
        recip = sb("recip", [P, 2, 2, HG])
        o_sb = sb("o", [P, 2, 2, D])
        if causal:
            ident_b = sb("ident_b", [P, P], BF16)
            mask_qk = sb("mask_qk", [P, QH], BF16)
            mask_kq = sb("mask_kq", [P, QH], BF16)
        if causal:
            ps_s = ps("ps_s", [P, 2, 512])
        else:
            ps_s = ps("ps_s", [P, 3, 512])
        ps_m = ps("ps_m", [P, 2, 512])
        ps_j = ps("ps_j", [P, 2, 512])
        ps_o = ps("ps_o", [P, 512])

        w_in, held = sem("w_in"), sem("held")
        ones_in = sem("ones_in")
        ct_in = [sem("ct_in0"), sem("ct_in1")]
        qs_in = [sem(f"qs_in{s}") for s in range(4)]
        ks_in = [sem(f"ks_in{s}") for s in range(4)]
        pj_made, pj_read = sem("pj_made"), sem("pj_read")
        k_hi_made, k_lo_made = sem("k_hi_made"), sem("k_lo_made")
        ring_made, ring_read = sem("ring_made"), sem("ring_read")
        col_made = sem("col_made")
        st_made, exp_made = sem("st_made"), sem("exp_made")
        pv_made, recip_made, o_made = sem("pv_made"), sem("recip_made"), sem("o_made")
        o_t_made, turned = sem("o_t_made"), sem("turned")
        o_out = [sem("o_out0"), sem("o_out1")]

        with ExitStack() as cc:
            zeroed = sem("zeroed")
            pre = cc.enter_context(nc.Block())

            @pre.gpsimd
            def _(pool):
                nc.gpsimd.memset(one_hot[:], 1.0).then_inc(zeroed, 1)
                nc.gpsimd.memset(v[:], 1.0).then_inc(zeroed, 1)
                nc.gpsimd.memset(m_col[:], 0.0).then_inc(zeroed, 1)
                nc.gpsimd.memset(o_t[:], 0.0).then_inc(zeroed, 1)
                n = 4
                if causal:
                    nc.gpsimd.tensor_copy(ident_b[:], ident[:]).then_inc(zeroed, 1)
                    nc.gpsimd.memset(mask_qk[:], 0.0).then_inc(zeroed, 1)
                    nc.gpsimd.memset(mask_kq[:], 0.0).then_inc(zeroed, 1)
                    n = 7
                pool.wait_ge(zeroed, n)
                nc.gpsimd.affine_select(out=one_hot[:], in_=one_hot[:], compare_op=ALU.is_equal, fill=0.0,
                                        base=0, pattern=[[-1, HG], [0, nkeys]], channel_multiplier=1
                                        ).then_inc(zeroed, 1)
                n += 1
                if causal:
                    nc.gpsimd.affine_select(out=mask_qk[:], in_=mask_qk[:], compare_op=ALU.is_ge, fill=MASKED,
                                            base=0, pattern=[[-1, QH]], channel_multiplier=1).then_inc(zeroed, 1)
                    nc.gpsimd.affine_select(out=mask_kq[:], in_=mask_kq[:], compare_op=ALU.is_ge, fill=MASKED,
                                            base=0, pattern=[[1, QH]], channel_multiplier=-1).then_inc(zeroed, 1)
                    n += 2
                pool.wait_ge(zeroed, n)

        block = c.enter_context(nc.Block())

        class Step:

            def __init__(self, i, last):
                self.i, self.last = i, last

            def unit(self, w):
                return self.i * 8 + w

            def batch(self, w):
                return self.i * BI + w // 4

        def skip(st, w, ahead):
            return st.last and w + ahead >= 8

        def projections(st, w):
            n, mine = 0, []
            for x in range(w + 1):
                items = [] if skip(st, x, KA) else [(j, "k", j) for j in range(n_kp)]
                if not skip(st, x, 4):
                    items += [(2 + m, "v", j) for m, j in enumerate(v_plan[x % 4])]
                mine = [(*item, n + m) for m, item in enumerate(items)]
                n += len(items)
            return mine

        def iterate(eng, unit):
            for w in range(8):
                unit(Step(0, False), w)
            with eng.Fori(1, NI - 1) as i:
                for w in range(8):
                    unit(Step(i, False), w)
            for w in range(8):
                unit(Step(NI - 1, True), w)

        @block.sync
        def _(sp):
            sp.dma_start(wk[:], wk_t.rearrange("(c p) n -> p c n", p=P)).then_inc(w_in, 16)
            sp.dma_start(wv[:], wv_t.rearrange("(c p) n -> p c n", p=P)).then_inc(w_in, 16)
            sp.dma_start(bk_sb[:], bk.rearrange("(c p) -> p c", p=P), allow_slow_non_contiguous=True).then_inc(w_in, 16)
            for s in range(4):
                sp.dma_start(ks[3 * DH:3 * DH + HG, s].bitcast(F32), one_hot[:]).then_inc(ones_in, 16)

            def load_ct(b, s):
                sp.dma_start(ct[:, s], ctx_t.rearrange("(c p) b n -> p c b n", p=P)[:, :, bass.ds(b, 1), 0:nkeys]
                             .rearrange("p c b n -> p c (b n)")).then_inc(ct_in[s], 16)

            def load_qs(b, g, s):
                for part, src in ((0, qh), (1, ql), (2, qh)):
                    sp.dma_start(qs[part * DH:(part + 1) * DH, s].bitcast(F32),
                                 src[g * P:(g + 1) * P, bass.ds(b * SQ, SQ)].rearrange("(j d) n -> d j n", d=DH)
                                 ).then_inc(qs_in[s], 16)

            def stack_keys(s, n):
                sp.wait_ge(k_hi_made, n)
                sp.wait_ge(k_lo_made, n)
                for j in range(HG):
                    for part, src in ((0, k_hi), (1, k_hi), (2, k_lo)):
                        sp.dma_start(ks[part * DH:(part + 1) * DH, s, j].bitcast(F32),
                                     src[j * DH:(j + 1) * DH, s % 2].bitcast(F32)).then_inc(ks_in[s], 16)

            load_ct(0, 0)
            load_ct(1, 1)
            for g in range(4):
                load_qs(0, g, g)
            for s in range(KA):
                stack_keys(s, (s + 1) * n_kp)

            def unit(st, w):
                u = st.unit(w)
                if w % 4 == 4 - KA and not st.last:
                    sp.wait_ge(pj_made, st.i * BI * pj_batch + pj_pro + projections(st, w)[0][3])
                    load_ct(st.batch(w) + 2, (w // 4) % 2)
                if not skip(st, w, KA):
                    if not early(u, 5 - KA):
                        hold(sp, st_made, (u + KA - 3) * HG * n_exp, held)
                    stack_keys((w + KA) % 4, (u + KA + 1) * n_kp)
                if not skip(st, w, 4):
                    hold(sp, st_made, (u + 1) * HG * n_exp, held)
                    load_qs(st.batch(w) + 1, w % 4, w % 4)
                if w % 4 == 0 and not early(u, 1):
                    store(u, st.batch(w) - 1, (w // 4 + 1) % 2)

            def store(u, b, s):
                sp.wait_ge(o_made, 2 * u)
                sp.dma_start(out[bass.ds(b * SQ, SQ), :].rearrange("(q p) n -> p q n", p=QH),
                             o_sb[0:QH, s]).then_inc(o_out[s], 16)
            iterate(sp, unit)
            store(NI * 8, B - 1, 1)
            for s in range(2):
                sp.wait_ge(o_out[s], 16 * NI)

        @block.gpsimd
        def _(pool):
            def split(j, n, s, done):
                a, e = k_cuts[j]
                f = j if n_kp == 2 else s
                hold(pool, pj_read, done, held)
                nc.gpsimd.tensor_copy(k_hi[:, s, a:e], k_f[:, f, 0:e - a]).then_inc(k_hi_made, 1)
                pool.wait_ge(k_hi_made, n + 1)
                nc.gpsimd.tensor_tensor(k_lo[:, s, a:e], k_f[:, f, 0:e - a], k_hi[:, s, a:e].bitcast(F32),
                                        ALU.subtract).then_inc(k_lo_made, 1)
            for n in range(KA * n_kp):
                if n // n_kp >= 2:
                    pool.wait_ge(ks_in[n // n_kp - 2], 16 * 3 * HG)
                split(n % n_kp, n, n // n_kp % 2, nc_k + n + 1)

            def unit(st, w):
                if skip(st, w, KA):
                    return
                pool.wait_ge(ks_in[(w + KA - 2) % 4], (st.i * 2 + (w + KA - 2) // 4 + 1) * 16 * 3 * HG)
                for _, kind, j, n in projections(st, w):
                    if kind == "k":
                        split(j, (st.unit(w) + KA) * n_kp + j, (w + KA) % 2, st.i * BI * pj_batch + pj_pro + n + 1)
            iterate(pool, unit)

        @block.scalar
        def _(act):
            def read_k(j, n, bank, s, g, piece):
                a, e = k_cuts[j]
                act.wait_ge(pj_made, n + 1)
                if not early(piece, 2):
                    act.wait_ge(k_lo_made, piece - 1)
                nc.scalar.activation(k_f[:, j if n_kp == 2 else s, 0:e - a], ps_j[:, bank, 0:e - a], ACT.Identity,
                                     bias=bk_sb[:, g:g + 1]).then_inc(pj_read, 1)

            def read_v(j, n, bank, s):
                act.wait_ge(pj_made, n + 1)
                nc.scalar.copy(v[0:ck, s, j, :, 0:DH], ps_j[0:ck, bank, :].rearrange("p (h d) -> p h d", d=DH)
                               ).then_inc(pj_read, 1)

            act.wait_ge(w_in, 48)
            for j in range(nc_k):
                read_v(j, j, j % 2, 0)
            for m in range(KA * n_kp):
                read_k(m % n_kp, nc_k + m, (nc_k + m) % 2, m // n_kp % 2, m // n_kp, m)

            def exponentials(hh, s):
                if not early(hh, 2):
                    act.wait_ge(pv_made, hh - 1)
                for x, (bank, banks, cols) in enumerate(s_pieces):
                    act.wait_ge(st_made, hh * n_exp + x + 1)
                    bank = s if causal else bank
                    off = x * 4 * SQ
                    nc.scalar.activation(
                        probs[0:ck, s, off:off + banks * cols].rearrange("p (b n) -> p b n", b=banks),
                        ps_s[0:ck, bank:bank + banks, 0:cols], ACT.Exp, scale=SC).then_inc(exp_made, 1)

            def copy_output(u):
                act.wait_ge(pv_made, (u + 1) * HG)
                for q in range(2):
                    nc.scalar.copy(o_t[64 * q:64 * q + DH + 1], ps_o[64 * q:64 * q + DH + 1, 0:HG * QH]
                                   ).then_inc(o_t_made, 1)

            exponentials(0, 0)

            def unit(st, w):
                u = st.unit(w)
                if not early(u, 1):
                    copy_output(u - 1)
                for slot in range(HG):
                    if not (skip(st, w, 1) and slot == 3):
                        exponentials(u * HG + slot + 1, (slot + 1) % 2)
                    for at, kind, j, n in projections(st, w):
                        if at != slot:
                            continue
                        number = st.i * BI * pj_batch + pj_pro + n
                        if kind == "k":
                            read_k(j, number, (pj_pro + n) % 2, (w + KA) % 2, (w + KA) % 4, (u + KA) * n_kp + j)
                        else:
                            read_v(j, number, (pj_pro + n) % 2, (w // 4 + 1) % 2)
            iterate(act, unit)
            copy_output(NI * 8 - 1)

        @block.vector
        def _(dve):
            def maxima_of(u, s, heads):
                for j in heads:
                    for x, (q, a, e) in enumerate(m_cuts):
                        r = j * len(m_cuts) + x
                        dve.wait_ge(ring_made, u * n_ring + r + 1)
                        nc.vector.tensor_reduce(maxima[0:QH, s, j, x:x + 1], ps_m[0:QH, r % 2, 0:e - a],
                                                axis=AX.X, op=ALU.max, negate=True).then_inc(ring_read, 1)

            def columns_of(u, s):
                dve.wait_ge(ring_read, u * n_ring + n_ring - 2)
                for q in range(2):
                    mine = [x for x, m in enumerate(m_cuts) if m[0] == q]
                    dst = m_col[0:QH, s, q, 3 * DH:3 * DH + HG]
                    if len(mine) == 2:
                        nc.vector.tensor_tensor(dst, maxima[0:QH, s, :, mine[0]], maxima[0:QH, s, :, mine[1]], ALU.min
                                                ).then_inc(col_made, 1)
                    else:
                        nc.vector.tensor_copy(dst, maxima[0:QH, s, :, mine[0]]).then_inc(col_made, 1)

            def rows_of(u, s4):
                for q in range(2):
                    dve.wait_ge(ring_made, u * n_ring + n_ring - 1 + q)
                    nc.vector.tensor_copy(
                        qs[3 * DH:3 * DH + HG, s4, :, q * QH:(q + 1) * QH],
                        ps_m[3 * DH:3 * DH + HG, q, None, 0:QH].broadcast_to([HG, HG, QH])).then_inc(ring_read, 1)

            def output(u, g, s, n_b):
                dve.wait_ge(turned, u + 1)
                if g == 0 and not early(n_b, 1):
                    dve.wait_ge(o_out[s], n_b * 16)
                turned_o = ps_o[0:QH, 0:HG * OC].rearrange("p (j x) -> p j x", x=OC)
                for q in range(2):
                    nc.vector.reciprocal(recip[0:QH, g % 2, q], turned_o[:, :, 64 * q + DH]).then_inc(recip_made, 1)
                dve.wait_ge(recip_made, 2 * u + 2)
                for q in range(2):
                    nc.vector.tensor_tensor(
                        o_sb[0:QH, s, q, g * P:(g + 1) * P].rearrange("p (j d) -> p j d", d=DH),
                        turned_o[:, :, 64 * q:64 * q + DH],
                        recip[0:QH, g % 2, q, :, None].broadcast_to([QH, HG, DH]), ALU.mult).then_inc(o_made, 1)

            maxima_of(0, 0, range(HG))
            columns_of(0, 0)
            rows_of(0, 0)

            def unit(st, w):
                u = st.unit(w)
                if not skip(st, w, 1):
                    maxima_of(u + 1, (w + 1) % 2, range(1))
                if not early(u, 1):
                    if w:
                        output(u - 1, (w - 1) % 4, (w - 1) // 4, st.i)
                    else:
                        output(u - 1, 3, 1, st.i - 1)
                if not skip(st, w, 1):
                    maxima_of(u + 1, (w + 1) % 2, range(1, HG))
                    columns_of(u + 1, (w + 1) % 2)
                    rows_of(u + 1, (w + 1) % 4)
            iterate(dve, unit)
            output(NI * 8 - 1, 3, 1, NI - 1)

        @block.tensor
        def _(pe):
            def project(kind, j, n, bank, s_k, s_v, g):
                if not early(n, 2):
                    pe.wait_ge(pj_read, n - 1)
                for k in range(KC):
                    if kind == "k":
                        a, e = k_cuts[j]
                        last = nc.tensor.matmul(ps_j[:, bank, 0:e - a], wk[:, k, g * P:(g + 1) * P],
                                                ct[:, s_k, k, a:e], start=k == 0, stop=k == KC - 1)
                    else:
                        last = nc.tensor.matmul(ps_j[0:ck, bank, :], ct[:, s_v, k, j * ck:(j + 1) * ck],
                                                wv[:, k], start=k == 0, stop=k == KC - 1)
                    if k == KC - 1:
                        last.then_inc(pj_made, 1)
                    yield

            def maxima_of(u, s4, heads):
                for j in heads:
                    for x, (q, a, e) in enumerate(m_cuts):
                        r = j * len(m_cuts) + x
                        if not (early(u, 1) and r < 2):
                            pe.wait_ge(ring_read, u * n_ring + r - 1)
                        last = nc.tensor.matmul(ps_m[0:QH, r % 2, 0:e - a],
                                                qs[0:3 * DH, s4, j, q * QH:(q + 1) * QH],
                                                ks[0:3 * DH, s4, j, a:e], start=True, stop=not causal)
                        if causal:
                            last = nc.tensor.matmul(ps_m[0:QH, r % 2, e - a - QH:e - a], ident_b[0:QH, 0:QH],
                                                    mask_qk[0:QH], start=False, stop=True)
                        last.then_inc(ring_made, 1)
                        yield

            def turn_maxima(u, s):
                for q in range(2):
                    pe.wait_ge(col_made, u * 2 + q + 1)
                    pe.wait_ge(ring_read, u * n_ring + n_ring - 3 + q)
                    nc.tensor.matmul(ps_m[0:3 * DH + HG, q, 0:QH], m_col[0:QH, s, q, 0:3 * DH + HG], ident[0:QH, 0:QH],
                                     start=True, stop=True).then_inc(ring_made, 1)

            def scores(u, s4, j):
                hh = u * HG + j
                if j == 0:
                    pe.wait_ge(ring_read, (u + 1) * n_ring)
                for x, (bank0, banks, cols) in enumerate(s_pieces):
                    if causal:
                        if not early(hh, 2):
                            pe.wait_ge(exp_made, hh - 1)
                    elif not early(hh, 1):
                        pe.wait_ge(exp_made, hh * n_exp - n_exp + x + 1)
                    mine = [y for y in s_cuts if causal or bank0 <= y[2] < bank0 + banks]
                    for y, (k, q0, bank, col, _) in enumerate(mine):
                        bank = j % 2 if causal else bank
                        dst = ps_s[0:ck, bank, col:col + SQ - q0]
                        last = nc.tensor.matmul(dst, ks[0:3 * DH + HG, s4, j, k * ck:(k + 1) * ck],
                                                qs[0:3 * DH + HG, s4, j, q0:SQ], start=True, stop=not causal)
                        if causal:
                            last = nc.tensor.matmul(ps_s[0:ck, bank, col:col + QH], ident_b[0:ck, 0:ck],
                                                    mask_kq[0:ck], start=False, stop=True)
                    last.then_inc(st_made, 1)

            def weigh(u, j, s_v, g, v_read):
                hh = u * HG + j
                if j == 0 and not early(u, 1):
                    pe.wait_ge(o_made, 2 * u)
                if j == 0 and g == 0:
                    pe.wait_ge(pj_read, v_read)
                pe.wait_ge(exp_made, (hh + 1) * n_exp)
                halves = [[y for y in s_cuts if q * QH >= y[1]] for q in range(2)]
                for y in range(len(s_cuts)):
                    for q, mine in enumerate(halves):
                        if y < len(mine):
                            k, q0, _, _, col = mine[y]
                            p0 = col + q * QH - q0
                            last = nc.tensor.matmul(ps_o[64 * q:64 * q + DH + 1, j * QH:(j + 1) * QH],
                                                    v[0:ck, s_v, k, g * HG + j], probs[0:ck, j % 2, p0:p0 + QH],
                                                    start=y == 0, stop=y == len(mine) - 1)
                last.then_inc(pv_made, 1)

            def turn_output(u):
                yield
                pe.wait_ge(o_t_made, 2 * u + 2)
                rows = 64 + DH + 1
                for j in range(HG):
                    last = nc.tensor.transpose(ps_o[0:QH, j * OC:j * OC + rows], o_t[0:rows, j * QH:(j + 1) * QH],
                                               ident[0:rows, 0:rows])
                last.then_inc(turned, 1)
                yield

            pe.wait_ge(w_in, 48)
            pe.wait_ge(ones_in, 64)
            pe.wait_ge(ct_in[0], 16)
            for n, (kind, j, g) in enumerate([("v", j, 0) for j in range(nc_k)]
                                             + [("k", j, u) for u in range(KA) for j in range(n_kp)]):
                for _ in project(kind, j, n, n % 2, 0, 0, g):
                    pass
            pe.wait_ge(qs_in[0], 48)
            pe.wait_ge(ks_in[0], 16 * 3 * HG)
            for _ in maxima_of(0, 0, range(HG)):
                pass
            turn_maxima(0, 0)
            scores(0, 0, 0)

            def unit(st, w):
                u = st.unit(w)
                for slot in range(HG):
                    if not (skip(st, w, 1) and slot == 3):
                        uu, ww, jj = (u, w, slot + 1) if slot < 3 else (u + 1, w + 1, 0)
                        scores(uu, ww % 4, jj)
                    works = []
                    for at, kind, j, n in projections(st, w):
                        if at != slot:
                            continue
                        batch = (w + KA) // 4 if kind == "k" else w // 4 + 1
                        s_b = batch % 2
                        pe.wait_ge(ct_in[s_b], (st.i + batch // 2) * 16 + 16)
                        works.append(project(kind, j, st.i * BI * pj_batch + pj_pro + n, (pj_pro + n) % 2, s_b, s_b,
                                             (w + KA) % 4))
                    if slot < 2 and not skip(st, w, 1):
                        if slot == 0:
                            pe.wait_ge(qs_in[(w + 1) % 4], (st.i * 2 + (w + 1) // 4 + 1) * 48)
                            pe.wait_ge(ks_in[(w + 1) % 4], (st.i * 2 + (w + 1) // 4 + 1) * 16 * 3 * HG)
                        works.append(maxima_of(u + 1, (w + 1) % 4, range(2 * slot, 2 * slot + 2)))
                    if slot == 2 and not skip(st, w, 1):
                        turn_maxima(u + 1, (w + 1) % 2)
                    if slot == 0 and not early(u, 1):
                        works.append(turn_output(u - 1))
                    take_turns(works)
                    weigh(u, slot, w // 4, w % 4, st.i * BI * pj_batch + pj_pro + w // 4 * pj_batch)

            def take_turns(works):
                works = list(works)
                while works:
                    for x in list(works):
                        for _ in range(2 if x.__name__ == "maxima_of" else 1):
                            if next(x, "end") == "end":
                                works.remove(x)
                                break
            iterate(pe, unit)
            take_turns([turn_output(NI * 8 - 1)])


def hold(eng, sem, value, held):
    eng.wait_ge(sem, value)
    eng.sem_inc(held, 1)


class Link:

    def __init__(self, eng, sem, per):
        self.eng, self.sem, self.per, self.base, self.k = eng, sem, per, 0, 0

    def start(self, t):
        assert self.k in (0, self.per), self.k
        self.base, self.k = t * self.per, 0

    def __call__(self, ins, held=None):
        self.k += 1
        ins.then_inc(self.sem, 1)
        self.eng.wait_ge(self.sem, self.base + self.k)
        if held is not None:
            self.eng.sem_inc(held, 1)


def out_project(nc, tag, ident, a, bv, wo_t, bo, x, out):
    with nc.cleanup_on_exit(), ExitStack() as c:
        def sb(name, shape, dt=F32):
            return c.enter_context(nc.sbuf_tensor(f"{tag}_{name}", shape, dt))

        def sem(name):
            return nc.alloc_semaphore(f"{tag}_{name}")

        w = sb("w", [P, KC, D])
        bv_sb = sb("bv", [P, KC])
        bo_sb = sb("bo", [P, D])
        ain = sb("ain", [P, 4, D])
        xin = sb("xin", [P, 4, D])
        xb = sb("xb", [P, 2, D])
        at = sb("at", [P, 2, KC, P])
        y = sb("y", [P, 2, D])
        ps_t = c.enter_context(nc.psum_tensor(f"{tag}_ps_t", [P, 2, KC, P], F32))
        ps_y = c.enter_context(nc.psum_tensor(f"{tag}_ps_y", [P, 2, D], F32))
        w_in = sem("w_in")
        a_in = [sem(f"a_in{s}") for s in range(4)]
        x_in = [sem(f"x_in{s}") for s in range(4)]
        y_out = [sem("y_out0"), sem("y_out1")]
        transposed, at_made, xb_made, ps_made, y_made = map(sem, ("transposed", "at_made", "xb_made", "ps_made", "y_made"))
        block = c.enter_context(nc.Block())

        @block.sync
        def _(sp):
            sp.dma_start(w[:], wo_t.rearrange("(c p) n -> p c n", p=P)).then_inc(w_in, 16)
            sp.dma_start(bv_sb[:], bv.rearrange("(c p) -> p c", p=P), allow_slow_non_contiguous=True).then_inc(w_in, 16)
            sp.dma_start(bo_sb[:], bo[None, :].broadcast_to([P, D])).then_inc(w_in, 16)

            def load(t, s):
                if not early(t, 4):
                    sp.wait_ge(transposed, t - 3)
                    sp.wait_ge(xb_made, t - 3)
                sp.dma_start(ain[:, s], a[bass.ds(t * P, P), :]).then_inc(a_in[s], 16)
                sp.dma_start(xin[:, s], x[bass.ds(t * P, P), :]).then_inc(x_in[s], 16)

            def store(t, s):
                sp.wait_ge(y_made, t + 1)
                sp.dma_start(out[bass.ds(t * P, P), :], y[:, s]).then_inc(y_out[s], 16)

            for s in range(4):
                load(s, s)
            with sp.Fori(0, NT // 4 - 1) as i:
                for s in range(4):
                    load(4 * i + s + 4, s)
                    store(4 * i + s, s % 2)
            for s in range(4):
                store(NT - 4 + s, s % 2)
            for s in range(2):
                sp.wait_ge(y_out[s], 16 * (NT // 2))

        @block.gpsimd
        def _(pool):
            pool.wait_ge(w_in, 48)

            def four(i, first):
                for s in range(4):
                    pool.wait_ge(x_in[s], 16 * i + 16)
                    if not (first and s < 2):
                        pool.wait_ge(y_made, 4 * i + s - 1)
                    nc.gpsimd.tensor_tensor(xb[:, s % 2], xin[:, s], bo_sb[:], ALU.add).then_inc(xb_made, 1)
            four(0, True)
            with pool.Fori(1, NT // 4) as i:
                four(i, False)

        @block.scalar
        def _(act):
            act.wait_ge(w_in, 48)

            def step(t, s):
                act.wait_ge(transposed, t + 1)
                if not early(t, 2):
                    act.wait_ge(ps_made, t - 1)
                for k in range(KC):
                    last = nc.scalar.activation(at[:, s, k], ps_t[:, s, k], ACT.Identity, bias=bv_sb[:, k:k + 1])
                last.then_inc(at_made, 1)
            over_tiles(act, step)

        @block.vector
        def _(dve):
            def pair(i, first):
                for s in range(2):
                    t = 2 * i + s
                    dve.wait_ge(ps_made, t + 1)
                    dve.wait_ge(xb_made, t + 1)
                    if not first:
                        dve.wait_ge(y_out[s], 16 * i)
                    nc.vector.tensor_tensor(y[:, s], ps_y[:, s], xb[:, s], ALU.add).then_inc(y_made, 1)
            pair(0, True)
            with dve.Fori(1, NT // 2) as i:
                pair(i, False)

        @block.tensor
        def _(pe):
            def turn(i, r):
                t, s = 4 * i + r, r % 2
                pe.wait_ge(a_in[r % 4], 16 * (i + r // 4 + 1))
                if not early(t, 2):
                    pe.wait_ge(at_made, t - 1)
                for k in range(KC):
                    last = nc.tensor.transpose(ps_t[:, s, k], ain[:, r % 4, k * P:(k + 1) * P], ident[:])
                last.then_inc(transposed, 1)

            def project(t, s):
                pe.wait_ge(at_made, t + 1)
                if not early(t, 2):
                    pe.wait_ge(y_made, t - 1)
                for k in range(KC):
                    last = nc.tensor.matmul(ps_y[:, s], at[:, s, k], w[:, k], start=k == 0, stop=k == KC - 1)
                last.then_inc(ps_made, 1)

            pe.wait_ge(w_in, 48)
            turn(0, 0)
            turn(0, 1)

            def four(i, last):
                for s in range(4):
                    project(4 * i + s, s % 2)
                    if not (last and s >= 2):
                        turn(i, s + 2)
            four(0, False)
            with pe.Fori(1, NT // 4 - 1) as i:
                four(i, False)
            four(NT // 4 - 1, True)


def quantized_ffn(nc, tag, ident, x, w8_t, w_scale, bias, out):
    FP8_MAX = 448.0
    U8 = mybir.dt.uint8
    with nc.cleanup_on_exit(), ExitStack() as c:
        def sb(name, shape, dt=F32):
            return c.enter_context(nc.sbuf_tensor(f"{tag}_{name}", shape, dt))

        def sem(name):
            return nc.alloc_semaphore(f"{tag}_{name}")

        w8 = sb("w8", [P, KC, D], U8)
        code = sb("code", [P, KC, D], I32)
        field = sb("field", [P, KC, D], I32)
        tmp = sb("tmp", [P, KC, D], F32)
        wv_ = sb("wval", [P, KC, D], F32)
        w = sb("w", [P, KC, D], BF16)
        ident_b = sb("ident_b", [P, P], BF16)
        ws = sb("ws", [P, 1])
        b_sb = sb("b", [P, D])
        xin = sb("xin", [P, 4, D])
        xb = sb("xb", [P, 4, D])
        stats = sb("stats", [P, 2, 6])
        mv = sb("mv", [P, 2, 2])
        ve = sb("ve", [P, 2, 1])
        rstd = sb("rstd", [P, 2, 1])
        power = sb("power", [P, 1])
        xn = sb("xn", [P, 2, D])
        amax = sb("amax", [P, 2, 1])
        xs = sb("xs", [P, 2, 1])
        inv = sb("inv", [P, 2, 1])
        scale = sb("scale", [P, 4, 1])
        v = sb("v", [P, 2, D])
        magic = sb("magic", [P, 2, D])
        vm = sb("vm", [P, 2, D])
        q = sb("q", [P, 2, D], BF16)
        qt = sb("qt", [P, 2, KC, P], BF16)
        y = sb("y", [P, 2, D])
        ps_t = c.enter_context(nc.psum_tensor(f"{tag}_ps_t", [P, 2, 2 * KC, P], BF16))
        ps_y = c.enter_context(nc.psum_tensor(f"{tag}_ps_y", [P, 2, D], F32))
        w_in, held, power_set, wchain = sem("w_in"), sem("held"), sem("power_set"), sem("wchain")
        x_in = [sem(f"x_in{s}") for s in range(4)]
        y_out = [sem("y_out0"), sem("y_out1")]
        a_chain, b_chain, d_chain, ve_made, rstd_made, inv_made, v_made, power_taken, magic_made = map(
            sem, ("a_chain", "b_chain", "d_chain", "ve_made", "rstd_made", "inv_made", "v_made", "power_taken",
                  "magic_made"))
        xb_made, q_made, transposed, qt_made, ps_made, y_made = map(
            sem, ("xb_made", "q_made", "transposed", "qt_made", "ps_made", "y_made"))
        block = c.enter_context(nc.Block())

        @block.sync
        def _(sp):
            sp.dma_start(w8[:], w8_t.rearrange("(c p) n -> p c n", p=P)).then_inc(w_in, 16)
            sp.dma_start(ws[:], w_scale[None, :].broadcast_to([P, 1])).then_inc(w_in, 16)
            sp.dma_start(b_sb[:], bias[None, :].broadcast_to([P, D])).then_inc(w_in, 16)

            def load(i, s, first):
                if not first:
                    sp.wait_ge(inv_made, 4 * i + s - 3)
                    sp.wait_ge(xb_made, 4 * i + s - 3)
                sp.dma_start(xin[:, s], x[bass.ds((4 * i + s) * P, P), :]).then_inc(x_in[s], 16)

            def store(i, s):
                sp.wait_ge(y_made, 4 * i + s + 1)
                sp.dma_start(out[bass.ds((4 * i + s) * P, P), :], y[:, s % 2]).then_inc(y_out[s % 2], 16)

            for s in range(4):
                load(0, s, True)
            with sp.Fori(0, NT // 4 - 1) as i:
                for s in range(4):
                    load(i + 1, s, False)
                    store(i, s)
            for s in range(4):
                store(NT // 4 - 1, s)
            for s in range(2):
                sp.wait_ge(y_out[s], 16 * (NT // 2))

        def iterate(eng, stages):
            def four(i, first, last):
                for s in range(4):
                    for k, stage in stages:
                        if first and s + k < 0 or last and s + k > 3:
                            continue
                        stage(*((i - 1, s + k + 4) if s + k < 0 else (i, s + k)))
            for n in range(-3, 0):
                for k, stage in stages:
                    if n + k >= 0:
                        stage(0, n + k)
            four(0, True, False)
            with eng.Fori(1, NT // 4 - 1) as i:
                four(i, False, False)
            four(NT // 4 - 1, False, True)
            for k, stage in stages:
                if k < 0:
                    stage(NT // 4 - 1, 4 + k)

        @block.gpsimd
        def _(pool):
            nc.gpsimd.memset(power[:], -0.5).then_inc(power_set, 1)
            nc.gpsimd.tensor_copy(ident_b[:], ident[:]).then_inc(power_set, 1)
            pool.wait_ge(power_set, 2)
            pool.wait_ge(w_in, 48)

            def rstd_of(i, r):
                t, s = 4 * i + r, r % 2
                pool.wait_ge(ve_made, t + 1)
                if not early(t, 2):
                    pool.wait_ge(inv_made, t - 1)
                nc.gpsimd.tensor_tensor(rstd[:, s], ve[:, s], power[:], ALU.pow).then_inc(rstd_made, 1)

            def add_bias(i, r):
                t, s = 4 * i + r, r % 4
                if not early(t, 4):
                    pool.wait_ge(y_made, t - 3)
                nc.gpsimd.tensor_tensor(xb[:, s], xin[:, s], b_sb[:], ALU.add).then_inc(xb_made, 1)

            def magic_of(i, r):
                t, s = 4 * i + r, r % 2
                hold(pool, power_taken, t + 1, held)
                nc.gpsimd.tensor_scalar(magic[:, s], magic[:, s], 2.0 ** -6, 1.5 * 2.0 ** 20, ALU.max, ALU.mult
                                        ).then_inc(magic_made, 1)
            iterate(pool, ((1, magic_of), (3, rstd_of), (2, add_bias)))

        @block.scalar
        def _(act):
            def copy_q(i, r):
                t, s = 4 * i + r, r % 2
                act.wait_ge(transposed, t + 1)
                if not early(t, 2):
                    act.wait_ge(ps_made, t - 1)
                nc.scalar.copy(qt[:, s], ps_t[:, s, 0:KC]).then_inc(qt_made, 1)

            def rescale(i, r):
                t, s = 4 * i + r, r % 2
                act.wait_ge(inv_made, t + 1)
                if not early(t, 2):
                    act.wait_ge(q_made, t - 1)
                nc.scalar.activation(v[:, s], xn[:, s], ACT.Copy, scale=inv[:, s]).then_inc(v_made, 1)
            iterate(act, ((0, copy_q), (2, rescale)))

        @block.vector
        def _(dve):
            dve.wait_ge(w_in, 48)
            wl = Link(dve, wchain, 12)
            wl(nc.vector.tensor_copy(code[:], w8[:]))
            wl(nc.vector.tensor_scalar(field[:], code[:], 3, 15, ALU.logical_shift_right, ALU.bitwise_and))
            wl(nc.vector.tensor_scalar(tmp[:], field[:], 0.5, 8.0, ALU.is_ge, ALU.mult))
            wl(nc.vector.tensor_scalar(field[:], field[:], 1.0, 117.0, ALU.max, ALU.add))
            wl(nc.vector.tensor_scalar(field[:], field[:], 23, None, ALU.logical_shift_left))
            wl(nc.vector.tensor_copy(wv_[:], field[:].bitcast(F32)))
            wl(nc.vector.tensor_scalar(field[:], code[:], 7, None, ALU.bitwise_and))
            wl(nc.vector.tensor_tensor(tmp[:], tmp[:], field[:], ALU.add))
            wl(nc.vector.tensor_tensor(tmp[:], tmp[:], wv_[:], ALU.mult))
            wl(nc.vector.tensor_scalar(field[:], code[:], 7, None, ALU.logical_shift_right))
            wl(nc.vector.tensor_scalar(wv_[:], field[:], -2.0, 1.0, ALU.mult, ALU.add))
            wl(nc.vector.tensor_tensor(w[:], tmp[:], wv_[:], ALU.mult))
            a_link, b_link, d_link = Link(dve, a_chain, 2), Link(dve, b_chain, 3), Link(dve, d_chain, 1)

            def statistics(i, r):
                t, s = 4 * i + r, r % 2
                a_link.start(t)
                dve.wait_ge(x_in[r % 4], 16 * (i + r // 4 + 1))
                a_link(nc.vector.bn_stats(stats[:, s], xin[:, r % 4]), held)
                a_link(nc.vector.bn_aggr(mv[:, s], stats[:, s]))
                if not early(t, 2):
                    dve.wait_ge(rstd_made, t - 1)
                nc.vector.tensor_scalar(ve[:, s], mv[:, s, 1:2], EPS, None, ALU.add).then_inc(ve_made, 1)

            def norm(i, r):
                t, s = 4 * i + r, r % 2
                b_link.start(t)
                dve.wait_ge(rstd_made, t + 1)
                if not early(t, 2):
                    dve.wait_ge(v_made, t - 1)
                b_link(nc.vector.tensor_scalar(xn[:, s], xin[:, r % 4], mv[:, s, 0:1], rstd[:, s],
                                               ALU.subtract, ALU.mult))
                b_link(nc.vector.tensor_reduce(amax[:, s], xn[:, s], axis=AX.X, op=ALU.max,
                                               apply_absolute_value=True))
                b_link(nc.vector.tensor_scalar(xs[:, s], amax[:, s], 1e-12, 1.0 / FP8_MAX, ALU.max, ALU.mult))
                if not early(t, 4):
                    dve.wait_ge(y_made, t - 3)
                nc.vector.tensor_scalar(scale[:, r % 4], xs[:, s], ws[:], None, ALU.mult)
                nc.vector.reciprocal(inv[:, s], xs[:, s]).then_inc(inv_made, 1)

            def powers(i, r):
                t, s = 4 * i + r, r % 2
                dve.wait_ge(v_made, t + 1)
                if not early(t, 2):
                    dve.wait_ge(q_made, t - 1)
                nc.vector.tensor_scalar(magic[:, s].bitcast(I32), v[:, s].bitcast(I32), 0x7F800000, None,
                                        ALU.bitwise_and).then_inc(power_taken, 1)

            def quantize(i, r):
                t, s = 4 * i + r, r % 2
                d_link.start(t)
                dve.wait_ge(magic_made, t + 1)
                d_link(nc.vector.tensor_tensor(vm[:, s], v[:, s], magic[:, s], ALU.add))
                if not early(t, 2):
                    dve.wait_ge(transposed, t - 1)
                nc.vector.tensor_tensor(q[:, s], vm[:, s], magic[:, s], ALU.subtract).then_inc(q_made, 1)

            def finish(i, r):
                t, s = 4 * i + r, r % 2
                dve.wait_ge(ps_made, t + 1)
                dve.wait_ge(xb_made, t + 1)
                if not early(t, 2):
                    dve.wait_ge(y_out[s], 8 * (t - s))
                nc.vector.scalar_tensor_tensor(y[:, s], ps_y[:, s], scale[:, r % 4], xb[:, r % 4], ALU.mult, ALU.add
                                               ).then_inc(y_made, 1)

            iterate(dve, ((0, quantize), (1, powers), (2, norm), (3, statistics), (-1, finish)))

        @block.tensor
        def _(pe):
            pe.wait_ge(power_set, 2)
            pe.wait_ge(wchain, 12)

            def step(i, s, first):
                t = 2 * i + s
                pe.wait_ge(q_made, t + 1)
                if not first:
                    pe.wait_ge(qt_made, t - 1)
                for k in range(KC):
                    last = nc.tensor.transpose(ps_t[:, s, k], q[:, s, k * P:(k + 1) * P], ident_b[:])
                last.then_inc(transposed, 1)
                pe.wait_ge(qt_made, t + 1)
                if not first:
                    pe.wait_ge(y_made, t - 1)
                for k in range(KC):
                    last = nc.tensor.matmul(ps_y[:, s], qt[:, s, k], w[:, k], start=k == 0, stop=k == KC - 1)
                last.then_inc(ps_made, 1)
            for s in range(2):
                step(0, s, True)
            with pe.Fori(1, NT // 2) as i:
                for s in range(2):
                    step(i, s, False)


E_, I_, KTOP = 128, 128, 8
NG, GE, TG = 8, 16, 4
NS = 2
TILES = N * KTOP // P + E_
BIG = 3.0e38


class RouteState:

    def __init__(self, nc, c):
        def sb(name, shape, dt=F32):
            return c.enter_context(nc.sbuf_tensor(f"r_{name}", shape, dt))
        self.mask = sb("mask", [P, NT, E_], BF16)
        self.cand = sb("cand", [P, NT, E_])
        self.top = sb("top", [P, NT, 8])
        self.rank = sb("rank", [P, NT, E_])
        self.before = sb("before", [P, NT + 1, E_], BF16)
        self.first = sb("first", [P, E_])
        self.eid = sb("eid", [1, TILES], I32)
        self.lofs = sb("lofs", [1, TILES], I32)
        self.ends = sb("ends", [1, E_], I32)


def route(nc, tag, ident, st, x, wg_t, ws_gu, ws_d, xf, base, lists):
    with nc.cleanup_on_exit(), ExitStack() as c:
        def sb(name, shape, dt=F32):
            return c.enter_context(nc.sbuf_tensor(f"{tag}_{name}", shape, dt))

        def sem(name):
            return nc.alloc_semaphore(f"{tag}_{name}")

        def ps(name, shape):
            return c.enter_context(nc.psum_tensor(f"{tag}_{name}", shape, F32))

        wg = sb("wg", [P, KC, E_])
        wgu = sb("wgu", [P, NS, KC, 2 * I_])
        wd = sb("wd", [P, NS, D])
        xin = sb("xin", [P, 2, D])
        xres = sb("xres", [P, 2, D])
        token_i = sb("token_i", [P, 2, 1], I32)
        stats = sb("stats", [P, 2, 6])
        mv = sb("mv", [P, 2, 2])
        ve = sb("ve", [P, 2, 1])
        rstd = sb("rstd", [P, 2, 1])
        power = sb("power", [P, 1])
        xn = sb("xn", [P, 2, D])
        xnt = sb("xnt", [P, 2, KC, P])
        silu = sb("silu", [P, 2, NS, P])
        hid = sb("hid", [P, 2, NS, P])
        lg = sb("lg", [P, 2, NG, GE + TG])
        top_g = sb("top_g", [P, NG, 8])
        take_g = sb("take_g", [P, NG, 8])
        rep_g = sb("rep_g", [P, NG, GE + TG])
        rep = sb("rep", [P, E_])
        cand = sb("cand", [P, E_])
        top = sb("top", [P, 8])
        slot = sb("slot", [P, 2, E_])
        ebase = sb("ebase", [P, E_])
        top_s = sb("top_s", [P, 8])
        slot_i = sb("slot_i", [P, 2, 8], I32)
        token = sb("token", [P, NT], I32)
        zeros = sb("zeros", [P, SQ * B], I32)
        tri = sb("tri", [P, P], BF16)
        ones = sb("ones", [P, P], BF16)
        y = sb("y", [P, 2, D])
        ps_t = ps("ps_t", [P, 2, KC, P])
        ps_l = ps("ps_l", [P, 512])
        ps_r = ps("ps_r", [P, 512])
        ps_g = ps("ps_g", [P, 2, 2 * NS, P])
        ps_y = ps("ps_y", [P, 2, D])
        w_in, const_made, held = sem("w_in"), sem("const_made"), sem("held")
        x_in = [sem("x_in0"), sem("x_in1")]
        xr_in = [sem("xr_in0"), sem("xr_in1")]
        xf_out = [sem("xf_out0"), sem("xf_out1")]
        y_out = [sem("y_out0"), sem("y_out1")]
        zero_out, list_out = sem("zero_out"), [sem("list_out0"), sem("list_out1")]
        chain, ve_made, rstd_made, normed, transposed, xnt_made = map(
            sem, ("chain", "ve_made", "rstd_made", "normed", "transposed", "xnt_made"))
        logits_made, lg_made, mask_made, before_made, rank_made, rank_read = map(
            sem, ("logits_made", "lg_made", "mask_made", "before_made", "rank_made", "rank_read"))
        gu_made, silu_made, hid_made, y_ps_made, y_made, slot_made, rchain, pchain, token_made = map(
            sem, ("gu_made", "silu_made", "hid_made", "y_ps_made", "y_made", "slot_made", "rchain", "pchain", "token_made"))
        block = c.enter_context(nc.Block())
        lists_rows = lists[:, :].rearrange("(e n) o -> e (n o)", n=N)

        @block.sync
        def _(sp):
            sp.dma_start(wg[:], wg_t.rearrange("(c p) n -> p c n", p=P)).then_inc(w_in, 16)
            for m in range(NS):
                sp.dma_start(wgu[:, m], ws_gu[m].rearrange("(c p) n -> p c n", p=P)).then_inc(w_in, 16)
                sp.dma_start(wd[:, m], ws_d[m]).then_inc(w_in, 16)
            sp.wait_ge(const_made, 1)
            sp.dma_start(lists_rows, zeros[:]).then_inc(zero_out, 16)

            def load_x(i, s, first):
                if not first:
                    sp.wait_ge(normed, 2 * i + s - 1)
                sp.dma_start(xin[:, s], x[bass.ds((2 * i + s) * P, P), :]).then_inc(x_in[s], 16)

            def load_xres(i, s, first):
                if not first:
                    sp.wait_ge(y_made, 2 * i + s - 1)
                sp.dma_start(xres[:, s], x[bass.ds((2 * i + s) * P, P), :]).then_inc(xr_in[s], 16)

            def store_xf(i, s):
                sp.wait_ge(normed, 2 * i + s + 1)
                sp.dma_start(xf[bass.ds((2 * i + s) * P, P), :], xn[:, s]).then_inc(xf_out[s], 16)

            def store_y(i, s):
                sp.wait_ge(y_made, 2 * i + s + 1)
                sp.dma_start(base[bass.ds((2 * i + s) * P, P), :], y[:, s]).then_inc(y_out[s], 16)

            for s in range(2):
                load_x(0, s, True)
                load_xres(0, s, True)
            for s in range(2):
                store_xf(0, s)
                load_x(1, s, False)

            def both(i, last):
                for s in range(2):
                    store_xf(i + 1, s)
                    if not last:
                        load_x(i + 2, s, False)
                    store_y(i, s)
                    load_xres(i + 1, s, False)
            with sp.Fori(0, NT // 2 - 2) as i:
                both(i, False)
            both(NT // 2 - 2, True)
            for s in range(2):
                store_y(NT // 2 - 1, s)
            for s in range(2):
                sp.wait_ge(y_out[s], 16 * (NT // 2))
                sp.wait_ge(xf_out[s], 16 * (NT // 2))

        @block.gpsimd
        def _(pool):
            nc.gpsimd.memset(zeros[:], 0).then_inc(const_made, 1)
            nc.gpsimd.memset(power[:], -0.5).then_inc(const_made, 1)
            nc.gpsimd.memset(ones[:], 1.0).then_inc(const_made, 1)
            nc.gpsimd.memset(tri[:], 1.0).then_inc(const_made, 1)
            nc.gpsimd.memset(lg[:], BIG).then_inc(const_made, 1)
            nc.gpsimd.memset(take_g[:], BIG).then_inc(const_made, 1)
            nc.gpsimd.memset(st.before[:, 0], 0.0).then_inc(const_made, 1)
            nc.gpsimd.iota(ebase[:], pattern=[[N, E_]], base=1, channel_multiplier=0,
                           allow_small_or_imprecise_dtypes=True).then_inc(const_made, 1)
            nc.gpsimd.iota(token[:], pattern=[[P, NT]], base=0, channel_multiplier=1).then_inc(const_made, 1)
            pool.wait_ge(const_made, 9)
            nc.gpsimd.affine_select(out=tri[:], in_=tri[:], compare_op=ALU.is_ge, fill=0.0, base=-1,
                                    pattern=[[1, P]], channel_multiplier=-1).then_inc(const_made, 1)
            pool.wait_ge(const_made, 10)

            def rstd_of(i, s, first):
                t = 2 * i + s
                pool.wait_ge(ve_made, t + 1)
                if not first:
                    pool.wait_ge(normed, t - 1)
                nc.gpsimd.tensor_tensor(rstd[:, s], ve[:, s], power[:], ALU.pow).then_inc(rstd_made, 1)

            def scatter(i, s):
                t = 2 * i + s
                if not (isinstance(t, int) and t < 2):
                    pool.wait_ge(list_out[s], 16 * KTOP * i)
                nc.gpsimd.tensor_copy(token_i[:, s], token[:, bass.ds(t, 1)]).then_inc(token_made, 1)
                pool.wait_ge(token_made, t + 1)
                hold(pool, slot_made, t + 1, held)
                for k in range(KTOP):
                    nc.gpsimd.indirect_dma_start(
                        lists[:, :], bass.IndirectOffsetOnAxis(ap=slot_i[:, s, k:k + 1], axis=0),
                        token_i[:, s], None).then_inc(list_out[s], 16)

            rstd_of(0, 0, True)
            rstd_of(0, 1, True)
            pool.wait_ge(zero_out, 16)
            rstd_of(1, 0, False)
            rstd_of(1, 1, False)
            scatter(0, 0)

            def both(i):
                rstd_of(i + 1, 0, False)
                scatter(i - 1, 1)
                rstd_of(i + 1, 1, False)
                scatter(i, 0)
            both(1)
            with pool.Fori(2, NT // 2 - 1) as i:
                both(i)
            scatter(NT // 2 - 2, 1)
            scatter(NT // 2 - 1, 0)
            scatter(NT // 2 - 1, 1)
            for s in range(2):
                pool.wait_ge(list_out[s], 16 * KTOP * (NT // 2))
            pool.wait_ge(before_made, NT)

        @block.scalar
        def _(act):
            act.wait_ge(const_made, 10)

            def turned(i, s, first):
                t = 2 * i + s
                act.wait_ge(transposed, t + 1)
                if not first:
                    act.wait_ge(gu_made, t - 1)
                nc.scalar.copy(xnt[:, s], ps_t[:, s]).then_inc(xnt_made, 1)

            def logits(i, s, first):
                t = 2 * i + s
                act.wait_ge(logits_made, t + 1)
                if not first:
                    act.wait_ge(mask_made, t - 1)
                nc.scalar.copy(lg[:, s, :, 0:GE], ps_l[:, 0:E_].rearrange("p (g e) -> p g e", g=NG)
                               ).then_inc(lg_made, 1)

            def gate(i, s, first):
                t = 2 * i + s
                act.wait_ge(gu_made, t + 1)
                if not first:
                    act.wait_ge(hid_made, t - 1)
                nc.scalar.activation(silu[:, s], ps_g[:, s, 0:NS], ACT.Silu).then_inc(silu_made, 1)

            def ranks(i, s):
                t = 2 * i + s
                act.wait_ge(rank_made, t + 1)
                nc.scalar.copy(st.rank[:, bass.ds(t, 1)], ps_r[:, None, 0:E_]).then_inc(rank_read, 1)

            turned(0, 0, True)
            logits(0, 0, True)
            gate(0, 0, True)
            turned(0, 1, True)
            logits(0, 1, True)
            gate(0, 1, True)
            ranks(0, 0)
            with act.Fori(1, NT // 2) as i:
                turned(i, 0, False)
                logits(i, 0, False)
                gate(i, 0, False)
                ranks(i - 1, 1)
                turned(i, 1, False)
                logits(i, 1, False)
                gate(i, 1, False)
                ranks(i, 0)
            ranks(NT // 2 - 1, 1)
            act.wait_ge(rank_read, NT)

        @block.vector
        def _(dve):
            dve.wait_ge(const_made, 10)
            nl = Link(dve, chain, 2)
            rl = Link(dve, rchain, 10)
            pl = Link(dve, pchain, 3)

            def statistics(i, s):
                t = 2 * i + s
                nl.start(t)
                dve.wait_ge(x_in[s], 16 * i + 16)
                nl(nc.vector.bn_stats(stats[:, s], xin[:, s]), held)
                nl(nc.vector.bn_aggr(mv[:, s], stats[:, s]))
                nc.vector.tensor_scalar(ve[:, s], mv[:, s, 1:2], EPS, None, ALU.add).then_inc(ve_made, 1)

            def norm(i, s, first):
                t = 2 * i + s
                dve.wait_ge(rstd_made, t + 1)
                if not first:
                    dve.wait_ge(transposed, t - 1)
                    dve.wait_ge(xf_out[s], 16 * i)
                nc.vector.tensor_scalar(xn[:, s], xin[:, s], mv[:, s, 0:1], rstd[:, s], ALU.subtract, ALU.mult
                                        ).then_inc(normed, 1)

            def hidden(i, s, first):
                t = 2 * i + s
                dve.wait_ge(silu_made, t + 1)
                if not first:
                    dve.wait_ge(y_ps_made, t - 1)
                nc.vector.tensor_tensor(hid[:, s], silu[:, s], ps_g[:, s, NS:2 * NS], ALU.mult).then_inc(hid_made, 1)

            def choose(i, s, first):
                t = 2 * i + s
                rl.start(t)
                hold(dve, lg_made, t + 1, held)
                for g in range(NG):
                    last = nc.vector.max(top_g[:, g], lg[:, s, g, 0:GE])
                rl(last)
                rl(nc.vector.tensor_copy(take_g[:, :, 0:TG], top_g[:, :, 0:TG]), held)
                for g in range(NG):
                    last = nc.vector.match_replace(rep_g[:, g], take_g[:, g], lg[:, s, g], -BIG)
                rl(last)
                rl(nc.vector.tensor_scalar(rep_g[:, :, 0:GE], rep_g[:, :, 0:GE], -BIG, 1.0, ALU.is_equal, ALU.subtract))
                rl(nc.vector.scalar_tensor_tensor(cand[:].rearrange("p (g e) -> p g e", g=NG), rep_g[:, :, 0:GE],
                                                  1.0e30, lg[:, s, :, 0:GE], ALU.mult, ALU.add), held)
                rl(nc.vector.max(top[:], cand[:]), held)
                rl(nc.vector.match_replace(rep[:], top[:], cand[:], -BIG))
                nc.vector.tensor_scalar(st.mask[:, bass.ds(t, 1)], rep[:, None, :], -BIG, None, ALU.is_equal
                                        ).then_inc(mask_made, 1)
                rl(nc.vector.tensor_copy(st.top[:, bass.ds(t, 1)], top[:, None, :]))
                dve.wait_ge(mask_made, t + 1)
                if not (isinstance(i, int) and t == 0):
                    dve.wait_ge(before_made, t)
                nc.vector.tensor_tensor(st.before[:, bass.ds(t + 1, 1)], st.before[:, bass.ds(t, 1)],
                                        st.mask[:, bass.ds(t, 1)], ALU.add).then_inc(before_made, 1)
                rl(nc.vector.tensor_scalar(rep[:], rep[:], -BIG, 1.0, ALU.is_equal, ALU.subtract))
                rl(nc.vector.scalar_tensor_tensor(st.cand[:, bass.ds(t, 1)], rep[:, None, :], 1.0e30, cand[:, None, :],
                                                  ALU.mult, ALU.add))

            def place(i, s, first):
                t = 2 * i + s
                pl.start(t)
                dve.wait_ge(rank_read, t + 1)
                pl(nc.vector.tensor_tensor(slot[:, s, None, :], st.rank[:, bass.ds(t, 1)], ebase[:, None, :], ALU.add))
                pl(nc.vector.tensor_tensor(slot[:, s, None, :], slot[:, s, None, :], st.mask[:, bass.ds(t, 1)], ALU.mult),
                   held)
                pl(nc.vector.max(top_s[:], slot[:, s]))
                if not first:
                    dve.wait_ge(list_out[s], 16 * KTOP * i)
                nc.vector.tensor_scalar(slot_i[:, s], top_s[:], -1.0, None, ALU.add).then_inc(slot_made, 1)

            def finish(i, s, first):
                t = 2 * i + s
                dve.wait_ge(y_ps_made, t + 1)
                dve.wait_ge(xr_in[s], 16 * i + 16)
                if not first:
                    dve.wait_ge(y_out[s], 16 * i)
                nc.vector.scalar_tensor_tensor(y[:, s], ps_y[:, s], 1.0 / NS, xres[:, s], ALU.mult, ALU.add
                                               ).then_inc(y_made, 1)

            for s in range(2):
                statistics(0, s)
                norm(0, s, True)

            def tile(i, s, first, last, before):
                if not last:
                    statistics(i + 1, s)
                choose(i, s, first)
                hidden(i, s, first)
                if before:
                    place(*before)
                    finish(*before)
                if not last:
                    norm(i + 1, s, False)

            tile(0, 0, True, False, None)
            tile(0, 1, True, False, (0, 0, True))
            tile(1, 0, False, False, (0, 1, True))
            tile(1, 1, False, False, (1, 0, False))
            with dve.Fori(2, NT // 2 - 1) as i:
                tile(i, 0, False, False, (i - 1, 1, False))
                tile(i, 1, False, False, (i, 0, False))
            last = NT // 2 - 1
            tile(last, 0, False, True, (last - 1, 1, False))
            tile(last, 1, False, True, (last, 0, False))
            place(last, 1, False)
            finish(last, 1, False)

        @block.tensor
        def _(pe):
            def turn(i, s, first):
                t = 2 * i + s
                pe.wait_ge(normed, t + 1)
                if not first:
                    pe.wait_ge(xnt_made, t - 1)
                for k in range(KC):
                    last = nc.tensor.transpose(ps_t[:, s, k], xn[:, s, k * P:(k + 1) * P], ident[:])
                last.then_inc(transposed, 1)

            def products(i, s, first):
                t = 2 * i + s
                pe.wait_ge(xnt_made, t + 1)
                if not (first and s == 0):
                    pe.wait_ge(lg_made, t)
                for k in range(KC):
                    last = nc.tensor.matmul(ps_l[:, 0:E_], xnt[:, s, k], wg[:, k], start=k == 0, stop=k == KC - 1)
                last.then_inc(logits_made, 1)
                if not first:
                    pe.wait_ge(hid_made, t - 1)
                for half in range(2):
                    for m in range(NS):
                        for k in range(KC):
                            last = nc.tensor.matmul(ps_g[:, s, half * NS + m], wgu[:, m, k, half * I_:(half + 1) * I_],
                                                    xnt[:, s, k], start=k == 0, stop=k == KC - 1)
                last.then_inc(gu_made, 1)

            def down(i, s, first):
                t = 2 * i + s
                pe.wait_ge(hid_made, t + 1)
                if not first:
                    pe.wait_ge(y_made, t - 1)
                for m in range(NS):
                    last = nc.tensor.matmul(ps_y[:, s], hid[:, s, m], wd[:, m], start=m == 0, stop=m == NS - 1)
                last.then_inc(y_ps_made, 1)

            def count(i, s, first):
                t = 2 * i + s
                pe.wait_ge(mask_made, t + 1)
                if not (first and s == 0):
                    pe.wait_ge(rank_read, t)
                    pe.wait_ge(before_made, t)
                nc.tensor.matmul(ps_r[:, 0:E_], tri[:], st.mask[:, bass.ds(t, 1)].rearrange("p o e -> p (o e)"),
                                 start=True, stop=False)
                nc.tensor.matmul(ps_r[:, 0:E_], ones[:], st.before[:, bass.ds(t, 1)].rearrange("p o e -> p (o e)"),
                                 start=False, stop=True).then_inc(rank_made, 1)

            pe.wait_ge(const_made, 10)
            pe.wait_ge(w_in, 16 * (1 + 2 * NS))
            turn(0, 0, True)
            products(0, 0, True)
            turn(0, 1, True)
            products(0, 1, True)
            count(0, 0, True)
            down(0, 0, True)

            def both(i):
                turn(i, 0, False)
                products(i, 0, False)
                count(i - 1, 1, False)
                down(i - 1, 1, isinstance(i, int) and i == 1)
                turn(i, 1, False)
                products(i, 1, False)
                count(i, 0, False)
                down(i, 0, False)

            both(1)
            with pe.Fori(2, NT // 2) as i:
                both(i)
            count(NT // 2 - 1, 1, False)
            down(NT // 2 - 1, 1, False)


def tables(nc, tag, ident, st):
    with nc.cleanup_on_exit(), ExitStack() as c:
        def sb(name, shape, dt=F32):
            return c.enter_context(nc.sbuf_tensor(f"{tag}_{name}", shape, dt))

        def sem(name):
            return nc.alloc_semaphore(f"{tag}_{name}")

        def ps(name, shape):
            return c.enter_context(nc.psum_tensor(f"{tag}_{name}", shape, F32))

        onesb = sb("onesb", [P, P], BF16)
        cnt = sb("cnt", [P, E_])
        ntile = sb("ntile", [P, E_])
        zero = sb("zero", [P, E_])
        ends = sb("ends", [P, E_])
        cols = sb("cols", [P, 2, P])
        number = sb("number", [P, TILES])
        past = sb("past", [P, TILES])
        sums_w = sb("sums_w", [P, 2])
        row = sb("row", [1, TILES])
        row2 = sb("row2", [1, TILES])
        ps_c = ps("ps_c", [P, 512])
        ps_t = ps("ps_t", [P, 2, 512])
        ps_e = ps("ps_e", [P, 2, 512])
        const_made, pe_made, link_s = map(sem, ("const_made", "pe_made", "link"))
        block = c.enter_context(nc.Block())

        @block.gpsimd
        def _(pool):
            nc.gpsimd.memset(onesb[:], 1.0).then_inc(const_made, 1)
            nc.gpsimd.memset(zero[:], 0.0).then_inc(const_made, 1)
            nc.gpsimd.memset(sums_w[:], 1.0).then_inc(const_made, 1)
            nc.gpsimd.iota(number[:], pattern=[[1, TILES]], base=0, channel_multiplier=0,
                           allow_small_or_imprecise_dtypes=True).then_inc(const_made, 1)

        @block.tensor
        def _(pe):
            pe.wait_ge(const_made, 4)
            nc.tensor.matmul(ps_c[:, 0:E_], onesb[:], st.before[:, NT], start=True, stop=True).then_inc(pe_made, 1)
            pe.wait_ge(link_s, 5)
            nc.tensor.transpose(ps_t[:, 0, 0:P], ends[:], ident[:]).then_inc(pe_made, 1)
            nc.tensor.transpose(ps_t[:, 1, 0:P], ntile[:], ident[:]).then_inc(pe_made, 1)
            pe.wait_ge(link_s, 11)
            nc.tensor.matmul(ps_e[0:1, 0, 0:TILES], sums_w[:, 0:1], past[:], start=True, stop=True).then_inc(pe_made, 1)
            nc.tensor.matmul(ps_e[0:1, 1, 0:TILES], sums_w[:, 1:2], past[:], start=True, stop=True).then_inc(pe_made, 1)

        @block.vector
        def _(dve):
            link = Link(dve, link_s, 16)
            dve.wait_ge(pe_made, 1)
            link(nc.vector.tensor_copy(cnt[:], ps_c[:, 0:E_]))
            link(nc.vector.tensor_scalar(ntile[:], cnt[:], 1.0 / P, 127.0 / P - 0.5 + 1.0 / 256, ALU.mult, ALU.add))
            link(nc.vector.tensor_scalar(ntile[:], ntile[:], 12582912.0, None, ALU.add))
            link(nc.vector.tensor_scalar(ntile[:], ntile[:], -12582912.0, 1.0, ALU.add, ALU.max))
            dve.wait_ge(const_made, 4)
            link(nc.vector.tensor_tensor_scan(ends[:], ntile[:], zero[:], 0.0, ALU.add, ALU.add))
            link(nc.vector.tensor_tensor(st.first[:], ends[:], ntile[:], ALU.subtract))
            link(nc.vector.tensor_scalar(st.first[:], st.first[:], float(P), 1.0, ALU.mult, ALU.add))
            link(nc.vector.tensor_copy(st.ends[:], ends[0:1]))
            dve.wait_ge(pe_made, 3)
            link(nc.vector.tensor_copy(cols[:], ps_t[:, :, 0:P]))
            link(nc.vector.tensor_scalar(sums_w[:, 1:2], cols[:, 1, 0:1], -float(P), float(N), ALU.mult, ALU.add))
            link(nc.vector.tensor_scalar(past[:], number[:], cols[:, 0, 0:1], None, ALU.is_ge))
            dve.wait_ge(pe_made, 5)
            link(nc.vector.tensor_scalar(row[:], ps_e[0:1, 0, 0:TILES], float(E_ - 1), None, ALU.min))
            link(nc.vector.tensor_copy(st.eid[:], row[:]))
            link(nc.vector.tensor_scalar(row2[:], number[0:1], float(P), None, ALU.mult))
            link(nc.vector.tensor_tensor(row2[:], row2[:], ps_e[0:1, 1, 0:TILES], ALU.add))
            link(nc.vector.tensor_scalar(st.lofs[:], row2[:], float(E_ * N - P), None, ALU.min))


def experts(nc, tag, ident, st, xf, w_gu, w_d, lists, yo):
    WR, GR, LR = 4, 4, 8
    UN = 16
    with nc.cleanup_on_exit(), ExitStack() as c:
        def sb(name, shape, dt=F32):
            return c.enter_context(nc.sbuf_tensor(f"{tag}_{name}", shape, dt))

        def sem(name):
            return nc.alloc_semaphore(f"{tag}_{name}")

        def ps(name, shape):
            return c.enter_context(nc.psum_tensor(f"{tag}_{name}", shape, F32))

        wgu = sb("wgu", [P, WR * KC * 2 * I_])
        wd = sb("wd", [P, WR * D])
        ids = sb("ids", [P, LR, 1], I32)
        xg = sb("xg", [P, GR, D])
        xt = sb("xt", [P, 2, KC, P])
        silu = sb("silu", [P, 2, I_])
        hid = sb("hid", [P, 2, I_])
        hid_t = sb("hid_t", [P, 2, P])
        y = sb("y", [P, 4, D])
        ps_t = ps("ps_t", [P, 2, KC, P])
        ps_g = ps("ps_g", [P, 2, 512])
        ps_h = ps("ps_h", [P, 2, 512])
        ps_y = ps("ps_y", [P, 2, D])
        held = sem("held")
        weights_ready = sem("weights_ready")
        w_in = [sem(f"w_in{s}") for s in range(WR)]
        ids_in = [sem(f"ids_in{s}") for s in range(LR)]
        xg_in = [sem(f"xg_in{s}") for s in range(GR)]
        y_out = [sem(f"y_out{s}") for s in range(4)]
        transposed, xt_made, gu_made, silu_made, hid_made, turned, hid_t_made, y_ps_made, y_made = map(
            sem, ("transposed", "xt_made", "gu_made", "silu_made", "hid_made", "turned", "hid_t_made", "y_ps_made",
                  "y_made"))
        block = c.enter_context(nc.Block())

        @block.sync
        def _(sp):
            def load(e, s):
                sp.dma_start(wgu[:, s * KC * 2 * I_:(s + 1) * KC * 2 * I_].rearrange("p (c n) -> p c n", c=KC),
                             w_gu[bass.ds(e * D, D), :].rearrange("(c p) n -> p c n", p=P)).then_inc(w_in[s], 16)
                sp.dma_start(wd[:, s * D:(s + 1) * D], w_d[bass.ds(e * I_, I_), :]).then_inc(w_in[s], 16)
            def arrived(i, s):
                sp.wait_ge(w_in[s], 32 * (i + 1))
                sp.sem_inc(weights_ready, 1)

            for s in range(WR):
                load(s, s)
            arrived(0, 0)
            arrived(0, 1)
            with sp.Fori(1, E_ // WR) as i:
                for s in range(WR):
                    arrived(*((i - 1, s + 2) if s + 2 < WR else (i, s + 2 - WR)))
                    end = sp.value_load(st.ends[0:1, bass.ds((i - 1) * WR + s, 1)], min_val=0, max_val=TILES)
                    sp.wait_ge(y_ps_made, end + 1)
                    load(i * WR + s, s)
            for s in range(2, WR):
                arrived(E_ // WR - 1, s)

        @block.gpsimd
        def _(pool):
            def gather(m, j, first):
                g = j % GR
                hold(pool, ids_in[j], 16 * m + 16, held)
                if not (first and j < GR):
                    hold(pool, transposed, 8 * m + j - GR + 1, held)
                nc.gpsimd.indirect_dma_start(xg[:, g], None, xf[:, :], bass.IndirectOffsetOnAxis(ap=ids[:, j], axis=0)
                                             ).then_inc(xg_in[g], 16)

            for s in range(LR // 2):
                at = pool.value_load(st.lofs[0:1, s:s + 1], min_val=0, max_val=E_ * N - P)
                nc.gpsimd.dma_start(ids[:, s], lists[bass.ds(at, P), :]).then_inc(ids_in[s], 16)

            def eight(m, first, last):
                for j in range(8):
                    gather(m, j, first)
                    ahead = j + LR // 2
                    if last and ahead >= 8:
                        continue
                    if not (first and ahead < 8):
                        pool.wait_ge(xg_in[ahead % GR], 16 * (2 * m + ahead // GR - 2 + 1))
                    at = pool.value_load(st.lofs[0:1, bass.ds(m * 8 + ahead, 1)], min_val=0, max_val=E_ * N - P)
                    nc.gpsimd.dma_start(ids[:, ahead % LR], lists[bass.ds(at, P), :]).then_inc(ids_in[ahead % LR], 16)
            eight(0, True, False)
            with pool.Fori(1, TILES // 8 - 1) as m:
                eight(m, False, False)
            eight(TILES // 8 - 1, False, True)

        @block.scalar
        def _(act):
            def store(i, s):
                act.wait_ge(y_made, i * 4 + s + 1)
                act.dma_start(yo[bass.ds((i * 4 + s) * P, P), :], y[:, s]).then_inc(y_out[s], 16)

            def copy_x(t, b, first):
                act.wait_ge(transposed, t + 1)
                if not first:
                    act.wait_ge(gu_made, t - 1)
                nc.scalar.copy(xt[:, b], ps_t[:, b]).then_inc(xt_made, 1)

            def gate(t, b, first):
                act.wait_ge(gu_made, t + 1)
                if not first:
                    act.wait_ge(hid_made, t - 1)
                nc.scalar.activation(silu[:, b], ps_g[:, b, 0:I_], ACT.Silu).then_inc(silu_made, 1)

            copy_x(0, 0, True)

            def four(i, first, last):
                for s in range(4):
                    t = i * 4 + s
                    gate(t, s % 2, first and s < 2)
                    if not (last and s == 3):
                        copy_x(t + 1, (s + 1) % 2, first and s < 1)
                    if not (first and s < 2):
                        store(*((i, s - 2) if s >= 2 else (i - 1, s + 2)))
            four(0, True, False)
            with act.Fori(1, TILES // 4 - 1) as i:
                four(i, False, False)
            four(TILES // 4 - 1, False, True)
            store(TILES // 4 - 1, 2)
            store(TILES // 4 - 1, 3)
            for s in range(4):
                act.wait_ge(y_out[s], 16 * (TILES // 4))

        @block.vector
        def _(dve):
            def multiply(t, b, first):
                dve.wait_ge(silu_made, t + 1)
                if not first:
                    dve.wait_ge(turned, t - 1)
                nc.vector.tensor_tensor(hid[:, b], silu[:, b], ps_g[:, b, I_:2 * I_], ALU.mult).then_inc(hid_made, 1)

            def copy_h(t, b, first):
                dve.wait_ge(turned, t + 1)
                if not first:
                    dve.wait_ge(y_ps_made, t)
                nc.vector.tensor_copy(hid_t[:, b], ps_h[:, b, 0:P]).then_inc(hid_t_made, 1)

            def copy_y(i, s, first):
                t = i * 4 + s
                dve.wait_ge(y_ps_made, t + 2)
                if not first:
                    dve.wait_ge(y_out[s], 16 * i)
                nc.vector.tensor_copy(y[:, s], ps_y[:, s % 2]).then_inc(y_made, 1)

            def four(i, first):
                for s in range(4):
                    t = i * 4 + s
                    multiply(t, s % 2, first and s < 2)
                    if not (first and s == 0):
                        copy_y(*((i, s - 1, first) if s else (i - 1, 3, False)))
                    copy_h(t, s % 2, first and s < 2)
            four(0, True)
            multiply(4, 0, False)
            dve.wait_ge(y_ps_made, 5)
            nc.vector.tensor_copy(y[:, 3], ps_y[:, 1]).then_inc(y_made, 1)
            copy_h(4, 0, False)
            for s in range(1, 4):
                multiply(4 + s, s % 2, False)
                copy_y(1, s - 1, False)
                copy_h(4 + s, s % 2, False)
            with dve.Fori(2, TILES // 4) as i:
                four(i, False)
            copy_y(TILES // 4 - 1, 3, False)

        @block.tensor
        def _(pe):
            def turn(t, s, n, first):
                pe.wait_ge(xg_in[s], 16 * n)
                if not first:
                    pe.wait_ge(xt_made, t - 1)
                for k in range(KC):
                    last = nc.tensor.transpose(ps_t[:, s % 2, k], xg[:, s, k * P:(k + 1) * P], ident[:])
                last.then_inc(transposed, 1)

            def weights_of(t):
                e = pe.value_load(st.eid[0:1, bass.ds(t, 1)], min_val=0, max_val=E_ - 1)
                pe.wait_ge(weights_ready, e + 1)
                slot = pe.snap(e & (WR - 1))
                return pe.snap(slot * (KC * 2 * I_)), pe.snap(slot * D)

            def gate_up(t, b, at, first):
                if not first:
                    pe.wait_ge(hid_made, t - 1)
                pe.wait_ge(xt_made, t + 1)
                for k in range(KC):
                    last = nc.tensor.matmul(ps_g[:, b, 0:2 * I_], xt[:, b, k], wgu[:, bass.ds(at + k * 2 * I_, 2 * I_)],
                                            start=k == 0, stop=k == KC - 1)
                last.then_inc(gu_made, 1)

            def turn_hidden(t, b, first):
                pe.wait_ge(hid_made, t + 1)
                if not first:
                    pe.wait_ge(hid_t_made, t - 1)
                nc.tensor.transpose(ps_h[:, b, 0:P], hid[:, b], ident[:]).then_inc(turned, 1)

            def down(t, b, at, first):
                if not first:
                    pe.wait_ge(y_made, t - 1)
                pe.wait_ge(hid_t_made, t + 1)
                nc.tensor.matmul(ps_y[:, b], hid_t[:, b], wd[:, bass.ds(at, D)], start=True, stop=True
                                 ).then_inc(y_ps_made, 1)

            pe.sem_inc(y_ps_made, 1)
            turn(0, 0, 1, True)

            def turn_of_loop(i, first, last):
                at = weights_of(i * UN)
                for s in range(UN):
                    t = i * UN + s
                    gate_up(t, s % 2, at[0], first and s < 2)
                    if not (last and s == UN - 1):
                        turn(t + 1, (s + 1) % GR, i * (UN // GR) + (s + 1) // GR + 1, first and s < 1)
                    if s:
                        down(t - 1, (s - 1) % 2, before, first and s < 3)
                    before = at[1]
                    if s < UN - 1:
                        at = weights_of(t + 1)
                    turn_hidden(t, s % 2, first and s < 2)
                down(i * UN + UN - 1, 1, before, False)
            turn_of_loop(0, True, False)
            with pe.Fori(1, TILES // UN - 1) as i:
                turn_of_loop(i, False, False)
            turn_of_loop(TILES // UN - 1, False, True)


def combine(nc, tag, st, base, yo, out):
    with nc.cleanup_on_exit(), ExitStack() as c:
        def sb(name, shape, dt=F32):
            return c.enter_context(nc.sbuf_tensor(f"{tag}_{name}", shape, dt))

        def sem(name):
            return nc.alloc_semaphore(f"{tag}_{name}")

        place = sb("place", [P, 2, 8], I32)
        rows = sb("rows", [P, 2, KTOP, D])
        bin_ = sb("bin", [P, 2, D])
        acc = sb("acc", [P, 2, D])
        nmax = sb("nmax", [P, NT])
        ex = sb("ex", [P, 2, E_])
        total = sb("total", [P, 2])
        rtotal = sb("rtotal", [P, 1])
        pos = sb("pos", [P, E_])
        top = sb("top", [P, 8])
        junk = sb("junk", [P, 8, E_])
        w8 = sb("w8", [P, 8])
        weight = sb("weight", [P, 2, 8])
        y = sb("y", [P, 2, D])
        b_in = [sem("b_in0"), sem("b_in1")]
        rows_in = [sem("rows_in0"), sem("rows_in1")]
        y_out = [sem("y_out0"), sem("y_out1")]
        place_made, chain, y_made, held = sem("place_made"), sem("chain"), sem("y_made"), sem("held")
        nmax_made, ex_made, picks, tile_link = sem("nmax_made"), sem("ex_made"), sem("picks"), sem("tile_link")
        weight_made = sem("weight_made")
        block = c.enter_context(nc.Block())

        @block.sync
        def _(sp):
            def load(i, s, first):
                if not first:
                    sp.wait_ge(y_made, 2 * i + s - 1)
                sp.dma_start(bin_[:, s], base[bass.ds((2 * i + s) * P, P), :]).then_inc(b_in[s], 16)

            def store(i, s):
                sp.wait_ge(y_made, 2 * i + s + 1)
                sp.dma_start(out[bass.ds((2 * i + s) * P, P), :], y[:, s]).then_inc(y_out[s], 16)
            load(0, 0, True)
            load(0, 1, True)
            with sp.Fori(0, NT // 2 - 1) as i:
                for s in range(2):
                    store(i, s)
                    load(i + 1, s, False)
            for s in range(2):
                store(NT // 2 - 1, s)
            for s in range(2):
                sp.wait_ge(y_out[s], 16 * (NT // 2))

        @block.gpsimd
        def _(pool):
            def gather(i, s, first):
                t = 2 * i + s
                if not first:
                    hold(pool, y_made, t - 1, held)
                hold(pool, place_made, t + 1, held)
                for k in range(KTOP):
                    nc.gpsimd.indirect_dma_start(rows[:, s, k], None, yo[:, :],
                                                 bass.IndirectOffsetOnAxis(ap=place[:, s, k:k + 1], axis=0)
                                                 ).then_inc(rows_in[s], 16)
            for s in range(2):
                gather(0, s, True)
            with pool.Fori(1, NT // 2) as i:
                for s in range(2):
                    gather(i, s, False)

        @block.scalar
        def _(act):
            act.wait_ge(nmax_made, 1)

            def exponentials(i, s, first):
                t = 2 * i + s
                if not first:
                    act.wait_ge(weight_made, t - 1)
                nc.scalar.activation(ex[:, s], st.cand[:, bass.ds(t, 1)].rearrange("p o e -> p (o e)"), ACT.Exp,
                                     bias=nmax[:, bass.ds(t, 1)], accum_out=total[:, s:s + 1]).then_inc(ex_made, 1)
            for s in range(2):
                exponentials(0, s, True)
            with act.Fori(1, NT // 2) as i:
                for s in range(2):
                    exponentials(i, s, False)

        @block.vector
        def _(dve):
            tl = Link(dve, tile_link, 4)
            nc.vector.tensor_scalar(nmax[:], st.top[:, :, 0], -1.0, None, ALU.mult).then_inc(nmax_made, 1)

            def choose(i, s, first):
                t = 2 * i + s
                tl.start(t)
                if not (first and s == 0):
                    dve.wait_ge(picks, (KTOP + 1) * t)
                tl(nc.vector.tensor_tensor(pos[:, None, :], st.rank[:, bass.ds(t, 1)], st.first[:, None, :], ALU.add))
                tl(nc.vector.tensor_tensor(pos[:, None, :], pos[:, None, :], st.mask[:, bass.ds(t, 1)], ALU.mult),
                   held)
                tl(nc.vector.max(top[:], pos[:]))
                if not first:
                    dve.wait_ge(rows_in[s], 16 * KTOP * i)
                nc.vector.tensor_scalar(place[:, s], top[:], -1.0, None, ALU.add).then_inc(place_made, 1)
                dve.wait_ge(ex_made, t + 1)
                tl(nc.vector.reciprocal(rtotal[:], total[:, s:s + 1]))

            def pick(s, k):
                nc.vector.scalar_tensor_tensor(junk[:, k], pos[:], top[:, k:k + 1], ex[:, s], ALU.is_equal,
                                               ALU.mult, accum_out=w8[:, k:k + 1]).then_inc(picks, 1)

            def weigh(i, s):
                t = 2 * i + s
                dve.wait_ge(picks, (KTOP + 1) * t + KTOP)
                nc.vector.tensor_scalar(weight[:, s], w8[:], rtotal[:], None, ALU.mult).then_inc(weight_made, 1)
                dve.sem_inc(picks, 1)

            def add(i, s, first, ahead):
                t = 2 * i + s
                dve.wait_ge(weight_made, t + 1)
                dve.wait_ge(b_in[s], 16 * i + 16)
                dve.wait_ge(rows_in[s], 16 * KTOP * i + 16 * KTOP)
                if not (first and s == 0):
                    dve.wait_ge(y_made, t)
                if not first:
                    dve.wait_ge(y_out[s], 16 * i)
                if ahead:
                    choose(i + 1, s, False)
                for k in range(KTOP):
                    if k:
                        dve.wait_ge(chain, t * (KTOP - 1) + k)
                    src = bin_[:, s] if k == 0 else acc[:, (k - 1) % 2]
                    dst = y[:, s] if k == KTOP - 1 else acc[:, k % 2]
                    nc.vector.scalar_tensor_tensor(dst, rows[:, s, k], weight[:, s, k:k + 1], src, ALU.mult, ALU.add
                                                   ).then_inc(chain if k < KTOP - 1 else y_made, 1)
                    if ahead:
                        pick(s, k)
                if ahead:
                    dve.wait_ge(y_made, t + 1)
                    weigh(i + 1, s)

            for s in range(2):
                choose(0, s, True)
                for k in range(KTOP):
                    pick(s, k)
                weigh(0, s)
            for s in range(2):
                add(0, s, True, True)
            with dve.Fori(1, NT // 2 - 1) as i:
                for s in range(2):
                    add(i, s, False, True)
            for s in range(2):
                add(NT // 2 - 1, s, False, False)


def two_layers(nc, a, out):
    def dram(name, shape, dt=F32):
        return nc.dram_tensor(name, shape, dt, kind="Internal").ap()

    qh, ql = dram("q_high", [D, N]), dram("q_low", [D, N])
    att, x1, xf = dram("attended", [N, D]), dram("x_1", [N, D]), dram("x_normed", [N, D])
    base, x2, x3 = dram("x_shared", [N, D]), dram("x_2", [N, D]), dram("x_3", [N, D])
    lists = dram("token_lists", [E_ * N, 1], I32)
    yo = dram("expert_rows", [TILES * P, D])
    with ExitStack() as c:
        ident = make_identity(nc, c, "identity")
        norm_query(nc, "q0", ident, a["x"], a["L0_xattn_W_Q"], a["L0_xattn_b_Q"], qh, ql)
        attend(nc, "a0", ident, qh, ql, a["ctx_1024"], a["L0_xattn_W_K"], a["L0_xattn_b_K"], a["L0_xattn_W_V"], att,
               a["ctx_1024"].shape[2], False)
        out_project(nc, "o0", ident, att, a["L0_xattn_b_V"], a["L0_xattn_W_O"], a["L0_xattn_b_O"], a["x"], x1)
        with ExitStack() as cc:
            st = RouteState(nc, cc)
            route(nc, "rt", ident, st, x1, a["L0_ffn_Wg"], a["L0_ffn_Ws_gate_up"], a["L0_ffn_Ws_down"], xf, base, lists)
            tables(nc, "tb", ident, st)
            experts(nc, "ex", ident, st, xf, a["L0_ffn_W_gate_up"].rearrange("e k n -> (e k) n"),
                    a["L0_ffn_W_down"].rearrange("e k n -> (e k) n"), lists, yo)
            combine(nc, "cb", st, base, yo, x2)
        norm_query(nc, "q1", ident, x2, a["L1_xattn_Wq"], a["L1_xattn_bq"], qh, ql)
        attend(nc, "a1", ident, qh, ql, a["ctx_1024"], a["L1_xattn_Wk"], a["L1_xattn_bk"], a["L1_xattn_Wv"], att,
               SQ, True)
        out_project(nc, "o1", ident, att, a["L1_xattn_bv"], a["L1_xattn_Wo"], a["L1_xattn_bo"], x2, x3)
        quantized_ffn(nc, "f1", ident, x3, a["L1_ffn_weight"].bitcast(mybir.dt.uint8), a["L1_ffn_weight_scale"],
                      a["L1_ffn_bias"], out)


_TURNED = ("L0_xattn_W_Q", "L0_xattn_W_K", "L0_xattn_W_V", "L0_xattn_W_O", "L0_ffn_Wg",
           "L1_xattn_Wq", "L1_xattn_Wk", "L1_xattn_Wv", "L1_xattn_Wo", "L1_ffn_weight")


def kernel(**inputs):
    import numpy as np
    import concourse.bacc as bacc
    from concourse.bass_utils import run_bass_kernel_spmd

    nc = bacc.Bacc("TRN2", target_bir_lowering=False, num_devices=1)
    arrays, args = {}, {}
    for name, value in inputs.items():
        v = np.asarray(value)
        if name in _TURNED:
            v = v.T
        if name == "ctx_1024":
            v = v.transpose(2, 0, 1)
        if name == "x":
            v = v.reshape(N, D)
        v = np.ascontiguousarray(v.reshape(1) if v.ndim == 0 else v)
        arrays[f"in_{name}"] = v
        args[name] = nc.dram_tensor(f"in_{name}", v.shape, mybir.dt.from_np(v.dtype), kind="ExternalInput").ap()
    out = nc.dram_tensor("out", (N, D), F32, kind="ExternalOutput").ap()
    two_layers(nc, args, out)
    r = run_bass_kernel_spmd(nc, [arrays], core_ids=[0])
    return r.results[0]["out"].reshape(B, SQ, D)
```
